# Optimizing a Trainium2 kernel written in Bass

```python
import numpy as np
import jax
import jax.numpy as jnp

def _softmax(x, axis=-1):
    return jax.nn.softmax(x, axis=axis)

def _gelu(x):
    return jax.nn.gelu(x, approximate=True)

def _silu(x):
    return jax.nn.silu(x)

def _sigmoid(x):
    return jax.nn.sigmoid(x)

def _layernorm(x, axis=-1, eps=1e-05):
    m = jnp.mean(x, axis=axis, keepdims=True)
    v = jnp.var(x, axis=axis, keepdims=True)
    return (x - m) / jnp.sqrt(v + eps)

def _scatter_add(tgt, idx, src, axis=0):
    return tgt.at[idx].add(src)

def _segment_sum(src, seg, n):
    return jax.ops.segment_sum(src, seg, n)
kernel_name = 'mk_conv_seq_d4_conv_nhwc256_r2_772e75'

def setup_inputs(seed: int=0):
    np.random.seed(seed)
    _w = jnp.asarray

    def _rec_inputs():
        import jax
        import jax.numpy as jnp
        _gk = jax.random.key(seed)
        x = -0.0005207 + 1.001 * jax.random.normal(jax.random.fold_in(_gk, 1), (2, 32, 32, 128), jnp.float32)
        return x
    x = _rec_inputs()

    def _L0_conv_setup():
        import jax, jax.numpy as jnp
        import numpy as np
        DIM, K, NH = (128, 7, 8)

        def _nbhd_idx(n, k):
            start = jnp.clip(jnp.arange(n) - k // 2, 0, n - k)
            idx = start[:, None] + jnp.arange(k)[None, :]
            bias = idx - jnp.arange(n)[:, None] + (k - 1)
            return (idx, bias)
        key = jax.random.key(seed)
        ks = jax.random.split(key, 8)
        s = lambda k_, sh, fan: jax.random.normal(k_, sh, jnp.float32) * fan ** (-0.5)
        return {'x': jax.random.normal(ks[0], (2, 32, 32, DIM), jnp.float32), 'qkv_w': s(ks[1], (DIM, 3 * DIM), DIM), 'qkv_b': jnp.zeros((3 * DIM,), jnp.float32), 'rpb': 0.02 * jax.random.normal(ks[2], (NH, 2 * K - 1, 2 * K - 1), jnp.float32), 'proj_w': s(ks[3], (DIM, DIM), DIM), 'proj_b': jnp.zeros((DIM,), jnp.float32), 'g1_w': s(ks[4], (DIM, DIM // 4), DIM), 'g1_b': jnp.zeros((DIM // 4,), jnp.float32), 'g2_w': s(ks[5], (DIM // 4, 1), DIM // 4), 'g2_b': jnp.zeros((1,), jnp.float32), 'ln_g': jnp.ones((DIM,), jnp.float32), 'ln_b': jnp.zeros((DIM,), jnp.float32)}
    _L0_conv_all = _L0_conv_setup()
    _L0_conv_in = {k: v for k, v in _L0_conv_all.items() if k in ('qkv_w', 'qkv_b', 'rpb', 'proj_w', 'proj_b', 'g1_w', 'g1_b', 'g2_w', 'g2_b', 'ln_g', 'ln_b')}
    del _L0_conv_all

    def _L1_conv_setup():
        import jax, jax.numpy as jnp
        import numpy as np
        N = 3
        B, R, C, CH = (32, 56, 56, 128)
        key = jax.random.key(seed)
        k1, k2 = jax.random.split(key)
        x = jax.random.normal(k1, (B, R, C, CH), dtype=jnp.float32)
        kernel = jax.random.normal(k2, (N, N, CH), dtype=jnp.float32) * 0.1
        return {'x': x, 'kernel': kernel}
    _L1_conv_all = _L1_conv_setup()
    _L1_conv_in = {k: v for k, v in _L1_conv_all.items() if k in ('kernel',)}
    del _L1_conv_all

    def _L2_conv_setup():
        import jax, jax.numpy as jnp
        import numpy as np
        N_HEADS = 8
        WINDOW = 7

        def _conv1x1(x, W, b):
            return jnp.einsum('bhwc,cd->bhwd', x, W) + b

        def _to_heads(t, nh):
            B, H, W, C = t.shape
            return jnp.transpose(t, (0, 3, 1, 2)).reshape(B, nh, C // nh, H * W)
        key = jax.random.key(seed)
        ks = jax.random.split(key, 8)
        B, H, W, C = (2, 56, 56, 128)
        x = jax.random.normal(ks[0], (B, H, W, C), dtype=jnp.float32)
        s = 1.0 / np.sqrt(C)
        Wq = jax.random.normal(ks[1], (C, C), dtype=jnp.float32) * s
        bq = jnp.zeros((C,), dtype=jnp.float32)
        Wk = jax.random.normal(ks[2], (C, C), dtype=jnp.float32) * s
        bk = jnp.zeros((C,), dtype=jnp.float32)
        Wv = jax.random.normal(ks[3], (C, C), dtype=jnp.float32) * s
        bv = jnp.zeros((C,), dtype=jnp.float32)
        gamma = jax.random.normal(ks[4], (1,), dtype=jnp.float32) * 0.1
        return {'x': x, 'Wq': Wq, 'bq': bq, 'Wk': Wk, 'bk': bk, 'Wv': Wv, 'bv': bv, 'gamma': gamma}
    _L2_conv_all = _L2_conv_setup()
    _L2_conv_in = {k: v for k, v in _L2_conv_all.items() if k in ('Wq', 'bq', 'Wk', 'bk', 'Wv', 'bv', 'gamma')}
    del _L2_conv_all

    def _L3_conv_setup():
        import jax, jax.numpy as jnp
        import numpy as np
        B, H, W, DIM = (2, 64, 64, 128)
        NB, EXP, HEADS = (16, 8, 8)
        BS = DIM // NB
        DH = DIM // HEADS
        EPS = 1e-05
        LAM = 0.01

        def _ln(x, g, b):
            mu = jnp.mean(x, axis=-1, keepdims=True)
            var = jnp.mean((x - mu) ** 2, axis=-1, keepdims=True)
            return (x - mu) * jax.lax.rsqrt(var + EPS) * g + b

        def _afno(x, w1, b1, w2, b2):
            bias = x
            Bx, Hx, Wx, C = x.shape
            xf = jnp.fft.rfft2(x, axes=(1, 2), norm='ortho')
            xf = xf.reshape(Bx, Hx, Wx // 2 + 1, NB, BS)
            xr, xi = (jnp.real(xf), jnp.imag(xf))
            mm = lambda t, w: jnp.einsum('bhwni,nio->bhwno', t, w)
            o1r = jax.nn.relu(mm(xr, w1[0]) - mm(xi, w1[1]) + b1[0])
            o1i = jax.nn.relu(mm(xi, w1[0]) + mm(xr, w1[1]) + b1[1])
            o2r = mm(o1r, w2[0]) - mm(o1i, w2[1]) + b2[0]
            o2i = mm(o1i, w2[0]) + mm(o1r, w2[1]) + b2[1]
            shrink = lambda t: jnp.sign(t) * jnp.maximum(jnp.abs(t) - LAM, 0.0)
            xf = (shrink(o2r) + 1j * shrink(o2i)).reshape(Bx, Hx, Wx // 2 + 1, C)
            out = jnp.fft.irfft2(xf, s=(Hx, Wx), axes=(1, 2), norm='ortho')
            return out + bias

        def _galerkin(h, wq, bq, wk, bk, wv, bv, lnk_g, lnk_b, lnv_g, lnv_b, wo, bo):
            Bx, N, C = h.shape
            split = lambda t, w, b: (t @ w.T + b).reshape(Bx, N, HEADS, DH).transpose(0, 2, 1, 3)
            q = split(h, wq, bq)
            k = split(h, wk, bk)
            v = split(h, wv, bv)
            k = _ln(k, lnk_g[None, :, None, :], lnk_b[None, :, None, :])
            v = _ln(v, lnv_g[None, :, None, :], lnv_b[None, :, None, :])
            kv = jnp.einsum('bhnd,bhne->bhde', k, v) / N
            out = jnp.einsum('bhnd,bhde->bhne', q, kv)
            out = out.transpose(0, 2, 1, 3).reshape(Bx, N, C)
            return out @ wo.T + bo

        def _forward(x, afno_w1, afno_b1, afno_w2, afno_b2, wq, bq, wk, bk, wv, bv, lnk_g, lnk_b, lnv_g, lnv_b, wo, bo, w_up, b_up, w_down, b_down, n1_g, n1_b, n2_g, n2_b, n3_g, n3_b):
            Bx, Hx, Wx, C = x.shape
            x = x + _afno(_ln(x, n1_g, n1_b), afno_w1, afno_b1, afno_w2, afno_b2)
            x = _ln(x, n2_g, n2_b)
            h = x.reshape(Bx, Hx * Wx, C)
            x = x + _galerkin(h, wq, bq, wk, bk, wv, bv, lnk_g, lnk_b, lnv_g, lnv_b, wo, bo).reshape(Bx, Hx, Wx, C)
            x = _ln(x, n3_g, n3_b)
            h = jax.nn.gelu(x @ w_up.T + b_up, approximate=False)
            x = x + h @ w_down.T + b_down
            return x
        key = jax.random.key(seed)
        ks = jax.random.split(key, 24)
        r = lambda i, shape, s: jax.random.normal(ks[i], shape, dtype=jnp.float32) * s
        z = lambda shape: jnp.zeros(shape, dtype=jnp.float32)
        o = lambda shape: jnp.ones(shape, dtype=jnp.float32)
        return dict(x=r(0, (B, H, W, DIM), 1.0), afno_w1=r(1, (2, NB, BS, BS * EXP), 0.02), afno_b1=r(2, (2, NB, BS * EXP), 0.02), afno_w2=r(3, (2, NB, BS * EXP, BS), 0.02), afno_b2=r(4, (2, NB, BS), 0.02), wq=r(5, (DIM, DIM), 0.02), bq=z((DIM,)), wk=r(6, (DIM, DIM), 0.02), bk=z((DIM,)), wv=r(7, (DIM, DIM), 0.02), bv=z((DIM,)), lnk_g=o((HEADS, DH)), lnk_b=z((HEADS, DH)), lnv_g=o((HEADS, DH)), lnv_b=z((HEADS, DH)), wo=r(8, (DIM, DIM), 0.02), bo=z((DIM,)), w_up=r(9, (DIM * EXP, DIM), 0.02), b_up=z((DIM * EXP,)), w_down=r(10, (DIM, DIM * EXP), 0.02), b_down=z((DIM,)), n1_g=o((DIM,)), n1_b=z((DIM,)), n2_g=o((DIM,)), n2_b=z((DIM,)), n3_g=o((DIM,)), n3_b=z((DIM,)))
    _L3_conv_all = _L3_conv_setup()
    _L3_conv_in = {k: v for k, v in _L3_conv_all.items() if k in ('afno_w1', 'afno_b1', 'afno_w2', 'afno_b2', 'wq', 'bq', 'wk', 'bk', 'wv', 'bv', 'lnk_g', 'lnk_b', 'lnv_g', 'lnv_b', 'wo', 'bo', 'w_up', 'b_up', 'w_down', 'b_down', 'n1_g', 'n1_b', 'n2_g', 'n2_b', 'n3_g', 'n3_b')}
    del _L3_conv_all
    return {'x': x, 'L0_conv_qkv_w': _L0_conv_in['qkv_w'], 'L0_conv_qkv_b': _L0_conv_in['qkv_b'], 'L0_conv_rpb': _L0_conv_in['rpb'], 'L0_conv_proj_w': _L0_conv_in['proj_w'], 'L0_conv_proj_b': _L0_conv_in['proj_b'], 'L0_conv_g1_w': _L0_conv_in['g1_w'], 'L0_conv_g1_b': _L0_conv_in['g1_b'], 'L0_conv_g2_w': _L0_conv_in['g2_w'], 'L0_conv_g2_b': _L0_conv_in['g2_b'], 'L0_conv_ln_g': _L0_conv_in['ln_g'], 'L0_conv_ln_b': _L0_conv_in['ln_b'], 'L1_conv_kernel': _L1_conv_in['kernel'], 'L2_conv_Wq': _L2_conv_in['Wq'], 'L2_conv_bq': _L2_conv_in['bq'], 'L2_conv_Wk': _L2_conv_in['Wk'], 'L2_conv_bk': _L2_conv_in['bk'], 'L2_conv_Wv': _L2_conv_in['Wv'], 'L2_conv_bv': _L2_conv_in['bv'], 'L2_conv_gamma': _L2_conv_in['gamma'], 'L3_conv_afno_w1': _L3_conv_in['afno_w1'], 'L3_conv_afno_b1': _L3_conv_in['afno_b1'], 'L3_conv_afno_w2': _L3_conv_in['afno_w2'], 'L3_conv_afno_b2': _L3_conv_in['afno_b2'], 'L3_conv_wq': _L3_conv_in['wq'], 'L3_conv_bq': _L3_conv_in['bq'], 'L3_conv_wk': _L3_conv_in['wk'], 'L3_conv_bk': _L3_conv_in['bk'], 'L3_conv_wv': _L3_conv_in['wv'], 'L3_conv_bv': _L3_conv_in['bv'], 'L3_conv_lnk_g': _L3_conv_in['lnk_g'], 'L3_conv_lnk_b': _L3_conv_in['lnk_b'], 'L3_conv_lnv_g': _L3_conv_in['lnv_g'], 'L3_conv_lnv_b': _L3_conv_in['lnv_b'], 'L3_conv_wo': _L3_conv_in['wo'], 'L3_conv_bo': _L3_conv_in['bo'], 'L3_conv_w_up': _L3_conv_in['w_up'], 'L3_conv_b_up': _L3_conv_in['b_up'], 'L3_conv_w_down': _L3_conv_in['w_down'], 'L3_conv_b_down': _L3_conv_in['b_down'], 'L3_conv_n1_g': _L3_conv_in['n1_g'], 'L3_conv_n1_b': _L3_conv_in['n1_b'], 'L3_conv_n2_g': _L3_conv_in['n2_g'], 'L3_conv_n2_b': _L3_conv_in['n2_b'], 'L3_conv_n3_g': _L3_conv_in['n3_g'], 'L3_conv_n3_b': _L3_conv_in['n3_b']}

def reference(x, L0_conv_qkv_w, L0_conv_qkv_b, L0_conv_rpb, L0_conv_proj_w, L0_conv_proj_b, L0_conv_g1_w, L0_conv_g1_b, L0_conv_g2_w, L0_conv_g2_b, L0_conv_ln_g, L0_conv_ln_b, L1_conv_kernel, L2_conv_Wq, L2_conv_bq, L2_conv_Wk, L2_conv_bk, L2_conv_Wv, L2_conv_bv, L2_conv_gamma, L3_conv_afno_w1, L3_conv_afno_b1, L3_conv_afno_w2, L3_conv_afno_b2, L3_conv_wq, L3_conv_bq, L3_conv_wk, L3_conv_bk, L3_conv_wv, L3_conv_bv, L3_conv_lnk_g, L3_conv_lnk_b, L3_conv_lnv_g, L3_conv_lnv_b, L3_conv_wo, L3_conv_bo, L3_conv_w_up, L3_conv_b_up, L3_conv_w_down, L3_conv_b_down, L3_conv_n1_g, L3_conv_n1_b, L3_conv_n2_g, L3_conv_n2_b, L3_conv_n3_g, L3_conv_n3_b):
    import jax
    import jax.numpy as jnp

    def _L0_conv_ref(x, qkv_w, qkv_b, rpb, proj_w, proj_b, g1_w, g1_b, g2_w, g2_b, ln_g, ln_b):
        import jax, jax.numpy as jnp
        import numpy as np
        DIM, K, NH = (128, 7, 8)

        def _nbhd_idx(n, k):
            start = jnp.clip(jnp.arange(n) - k // 2, 0, n - k)
            idx = start[:, None] + jnp.arange(k)[None, :]
            bias = idx - jnp.arange(n)[:, None] + (k - 1)
            return (idx, bias)
        B, H, W, C = x.shape
        hd = C // NH
        scale = hd ** (-0.5)
        qkv = x @ qkv_w + qkv_b
        q, kk, v = jnp.split(qkv, 3, axis=-1)
        q = q.reshape(B, H, W, NH, hd) * scale
        kk = kk.reshape(B, H, W, NH, hd)
        v = v.reshape(B, H, W, NH, hd)
        ih, bh = _nbhd_idx(H, K)
        iw, bw = _nbhd_idx(W, K)
        kn = kk[:, ih][:, :, :, iw].transpose(0, 1, 3, 5, 2, 4, 6)
        vn = v[:, ih][:, :, :, iw].transpose(0, 1, 3, 5, 2, 4, 6)
        attn = jnp.einsum('bijnd,bijnpqd->bijnpq', q, kn)
        bias = rpb[:, bh][:, :, :, bw]
        bias = bias.transpose(1, 3, 0, 2, 4)
        attn = attn + bias[None]
        a = jax.nn.softmax(attn.reshape(B, H, W, NH, K * K), axis=-1)
        a = a.reshape(B, H, W, NH, K, K)
        out = jnp.einsum('bijnpq,bijnpqd->bijnd', a, vn).reshape(B, H, W, C)
        out = out @ proj_w + proj_b
        gate = jax.nn.sigmoid(jax.nn.relu(x @ g1_w + g1_b) @ g2_w + g2_b)
        y = x + out * gate
        mu = jnp.mean(y, axis=-1, keepdims=True)
        var = jnp.var(y, axis=-1, keepdims=True)
        return (y - mu) / jnp.sqrt(var + 1e-05) * ln_g + ln_b

    def _L1_conv_ref(x, kernel):
        import jax, jax.numpy as jnp
        import numpy as np
        N = 3
        B, R, C, CH = (32, 56, 56, 128)
        n = kernel.shape[0]
        ch = kernel.shape[2]
        mask = jnp.ones((n, n, 1), dtype=kernel.dtype).at[n // 2, n // 2, 0].set(0.0)
        k = kernel * mask
        k_hwio = k[:, :, None, :]
        out = jax.lax.conv_general_dilated(x, k_hwio, window_strides=(1, 1), padding='SAME', dimension_numbers=('NHWC', 'HWIO', 'NHWC'), feature_group_count=ch)
        return out + x

    def _L2_conv_ref(x, Wq, bq, Wk, bk, Wv, bv, gamma):
        import jax, jax.numpy as jnp
        import numpy as np
        N_HEADS = 8
        WINDOW = 7

        def _conv1x1(x, W, b):
            return jnp.einsum('bhwc,cd->bhwd', x, W) + b

        def _to_heads(t, nh):
            B, H, W, C = t.shape
            return jnp.transpose(t, (0, 3, 1, 2)).reshape(B, nh, C // nh, H * W)
        B, H, W, C = x.shape
        p = WINDOW // 2
        xp = jnp.pad(x, ((0, 0), (p, p), (p, p), (0, 0)), mode='reflect')
        q = _to_heads(_conv1x1(x, Wq, bq), N_HEADS)
        k = _to_heads(_conv1x1(xp, Wk, bk), N_HEADS)
        v = _to_heads(_conv1x1(xp, Wv, bv), N_HEADS)
        energy = jnp.einsum('bhdq,bhdk->bhqk', q, k)
        attn = jax.nn.softmax(energy, axis=-1)
        out = jnp.einsum('bhdk,bhqk->bhdq', v, attn)
        out = out.reshape(B, C, H, W).transpose(0, 2, 3, 1)
        return gamma * out + x

    def _L3_conv_ref(x, afno_w1, afno_b1, afno_w2, afno_b2, wq, bq, wk, bk, wv, bv, lnk_g, lnk_b, lnv_g, lnv_b, wo, bo, w_up, b_up, w_down, b_down, n1_g, n1_b, n2_g, n2_b, n3_g, n3_b):
        import jax, jax.numpy as jnp
        import numpy as np
        B, H, W, DIM = (2, 64, 64, 128)
        NB, EXP, HEADS = (16, 8, 8)
        BS = DIM // NB
        DH = DIM // HEADS
        EPS = 1e-05
        LAM = 0.01

        def _ln(x, g, b):
            mu = jnp.mean(x, axis=-1, keepdims=True)
            var = jnp.mean((x - mu) ** 2, axis=-1, keepdims=True)
            return (x - mu) * jax.lax.rsqrt(var + EPS) * g + b

        def _afno(x, w1, b1, w2, b2):
            bias = x
            Bx, Hx, Wx, C = x.shape
            xf = jnp.fft.rfft2(x, axes=(1, 2), norm='ortho')
            xf = xf.reshape(Bx, Hx, Wx // 2 + 1, NB, BS)
            xr, xi = (jnp.real(xf), jnp.imag(xf))
            mm = lambda t, w: jnp.einsum('bhwni,nio->bhwno', t, w)
            o1r = jax.nn.relu(mm(xr, w1[0]) - mm(xi, w1[1]) + b1[0])
            o1i = jax.nn.relu(mm(xi, w1[0]) + mm(xr, w1[1]) + b1[1])
            o2r = mm(o1r, w2[0]) - mm(o1i, w2[1]) + b2[0]
            o2i = mm(o1i, w2[0]) + mm(o1r, w2[1]) + b2[1]
            shrink = lambda t: jnp.sign(t) * jnp.maximum(jnp.abs(t) - LAM, 0.0)
            xf = (shrink(o2r) + 1j * shrink(o2i)).reshape(Bx, Hx, Wx // 2 + 1, C)
            out = jnp.fft.irfft2(xf, s=(Hx, Wx), axes=(1, 2), norm='ortho')
            return out + bias

        def _galerkin(h, wq, bq, wk, bk, wv, bv, lnk_g, lnk_b, lnv_g, lnv_b, wo, bo):
            Bx, N, C = h.shape
            split = lambda t, w, b: (t @ w.T + b).reshape(Bx, N, HEADS, DH).transpose(0, 2, 1, 3)
            q = split(h, wq, bq)
            k = split(h, wk, bk)
            v = split(h, wv, bv)
            k = _ln(k, lnk_g[None, :, None, :], lnk_b[None, :, None, :])
            v = _ln(v, lnv_g[None, :, None, :], lnv_b[None, :, None, :])
            kv = jnp.einsum('bhnd,bhne->bhde', k, v) / N
            out = jnp.einsum('bhnd,bhde->bhne', q, kv)
            out = out.transpose(0, 2, 1, 3).reshape(Bx, N, C)
            return out @ wo.T + bo

        def _forward(x, afno_w1, afno_b1, afno_w2, afno_b2, wq, bq, wk, bk, wv, bv, lnk_g, lnk_b, lnv_g, lnv_b, wo, bo, w_up, b_up, w_down, b_down, n1_g, n1_b, n2_g, n2_b, n3_g, n3_b):
            Bx, Hx, Wx, C = x.shape
            x = x + _afno(_ln(x, n1_g, n1_b), afno_w1, afno_b1, afno_w2, afno_b2)
            x = _ln(x, n2_g, n2_b)
            h = x.reshape(Bx, Hx * Wx, C)
            x = x + _galerkin(h, wq, bq, wk, bk, wv, bv, lnk_g, lnk_b, lnv_g, lnv_b, wo, bo).reshape(Bx, Hx, Wx, C)
            x = _ln(x, n3_g, n3_b)
            h = jax.nn.gelu(x @ w_up.T + b_up, approximate=False)
            x = x + h @ w_down.T + b_down
            return x
        return _forward(x, afno_w1, afno_b1, afno_w2, afno_b2, wq, bq, wk, bk, wv, bv, lnk_g, lnk_b, lnv_g, lnv_b, wo, bo, w_up, b_up, w_down, b_down, n1_g, n1_b, n2_g, n2_b, n3_g, n3_b)

    def _gn(v, G=32, eps=1e-05):
        B_, H_, W_, C_ = v.shape
        g = v.reshape(B_, H_, W_, G, C_ // G)
        m = jnp.mean(g, axis=(1, 2, 4), keepdims=True)
        s = jnp.var(g, axis=(1, 2, 4), keepdims=True)
        return ((g - m) / jnp.sqrt(s + eps)).reshape(v.shape)

    def _ln_c(v, eps=1e-06):
        m = jnp.mean(v, axis=-1, keepdims=True)
        s = jnp.var(v, axis=-1, keepdims=True)
        return (v - m) / jnp.sqrt(s + eps)

    def _ln_t(v, eps=1e-05):
        m = jnp.mean(v, axis=-1, keepdims=True)
        s = jnp.var(v, axis=-1, keepdims=True)
        return (v - m) / jnp.sqrt(s + eps)

    def _to_tokens(v):
        B_, H_, W_, C_ = v.shape
        return v.reshape(B_, H_ * W_, C_)

    def _from_tokens(t, like):
        return t.reshape(like.shape)
    x = _L0_conv_ref(x, L0_conv_qkv_w, L0_conv_qkv_b, L0_conv_rpb, L0_conv_proj_w, L0_conv_proj_b, L0_conv_g1_w, L0_conv_g1_b, L0_conv_g2_w, L0_conv_g2_b, L0_conv_ln_g, L0_conv_ln_b)
    x = _L1_conv_ref(x, L1_conv_kernel)
    x = _L2_conv_ref(x, L2_conv_Wq, L2_conv_bq, L2_conv_Wk, L2_conv_bk, L2_conv_Wv, L2_conv_bv, L2_conv_gamma)
    x = _L3_conv_ref(x, L3_conv_afno_w1, L3_conv_afno_b1, L3_conv_afno_w2, L3_conv_afno_b2, L3_conv_wq, L3_conv_bq, L3_conv_wk, L3_conv_bk, L3_conv_wv, L3_conv_bv, L3_conv_lnk_g, L3_conv_lnk_b, L3_conv_lnv_g, L3_conv_lnv_b, L3_conv_wo, L3_conv_bo, L3_conv_w_up, L3_conv_b_up, L3_conv_w_down, L3_conv_b_down, L3_conv_n1_g, L3_conv_n1_b, L3_conv_n2_g, L3_conv_n2_b, L3_conv_n3_g, L3_conv_n3_b)
    return x

_drawn_inputs = setup_inputs


def setup_inputs(seed=0):
    import zlib

    import numpy as np

    out = dict(_drawn_inputs(seed))
    spreads = {'L0_conv_qkv_b': (0.0, 0.1),
     'L0_conv_proj_b': (0.0, 0.1),
     'L0_conv_g1_b': (0.0, 0.8),
     'L0_conv_ln_g': (1.0, 0.2),
     'L0_conv_ln_b': (0.0, 0.1),
     'L2_conv_bq': (0.0, 0.75),
     'L2_conv_bk': (0.0, 0.8),
     'L2_conv_bv': (0.0, 0.8),
     'L3_conv_bq': (0.0, 0.281),
     'L3_conv_bk': (0.0, 0.1),
     'L3_conv_bv': (0.0, 0.1),
     'L3_conv_lnk_g': (1.0, 0.6),
     'L3_conv_lnk_b': (0.0, 0.689),
     'L3_conv_lnv_g': (1.0, 0.6),
     'L3_conv_lnv_b': (0.0, 0.695),
     'L3_conv_bo': (0.0, 0.1),
     'L3_conv_b_up': (0.0, 0.1),
     'L3_conv_b_down': (0.0, 0.1),
     'L3_conv_n1_g': (1.0, 0.2),
     'L3_conv_n1_b': (0.0, 0.1),
     'L3_conv_n2_g': (1.0, 0.2),
     'L3_conv_n2_b': (0.0, 0.1),
     'L3_conv_n3_g': (1.0, 0.2),
     'L3_conv_n3_b': (0.0, 0.1)}
    factors = {'L0_conv_rpb': 8.0,
     'L3_conv_afno_w1': 8.0,
     'L3_conv_afno_b1': 8.0,
     'L3_conv_afno_w2': 8.0,
     'L3_conv_afno_b2': 6.869}
    for name, (base, spread) in spreads.items():
        noise = np.random.default_rng([zlib.crc32(name.encode()), seed]).standard_normal(out[name].shape)
        drawn = base * np.exp(spread * noise) if base else spread * noise
        out[name] = jnp.asarray(drawn.astype(out[name].dtype))
    for name, factor in factors.items():
        out[name] = (out[name] * factor).astype(out[name].dtype)
    return out
```

```python
from contextlib import ExitStack

import numpy as np

import concourse.bass as bass
from concourse import mybir

F32 = mybir.dt.float32
BF16 = mybir.dt.bfloat16
ALU = mybir.AluOpType
ACT = mybir.ActivationFunctionType
AXIS = mybir.AxisListType

C = 128
IMG, H, W = 2, 32, 32
TOK = H * W
T = IMG * TOK
TILE = 512
NT = T // TILE
NH, HD = 8, 16
HG = 4
NG = NH // HG
NB = IMG * NG
K = 7
NCH = TOK // 128
NEG = -float(2 ** 100)
RMOD = 16
R_SPLIT = 6 * HD
K1_L0 = R_SPLIT + RMOD
K2_L0 = K1_L0 + 2
K1_L2 = R_SPLIT
K2_L2 = R_SPLIT + 2
Q_PARTS = (0, 0, 1, 1, 0, 2)
K_PARTS = (0, 1, 0, 1, 2, 0)
QROWS = 4
KWIN = 10
CROWS, CCOLS = 8, 16
QWIN_R, QWIN_C = 14, 19
NB_AF, BS, EXPF = 16, 8, 8
HALF = C // 2
KX = W // 2 + 1
NF = KX * IMG * H
DH_G = 16
FF = 8 * C // 128


def window(n):
    return np.clip(np.arange(n) - K // 2, 0, n - K)


def key_rows(qb):
    s = window(H)
    return int(s[QROWS * qb]), int(s[QROWS * qb + QROWS - 1]) + K


def query_rows(rb):
    s = window(H)
    hit = [i for i in range(H) if s[i] < CROWS * (rb + 1) and s[i] + K > CROWS * rb]
    return hit[0], hit[-1] + 1


def query_cols(half):
    return (0, QWIN_C) if half == 0 else (W - QWIN_C, W)


def key_order():
    return np.arange(TOK).reshape(H, W // CCOLS, CCOLS).transpose(1, 0, 2).reshape(-1)


def kx_order():
    return [0, W // 2] + list(range(1, W // 2))


def shape_constants():
    c = {}
    eye = np.eye(C)
    c["ident"] = eye
    c["cen"] = eye - 1.0 / C
    c["avg"] = np.full((C, C), 1.0 / C)
    den = np.zeros((C, C))
    for h in range(HG):
        den[32 * h + HD, 32 * h:32 * h + 32] = 1.0
    c["den"] = den
    for g in range(NG):
        s = np.zeros((C, C))
        for h in range(HG):
            for j in range(HD):
                s[32 * h + j, 64 * g + HD * h + j] = 1.0
        c[f"sel{g}"] = s
    pad = K // 2
    mult = np.ones(H)
    mult[1:1 + pad] += 1
    mult[H - 1 - pad:H - 1] += 1
    c["mult"] = np.outer(mult, mult).reshape(NCH, 128).T
    head = np.kron(np.eye(C // DH_G), np.ones((DH_G, DH_G)))
    c["cenhead"] = eye - head / DH_G
    c["kvmask"] = head / TOK
    k = np.arange(W)
    n = float(W) ** -0.5
    f1 = np.zeros((W, W))
    g = np.zeros((W, W))
    for f in range(W):
        kx = (0, W // 2)[f] if f < 2 else f // 2
        im = f >= 2 and f % 2
        ang = 2 * np.pi * kx * k / W
        f1[:, f] = n * (-np.sin(ang) if im else np.cos(ang))
        g[f, :] = n * (1.0 if f < 2 else 2.0) * (-np.sin(ang) if im else np.cos(ang))
    c["f1"] = np.kron(np.eye(4), f1)
    c["g"] = np.kron(np.eye(4), g)
    ch = n * np.cos(2 * np.pi * np.outer(k, k) / H)
    sh = n * np.sin(2 * np.pi * np.outer(k, k) / H)
    d0 = np.zeros((H, 4, 2, 3, H))
    d0[:, 0, 0, 0], d0[:, 0, 1, 0] = ch, -sh
    d0[:, 1, 0, 1], d0[:, 1, 1, 1] = ch, -sh
    d0[:, 2, 0, 2], d0[:, 2, 1, 2] = ch, -sh
    d0[:, 3, 0, 2], d0[:, 3, 1, 2] = sh, ch
    c["d0"] = d0.reshape(128, -1)
    dg = np.zeros((H, 4, 2, 2, H))
    for b in range(2):
        dg[:, 2 * b, 0, b], dg[:, 2 * b, 1, b] = ch, -sh
        dg[:, 2 * b + 1, 0, b], dg[:, 2 * b + 1, 1, b] = sh, ch
    c["dg"] = dg.reshape(128, -1)
    e0 = np.zeros((2, 2, IMG, H, IMG, 2, H))
    eg = np.zeros((2, 2, IMG, H, IMG, 4, H))
    for i in range(IMG):
        for b in range(2):
            e0[0, b, i, :, i, b], e0[1, b, i, :, i, b] = ch, -sh
            eg[0, b, i, :, i, 2 * b], eg[0, b, i, :, i, 2 * b + 1] = ch, sh
            eg[1, b, i, :, i, 2 * b], eg[1, b, i, :, i, 2 * b + 1] = -sh, ch
    for p in range(2):
        c[f"e0{p}"] = e0[p].reshape(128, -1)
        c[f"eg{p}"] = eg[p].reshape(128, -1)
    c["sign"] = np.where(np.arange(C) < HALF, 1.0, -1.0)[:, None]
    return c


def place_constants():
    at, parts, n = {}, [], 0
    for name, a in shape_constants().items():
        at[name] = (n, a.shape[1])
        parts.append(a.astype(np.float32))
        n += a.shape[1]
    return at, np.ascontiguousarray(np.concatenate(parts, axis=1))


CAT, CONSTS = place_constants()


def mask_rows():
    row = np.arange(TOK) // W
    s = window(H)
    k = (row[key_order()][None] % RMOD == np.arange(RMOD)[:, None]).astype(np.float32)
    q = np.full((RMOD, TOK), NEG, np.float32)
    for t in range(TOK):
        for r in range(s[row[t]], s[row[t]] + K):
            q[r % RMOD, t] = 0.0
    one = np.ones((2, TOK), np.float32)
    m = np.concatenate([k, one, q], axis=0)
    return np.repeat(m[:, None], HG, axis=1).astype(mybir.dt.np(BF16))


VEC = ["bq0", "bk0", "pb0", "lng0", "lnb0", "g1b", "g2b"] + [f"kc{i}" for i in range(9)] + \
      ["bq2", "bk2", "bv2", "gamma", "n1g", "n1b", "n2g", "n2b", "n3g", "n3b", "bq3", "bk3", "bv3", "bo3", "bdn",
       "lvg", "lvb"] + [f"bup{i}" for i in range(FF)] + [f"ab1_{i}" for i in range(16)] + ["ab2_0", "ab2_1", "bv0"]
VAT = {n: i for i, n in enumerate(VEC)}
W0 = [("wq", C), ("wk", C), ("wv", C), ("pw", C), ("pwg0", C), ("pwg1", C), ("g1w", C // 4), ("g2w", C)]
W2 = [("wq2", C), ("wk2", C), ("wv2", C)]
W3 = [("wq3", C), ("wk3", C), ("wv3", C), ("wo3", C), ("lkg", C), ("lkb", C), ("aw1", 2048), ("aw2", 512),
      ("wup", 1024), ("wdn", 1024)]


def places(ws):
    at, n = {}, 0
    for name, w in ws:
        at[name] = (n, w)
        n += w
    return at, n



def build(nc, io):
    W0A, W0N = places(W0)
    W2A, W2N = places(W2)
    W3A, W3N = places(W3)
    ctx = ExitStack()
    with ctx:
        def sb(name, shape, dt=F32):
            return ctx.enter_context(nc.sbuf_tensor(name, shape, dt))

        sems = {}

        def sem(name):
            if name not in sems:
                sems[name] = ctx.enter_context(nc.semaphore(name))
            return sems[name]

        ps = ctx.enter_context(nc.psum_tensor("ps", [128, 8, TILE], F32))

        cst = sb("cst", [C, CONSTS.shape[1]])
        vec = sb("vec", [C, len(VEC)])
        w0 = sb("w0", [C, W0N])
        w2 = sb("w2", [C, W2N])
        kd = sb("kd", [C, 9, C])
        identb = sb("identb", [C, C], BF16)
        zerob = sb("zerob", [C, TILE], BF16)
        ones = sb("ones", [C, C])
        small = sb("small", [C, 16])
        eps, pbe, gb2, sv, bvec = (small[:, i:i + 1] for i in (0, 1, 2, 3, 4))
        bvecs = small[:, 4:6]
        xt = sb("xt", [C, T])
        pad = sb("pad", [C, IMG, H + 2, W + 2])
        x2 = sb("x2", [C, T])
        vaug = sb("vaug", [C, IMG * NCH, NH, 32])
        mx = sb("mx", [C, 32])
        mcat = sb("mcat", [C, 64], BF16)
        mt = sb("mt", [64, C], BF16)
        r_tab = sb("r_tab", [C, 9216])
        r_stk = sb("r_stk", [C, 12288])
        r_prt = sb("r_prt", [C, 4096])
        r_p = sb("r_p", [C, 6144])
        r_o = sb("r_o", [C, 4096])

        def cc(name):
            o, n = CAT[name]
            return cst[:, o:o + n]

        def vv(name, n=1):
            return vec[:, VAT[name]:VAT[name] + n]

        def ww(t, at, name):
            o, n = at[name]
            return t[:, o:o + n]

        ident, cen, avg, dens = cc("ident"), cc("cen"), cc("avg"), cc("den")
        TAB1 = NH * KWIN * W
        TW = 2 * QWIN_R * QWIN_C
        HT = NH // 2 * TW
        tab1 = r_tab[:, 0:TAB1].rearrange("p (n f v c) -> p n f (v c)", n=NH, f=2, c=CCOLS)
        tab2f = [r_tab[:, TAB1 + i * NH * TW // 2:TAB1 + (i + 1) * NH * TW // 2].bitcast(BF16) for i in range(3)]
        tab2 = [a.rearrange("p (n f u c) -> p n f (u c)", n=NH, f=2, c=QWIN_C) for a in tab2f]
        u_raw = r_p[:, 0:NH * TW]
        stk = r_stk[:, :].bitcast(BF16).rearrange("p (s a h n) -> p s a h n", s=3, a=2, h=HG)
        parts = r_prt[:, 0:3072].bitcast(BF16).rearrange("p (b a r n) -> p b a r n", b=2, a=2, r=3)
        rem = r_prt[:, 3072:4096].rearrange("p (b n) -> p b n", b=2)
        NP0 = QWIN_R * QWIN_C
        pa0 = r_p[:, 0:8 * NP0].rearrange("p (s h n) -> p s h n", s=4, h=2)
        junk = r_p[:, NH * TW:NH * TW + 2 * KWIN * W].rearrange("p (s n) -> p s n", s=2)
        pa2 = r_p[:, :].rearrange("p (s n) -> p s n", s=12)
        oraw = r_o[:, :].rearrange("p (b n) -> p b n", b=NB)
        rec = r_stk[:, 0:4096].rearrange("p (i n) -> p i n", n=TILE)
        og = r_stk[:, 4096:8192].rearrange("p (i n) -> p i n", n=TILE)
        gate = r_stk[:, 8192:10240].rearrange("p (t n) -> p t n", n=TILE)
        ysum = r_stk[:, 10240:12288].rearrange("p (t n) -> p t n", n=TILE)
        g1s = x2[0:C // 4, :].rearrange("p (t n) -> p t n", n=TILE)
        sqs = r_p[:, 0:2048].rearrange("p (t n) -> p t n", n=TILE)
        rss = r_p[:, 2048:4096].rearrange("p (t n) -> p t n", n=TILE)
        t1s = r_p[:, 4096:6144].rearrange("p (t n) -> p t n", n=TILE)
        tmp = r_prt[:, 0:2048].rearrange("p (t n) -> p t n", n=TILE)
        x3n = r_o[:, 0:2048]
        x4 = r_o[:, 2048:4096]
        x3t = r_stk[:, 0:2048]
        a1 = r_stk[:, 2048:4096]
        zt = r_stk[:, 4096:6144]
        sf = [r_stk[:, 6144 + i * NF:6144 + (i + 1) * NF] for i in range(2)]
        yf = [r_stk[:, 8320 + i * NF:8320 + (i + 1) * NF] for i in range(2)]
        yt = r_stk[:, 0:2304].rearrange("p (o n) -> p o n", o=2)
        zf = r_stk[:, 2304:4352]
        zt2 = r_stk[:, 4352:6400]
        h5 = r_stk[:, 6400:8448]
        FT = 384
        ftiles = [(o, min(FT, NF - o)) for o in range(0, NF, FT)]
        hid = r_p[:, :].rearrange("p (b m n) -> p b m n", b=2, m=8)
        tsh = r_prt[:, 0:2 * FT].rearrange("p (b n) -> p b n", b=2)
        csh = r_prt[:, 2 * FT:4 * FT].rearrange("p (b n) -> p b n", b=2)
        cw = r_prt[:, 0:256]
        cwb = r_prt[:, 256:512]
        cbs = r_prt[:, 512:768]
        kvt = r_prt[:, 768:768 + 2 * C].rearrange("p (i n) -> p i n", i=IMG)
        kws = r_prt[:, 1024:1024 + 2 * C].rearrange("p (i n) -> p i n", i=IMG)
        ms = r_prt[:, 1280:1280 + 2 * C].rearrange("p (i n) -> p i n", i=IMG)
        kvx = r_prt[:, 1536:1536 + 6 * C].rearrange("p (i n) -> p i n", n=C)
        rsk = r_prt[:, 2304:2560]
        kc = r_p[:, 0:4096].rearrange("p (t n) -> p t n", t=16)
        ksq = r_stk[:, 0:4096]
        x7 = r_o[:, 0:2048]
        hid8 = r_stk[:, 0:8192].rearrange("p (b m n) -> p b m n", b=2, m=FF)
        aw1 = ww(r_tab, W3A, "aw1").rearrange("p (f t m n) -> p f t m n", f=2, t=2, m=4)
        aw2 = ww(r_tab, W3A, "aw2").rearrange("p (f t m n) -> p f t m n", f=2, t=2, m=4)

        scr = nc.dram_tensor("scr", (2, 2, 3, C, T), BF16, kind="Internal").ap()
        block = ctx.enter_context(nc.Block())

        def tile(t):
            return slice(t * TILE, (t + 1) * TILE)

        def mm(out, lhsT, rhs, start=True, stop=True, **kw):
            return nc.tensor.matmul(out, lhsT, rhs, start=start, stop=stop, **kw)

        seg = {}
        for rb in range(H // CROWS):
            a, b = query_rows(rb)
            seg[rb] = [(s, max(a, 16 * s), min(b, 16 * s + 16)) for s in range(2) if max(a, 16 * s) < min(b, 16 * s + 16)]
        U0 = TOK // 128 * HG + 1
        U2 = TILE // 128 * HG + 1
        LEAD0, LEAD2 = 6, 5
        NB2 = 2 * NB

        @block.sync
        def _(sp):
            sp.dma_start(w0[:, :], io["w0"]).then_inc(sem("in_w0"), 16)
            sp.dma_start(vec[:, :], io["vec"]).then_inc(sem("in_vec"), 16)
            for t in range(NT):
                sp.dma_start(xt[:, tile(t)], io["xT"][:, tile(t)]).then_inc(sem(f"in_x{t}"), 16)
            sp.dma_start(x2[:, :], io["xK"]).then_inc(sem("in_xK"), 16)
            sp.dma_start(cst[:, :], io["cst"]).then_inc(sem("in_cst"), 16)
            sp.dma_start(u_raw, io["tab2"]).then_inc(sem("in_u"), 16)
            sp.dma_start(r_tab[:, 0:TAB1], io["tab1"]).then_inc(sem("in_tab1"), 16)
            sp.dma_start(w2[:, :], io["w2"]).then_inc(sem("in_w2"), 16)

            def load_stack(layer, b):
                img, g, s = b // NG, b % NG, b % 3
                for a, pick in enumerate((Q_PARTS, K_PARTS)):
                    for r in range(6):
                        src = scr[layer // 2, a, pick[r], 64 * g:64 * g + 64, img * TOK:(img + 1) * TOK]
                        sp.dma_start(stk[HD * r:HD * (r + 1), s, a], src.rearrange("(h j) n -> j h n", h=HG))\
                            .then_inc(sem(f"stk{layer}_{b}"), 16)
                if layer == 0:
                    sp.dma_start(stk[96:96 + RMOD + 2, s, 1], io["mrows"][0:RMOD + 2]).then_inc(sem(f"stk{layer}_{b}"), 16)
                    sp.dma_start(stk[96:96 + RMOD, s, 0], io["mrows"][RMOD + 2:2 * RMOD + 2]).then_inc(sem(f"stk{layer}_{b}"), 16)
                else:
                    sp.dma_start(stk[96:98, s, 1], io["mrows"][RMOD:RMOD + 2]).then_inc(sem(f"stk{layer}_{b}"), 16)

            def stacks(layer):
                for t in range(NT):
                    for a in range(2):
                        sp.wait_ge(sem("split"), 2 * NT * (layer // 2) + 2 * t + a + 1)
                        sp.dma_start(scr[layer // 2, a].rearrange("r p n -> p r n")[:, :, tile(t)],
                                     parts[:, t % 2, a]).then_inc(sem(f"parts_out{layer}_{t}"), 16)
                    if t % 2:
                        sp.wait_ge(sem(f"parts_out{layer}_{t - 1}"), 32)
                        sp.wait_ge(sem(f"parts_out{layer}_{t}"), 32)
                        for g in range(NG):
                            b = t // 2 * NG + g
                            if b < 3:
                                load_stack(layer, b)

            stacks(0)
            for b in range(NB):
                sp.wait_ge(sem("p1_taken0"), U0 * (b + 1))
                for part in range(2):
                    sp.dma_start(stk[K1_L0 + part:K1_L0 + part + 1, b % 3, 0].rearrange("p h (a n) -> p (h a) n", n=128),
                                 mt[32 * part:32 * part + 32, :]).then_inc(sem("mrow0"), 16)
                if b == 1:
                    sp.wait_ge(sem("pv0"), NCH)
                    load_stack(0, 3)
            sp.wait_ge(sem("pv0"), NCH * NB)
            sp.dma_start(r_tab[:, 0:W3N], io["w3"]).then_inc(sem("in_w3"), 16)

            sp.wait_ge(sem("og"), 8)
            sp.wait_ge(sem("lnout"), NT)
            stacks(2)
            for n in range(NB2):
                b, qh = n // 2, n % 2
                sp.wait_ge(sem("p1_taken2"), U2 * (n + 1))
                for part in range(2):
                    for h in range(HG):
                        sp.dma_start(stk[K1_L2 + part:K1_L2 + part + 1, b % 3, 0, h, tile(qh)].rearrange("p (a n) -> p a n", n=128),
                                     mt[16 * part + 4 * h:16 * part + 4 * h + 4, :]).then_inc(sem("mrow2"), 16)
                if n == 2:
                    sp.wait_ge(sem("pv2"), 2 * NCH)
                    load_stack(2, 3)
            for t in range(NT):
                sp.wait_ge(sem("y_ready"), t + 1)
                sp.dma_start(io["out"][:, tile(t)], x2[:, tile(t)]).then_inc(sem("out"), 16)
            sp.wait_ge(sem("out"), 16 * NT)

        @block.tensor
        def _(pe):
            def project(layer, src, keys, w, at, suffix):
                for t in range(NT):
                    if layer == 0:
                        pe.wait_ge(sem(f"in_x{t}"), 16)
                        pe.wait_ge(sem("wq_scaled"), 2)
                    for a, name in enumerate(("wq", "wk")):
                        if t >= 2:
                            pe.wait_ge(sem("rem"), 2 * NT * (layer // 2) + 2 * (t - 2) + a + 1)
                        if a and layer == 0:
                            pe.wait_ge(sem("in_xK"), 16)
                        mm(ps[:, 4 + 2 * (t % 2) + a, :], ww(w, at, name + suffix), (src, keys)[a][:, tile(t)]).then_inc(sem("qk"), 1)
                for j in range(4):
                    for i in range(4):
                        c = 4 * j + i
                        last = mm(ps[:, j, 128 * i:128 * i + 128], keys[:, 128 * c:128 * c + 128], ww(w, at, "wv" + suffix))
                    last.then_inc(sem("v"), 1)

            def heads_back(layer, wa, wb):
                for i in range(2 * NT):
                    t, g = i // 2, i % 2
                    mm(ps[:, i, :], dens, oraw[:, 2 * (t // 2) + g, tile(t % 2)]).then_inc(sem("den"), 1)
                for t in range(NT):
                    pe.wait_ge(sem("og"), 2 * NT * (layer - 3) + 2 * t + 2)
                    mm(ps[:, t, :], wa, og[:, 2 * t, :], stop=False)
                    mm(ps[:, t, :], wb, og[:, 2 * t + 1, :], start=False).then_inc(sem("hb"), 1)

            def norm(k, src, ready, per=1):
                for t in range(NT):
                    pe.wait_ge(sem(ready), per * (t + 1))
                    mm(ps[:, 4 + t, :], cen, src(t)).then_inc(sem("cen"), 1)
                    if t:
                        pe.wait_ge(sem("sq"), NT * k + t)
                        mm(ps[:, t - 1, :], avg, sqs[:, t - 1, :]).then_inc(sem("var"), 1)
                pe.wait_ge(sem("sq"), NT * k + NT)
                mm(ps[:, NT - 1, :], avg, sqs[:, NT - 1, :]).then_inc(sem("var"), 1)

            pe.wait_ge(sem("in_w0"), 16)
            project(0, xt, x2, w0, W0A, "")
            pe.wait_ge(sem("in_vec"), 16)
            pe.wait_ge(sem("split"), 2 * NT)
            mm(ps[:, 6, 0:1], ww(w0, W0A, "pw"), vv("bv0")).then_inc(sem("pbe_mm"), 1)

            def l0_first(i):
                b, r = i // U0, i % U0
                bank = i % 2
                if i > 1:
                    pe.wait_ge(sem("p1_taken0"), i - 1)
                if r == 0:
                    pe.wait_ge(sem(f"stk0_{b}"), 14 * 16)
                if r < U0 - 1:
                    qb, h = r // HG, r % HG
                    k0, k1 = key_rows(qb)
                    mm(ps[:, bank, 0:(k1 - k0) * W].rearrange("p (f n) -> p f n", f=2), stk[0:K1_L0, b % 3, 0, h, 128 * qb:128 * qb + 128],
                       stk[0:K1_L0, b % 3, 1, h].rearrange("p (f n) -> p f n", f=2)[:, :, k0 * CCOLS:k1 * CCOLS]).then_inc(sem("s1_0"), 1)
                else:
                    pe.wait_ge(sem("mcat0"), b + 1)
                    nc.tensor.transpose(ps[0:64, bank, 0:64].bitcast(BF16), mcat[:, :], identb[:, :]).then_inc(sem("s1_0"), 1)

            def l0_second(u):
                b, c, pair = u // 16, u // 2 % 8, u % 2
                rb, half = c % 4, c // 4
                r0, r1 = query_rows(rb)
                c0, c1 = query_cols(half)
                n = (r1 - r0) * QWIN_C
                bank = 2 + 2 * (u % 2)
                if u % 16 == 0:
                    pe.wait_ge(sem("mrow0"), 32 * (b + 1))
                if u > 1:
                    pe.wait_ge(sem("exp0"), u - 1)
                u0 = (r0 - CROWS * rb + K // 2) * QWIN_C
                for hh in range(2):
                    h = 2 * pair + hh
                    qv = stk[0:K2_L0, b % 3, 0, h].rearrange("p (r c) -> p r c", c=W)
                    out = ps[:, bank + hh, 0:n]
                    mm(out.rearrange("p (r c) -> p r c", c=QWIN_C), stk[0:K2_L0, b % 3, 1, h, 128 * c:128 * c + 128],
                       qv[:, r0:r1, c0:c1], stop=False)
                    for i in range(3):
                        last = mm(out, identb[:, :], tab2[i][:, HG * (b % NG) + h, half, u0:u0 + n], start=False, stop=i == 2)
                last.then_inc(sem("s2_0"), 1)

            def l0_values(cc_):
                b, c = cc_ // NCH, cc_ % NCH
                rb, half = c % 4, c // 4
                r0, _ = query_rows(rb)
                c0, c1 = query_cols(half)
                if c == 0:
                    if b:
                        pe.wait_ge(sem("accev0"), b)
                    for s in range(2):
                        mm(ps[:, 6 + s, :], zerob[:, 0:C], zerob[:, :])
                pe.wait_ge(sem("exp0"), 2 * cc_ + 2)
                for s, a, z in seg[rb]:
                    for h in range(HG):
                        out = ps[32 * h:32 * h + 32, 6 + s, :].rearrange("p (r c) -> p r c", c=W)[:, a - 16 * s:z - 16 * s, c0:c1]
                        last = mm(out, vaug[:, b // NG * NCH + c, HG * (b % NG) + h, :],
                                  pa0[:, (2 * cc_ + h // 2) % 4, h % 2, (a - r0) * QWIN_C:(z - r0) * QWIN_C]
                                  .rearrange("p (r c) -> p r c", c=QWIN_C),
                                  start=False, stop=True, skip_group_check=True)
                last.then_inc(sem("pv0"), 1)

            pe.wait_ge(sem("identb"), 1)
            pe.wait_ge(sem("vev0"), 4)
            issued = 0
            for s in range(NB * NCH):
                upto = min(U0 + LEAD0 + (s + 1) * U0 // NCH, NB * U0)
                if s == 0:
                    while issued < U0:
                        l0_first(issued)
                        issued += 1
                    pe.wait_ge(sem("tab2_ready"), 2)
                    pe.wait_ge(sem("pbe_ready"), 1)
                    pe.wait_ge(sem("zeros"), 3)
                while issued < (upto + issued + 1) // 2:
                    l0_first(issued)
                    issued += 1
                l0_second(2 * s)
                while issued < upto:
                    l0_first(issued)
                    issued += 1
                l0_second(2 * s + 1)
                if s:
                    l0_values(s - 1)
            l0_values(NB * NCH - 1)
            pe.wait_ge(sem("accev0"), NB)

            heads_back(3, ww(w0, W0A, "pwg0"), ww(w0, W0A, "pwg1"))
            for t in range(NT):
                pe.wait_ge(sem("lnd"), 5 + t)
                mm(ps[0:C // 4, 4 + t, :], ww(w0, W0A, "g1w"), xt[:, tile(t)]).then_inc(sem("g1"), 1)
            for t in range(NT):
                pe.wait_ge(sem("g1r"), t + 1)
                mm(ps[:, 4 + t, :], ww(w0, W0A, "g2w")[0:C // 4, :], g1s[:, t, :]).then_inc(sem("g2"), 1)
            norm(0, lambda t: ysum[:, t, :], "y3")

            pe.wait_ge(sem("kd"), 9)
            for t in range(NT):
                img, r0 = t // 2, 16 * (t % 2)
                pe.wait_ge(sem("lnout"), 2 * (img + 1))
                for i in range(9):
                    dy, dx = i // 3, i % 3
                    last = mm(ps[:, t, :], kd[:, i, :], pad[:, img, r0 + dy:r0 + dy + 16, dx:dx + W], start=i == 0, stop=i == 8)
                last.then_inc(sem("conv"), 1)

            pe.wait_ge(sem("in_w2"), 16)
            pe.wait_ge(sem("x2_ready"), NT)
            pe.wait_ge(sem("lnout"), NT)
            project(2, x2, x2, w2, W2A, "2")

            def l2_first(i):
                n, r = i // U2, i % U2
                b, qh = n // 2, n % 2
                bank = 2 * (i % 2)
                if i > 1:
                    pe.wait_ge(sem("p1_taken2"), i - 1)
                if n % 2 == 0 and r == 0:
                    pe.wait_ge(sem(f"stk2_{b}"), 13 * 16)
                if r < U2 - 1:
                    qt, h = r // HG, r % HG
                    q0 = qh * TILE + 128 * qt
                    for kh in range(2):
                        last = mm(ps[:, bank + kh, :], stk[0:K1_L2, b % 3, 0, h, q0:q0 + 128],
                                  stk[0:K1_L2, b % 3, 1, h, tile(kh)])
                    last.then_inc(sem("s1_2"), 1)
                else:
                    pe.wait_ge(sem("mcat2"), n + 1)
                    nc.tensor.transpose(ps[0:32, bank, 0:64].bitcast(BF16), mcat[:, 0:32], identb[:, :]).then_inc(sem("s1_2"), 1)

            def l2_second(u):
                n, c, h = u // 32, u // 4 % 8, u % 4
                b, qh = n // 2, n % 2
                if u % 32 == 0:
                    pe.wait_ge(sem("mrow2"), 128 * (n + 1))
                if u > 2:
                    pe.wait_ge(sem("exp2"), u - 2)
                mm(ps[:, 4 + u % 3, :], stk[0:K2_L2, b % 3, 1, h, 128 * c:128 * c + 128],
                   stk[0:K2_L2, b % 3, 0, h, tile(qh)]).then_inc(sem("s2_2"), 1)

            def l2_values(cc_):
                n, c = cc_ // NCH, cc_ % NCH
                b = n // 2
                if c == 0:
                    if n:
                        pe.wait_ge(sem("accev2"), n)
                pe.wait_ge(sem("exp2"), 4 * cc_ + 4)
                for h in range(HG):
                    last = mm(ps[32 * h:32 * h + 32, 7, :], vaug[:, b // NG * NCH + c, HG * (b % NG) + h, :],
                              pa2[:, (4 * cc_ + h) % 12, :], start=c == 0, stop=c == NCH - 1)
                last.then_inc(sem("pv2"), 1)

            pe.wait_ge(sem("vev2"), 16)
            pe.wait_ge(sem("split"), 2 * NT + 2 * NT)
            issued = 0
            for s in range(NB2 * NCH):
                upto = min(U2 + LEAD2 + (s + 1) * U2 // NCH, NB2 * U2)
                if s == 0:
                    while issued < U2:
                        l2_first(issued)
                        issued += 1
                for h in range(HG):
                    if h % 2 == 0 and issued < upto:
                        l2_first(issued)
                        issued += 1
                    while h == 3 and issued < upto:
                        l2_first(issued)
                        issued += 1
                    l2_second(4 * s + h)
                if s:
                    l2_values(s - 1)
            l2_values(NB2 * NCH - 1)
            pe.wait_ge(sem("accev2"), NB2)

            heads_back(4, cc("sel0"), cc("sel1"))
            norm(1, lambda t: xt[:, tile(t)], "x3_ready")

            for t in range(NT):
                pe.wait_ge(sem("lnout"), NT + t + 1)
                for i in range(4):
                    last = nc.tensor.transpose(ps[:, t, 128 * i:128 * i + 128], x3n[:, t * TILE + 128 * i:t * TILE + 128 * i + 128], ident)
                last.then_inc(sem("fa"), 1)
            for t in range(NT):
                pe.wait_ge(sem("fa_ev"), t + 1)
                for i in range(4):
                    last = mm(ps[:, 4 + t, 128 * i:128 * i + 128], x3t[:, t * TILE + 128 * i:t * TILE + 128 * i + 128], cc("f1"))
                last.then_inc(sem("fb"), 1)
            for q in range(4):
                pe.wait_ge(sem("fb_ev"), 2 * (q // 2) + 2)
                for i in range(4):
                    last = nc.tensor.transpose(ps[:, q, 128 * i:128 * i + 128], a1[:, q * TILE + 128 * i:q * TILE + 128 * i + 128], ident)
                last.then_inc(sem("fc"), 1)
            pe.wait_ge(sem("fb_ev"), 4)
            d0 = cc("d0").rearrange("p (o n) -> p o n", o=2)
            dg = cc("dg").rearrange("p (o n) -> p o n", o=2)
            for m in range(4):
                img, half = m // 2, m % 2
                pe.wait_ge(sem("fc_ev"), 2 * img + 2)
                bank = (5, 6, 7, 0)[m]
                if m == 3:
                    pe.wait_ge(sem("fc_ev"), 4)
                for ro in range(2):
                    o = slice(64 * ro, 64 * ro + 64)
                    for j in range(8):
                        wgt = zt[:, (8 * img + j) * C + 64 * half:(8 * img + j) * C + 64 * half + 64]
                        if j == 0:
                            last = mm(ps[o, 4, 96 * m:96 * m + 96], wgt, d0[:, ro, :])
                        else:
                            last = mm(ps[o, bank, 64 * (j - 1):64 * j], wgt, dg[:, ro, :])
                last.then_inc(sem("fd"), 1)

            pe.wait_ge(sem("in_w3"), 16)
            pe.wait_ge(sem("aw_signed"), 2)
            pe.wait_ge(sem("fdA"), 4)
            pe.wait_ge(sem("fdD"), 4)

            def af_up(q):
                half, (o, n) = q // 3, ftiles[q % 3]
                for m in range(8):
                    cnt = 8 * q + m
                    if cnt >= 6:
                        pe.wait_ge(sem("ahA" if cnt % 2 == 0 else "ahD"), (cnt - 6) // 2 + 1)
                    mm(ps[:, cnt % 6, 0:n], aw1[:, half, m // 4, m % 4, :], sf[half][:, o:o + n])\
                        .then_inc(sem("au"), 1)

            def af_down(q):
                half, (o, n) = q // 3, ftiles[q % 3]
                pe.wait_ge(sem("ahA"), 4 * (q + 1))
                pe.wait_ge(sem("ahD"), 4 * (q + 1))
                if q > 1:
                    pe.wait_ge(sem("tsh"), q - 1)
                for t in range(2):
                    for p in range(4):
                        last = mm(ps[32 * p:32 * p + 32, 6 + q % 2, 0:n], aw2[:, half, t, p, :],
                                  hid[:, q % 2, 4 * t + p, 0:n], start=t == 0, stop=t == 1)
                last.then_inc(sem("ad"), 1)

            for q in range(6):
                af_up(q)
                if q:
                    af_down(q - 1)
            af_down(5)

            pe.wait_ge(sem("ahA"), 24)
            pe.wait_ge(sem("ahD"), 24)
            for i in range(18):
                kp, half = i // 2, i % 2
                pe.wait_ge(sem("yf"), 6 if half else 3)
                o = min(128 * kp, NF - 128)
                last = nc.tensor.transpose(ps[:, i // 4, 128 * (i % 4):128 * (i % 4) + 128], yf[half][:, o:o + 128], ident)
                if i % 4 == 3 or i == 17:
                    last.then_inc(sem("ba"), 1)
            for kp in range(9):
                pe.wait_ge(sem("ba_ev"), 2 * (kp // 2 + 1))
                if kp == 0:
                    pe.wait_ge(sem("tsh"), 6)
                if kp > 2:
                    pe.wait_ge(sem("bb_ev"), kp - 2)
                bank = 5 + kp % 3
                rows = slice(64, 128) if kp == 8 else slice(0, 128)
                for half in range(2):
                    for part in range(2):
                        e = cc(f"e0{part}" if kp == 0 else f"eg{part}").rearrange("p (i f h) -> p i f h", i=IMG, h=H)
                        if kp == 8:
                            e = e[:, :, 2:4, :]
                        n = 128 if kp in (0, 8) else 256
                        last = mm(ps[64 * half:64 * half + 64, bank, 0:n], yt[rows, part, 64 * (2 * kp + half):64 * (2 * kp + half) + 64], e[rows], start=part == 0, stop=part == 1)
                last.then_inc(sem("bb"), 1)
            for q in range(4):
                pe.wait_ge(sem("bb_ev"), 9)
                pe.wait_ge(sem("ba_ev"), 10)
                for i in range(4):
                    last = nc.tensor.transpose(ps[:, q, 128 * i:128 * i + 128], zf[:, q * TILE + 128 * i:q * TILE + 128 * i + 128], ident)
                last.then_inc(sem("bc"), 1)
            for t in range(NT):
                pe.wait_ge(sem("bc_ev"), t + 1)
                for i in range(4):
                    last = mm(ps[:, 4 + t, 128 * i:128 * i + 128], zt2[:, t * TILE + 128 * i:t * TILE + 128 * i + 128], cc("g"))
                last.then_inc(sem("bd"), 1)
            norm(2, lambda t: x4[:, tile(t)], "x4_ready")

            pe.wait_ge(sem("lnout"), 2 * NT + NT)
            for a, name in enumerate(("wk3", "wv3")):
                mm(ps[:, 0, 128 * a:128 * a + 128], ww(r_tab, W3A, name), cc("cenhead"))
            pe.wait_ge(sem("cbs"), 2)
            mm(ps[:, 1, 0:256], ones[:, :], cbs).then_inc(sem("gw"), 1)
            for j in range(8):
                if j == 0:
                    pe.wait_ge(sem("gw_ev"), 2)
                for i in range(2):
                    tk = 2 * j + i
                    last = mm(ps[:, j, 256 * i:256 * i + 256], h5[:, 128 * tk:128 * tk + 128], cw)
                last.then_inc(sem("gk"), 1)
            for img in range(IMG):
                for i in range(8):
                    pe.wait_ge(sem("kn"), 4 * img + i // 2 + 1)
                    tk = 8 * img + i
                    if i == 0:
                        pe.wait_ge(sem("kc"), 8)
                    st, sp_ = i == 0, i == 7
                    mm(ps[:, 3 * img, 0:128], kc[:, tk, 128:256], kc[:, tk, 0:128], start=st, stop=sp_)
                    mm(ps[:, 3 * img + 1, 0:1], kc[:, tk, 128:256], ones[:, 0:1], start=st, stop=sp_)
                    last = mm(ps[:, 3 * img + 2, 0:128], ones[:, :], kc[:, tk, 0:128], start=st, stop=sp_)
                last.then_inc(sem("kv"), 1)
            for img in range(IMG):
                pe.wait_ge(sem("kvt"), img + 1)
                mm(ps[:, 6, 128 * img:128 * img + 128], kvt[:, img, :], ww(r_tab, W3A, "wo3")).then_inc(sem("kw"), 1)
                pe.wait_ge(sem("kw_ev"), img + 1)
                mm(ps[:, 7, 128 * img:128 * img + 128], ww(r_tab, W3A, "wq3"), kws[:, img, :])
                mm(ps[:, 7, 256 + img:257 + img], kws[:, img, :], vv("bq3")).then_inc(sem("km"), 1)
                pe.wait_ge(sem("km_ev"), 2 * img + 2)
            for t in range(NT):
                if t == 0:
                    pe.wait_ge(sem("kvt"), IMG)
                mm(ps[:, t, :], ms[:, t // 2, :], h5[:, tile(t)]).then_inc(sem("att"), 1)
            norm(3, lambda t: xt[:, tile(t)], "x6_ready")

            pe.wait_ge(sem("lnout"), 3 * NT + NT)

            def up(t):
                for m in range(FF):
                    cnt = FF * t + m
                    if cnt > 5:
                        pe.wait_ge(sem("gelu"), cnt - 5)
                    mm(ps[:, cnt % 6, :], ww(r_tab, W3A, "wup")[:, 128 * m:128 * m + 128], x7[:, tile(t)]).then_inc(sem("up"), 1)

            def down(t):
                pe.wait_ge(sem("gelu"), FF * (t + 1))
                if t > 1:
                    pe.wait_ge(sem("y_ready"), t - 1)
                for m in range(FF):
                    last = mm(ps[:, 6 + t % 2, :], ww(r_tab, W3A, "wdn")[:, 128 * m:128 * m + 128], hid8[:, t % 2, m, :],
                              start=m == 0, stop=m == FF - 1)
                last.then_inc(sem("down"), 1)

            for t in range(NT):
                up(t)
                if t:
                    down(t - 1)
            down(NT - 1)

        @block.scalar
        def _(act):
            def split(layer, bq, bk):
                for i in range(2 * NT + 1):
                    if i < 2 * NT:
                        t, a = i // 2, i % 2
                        act.wait_ge(sem("qk"), 2 * NT * (layer // 2) + i + 1)
                        if t >= 2:
                            act.wait_ge(sem(f"parts_out{layer}_{t - 2}"), 32)
                        nc.scalar.activation(parts[:, t % 2, a, 0, :], ps[:, 4 + 2 * (t % 2) + a, :], ACT.Identity,
                                             bias=vv((bq, bk)[a])).then_inc(sem("hi"), 1)
                    if i:
                        t, a = (i - 1) // 2, (i - 1) % 2
                        act.wait_ge(sem("rem"), 2 * NT * (layer // 2) + i)
                        nc.scalar.activation(parts[:, t % 2, a, 1, :], rem[:, (i - 1) % 2, :], ACT.Copy).then_inc(sem("mid"), 1)

            def normalise(layer):
                for i in range(2 * NT + 1):
                    if i < 2 * NT:
                        act.wait_ge(sem("den"), 2 * NT * (layer - 3) + i + 1)
                        nc.scalar.activation(rec[:, i, :], ps[:, i, :], ACT.Ln).then_inc(sem("lnd"), 1)
                    if i:
                        act.wait_ge(sem("lnd"), 2 * NT * (layer - 3) + i)
                        nc.scalar.activation(rec[:, i - 1, :], rec[:, i - 1, :], ACT.Exp, scale=-1.0).then_inc(sem("rec"), 1)

            def norm(k):
                for t in range(NT + 1):
                    if t < NT:
                        act.wait_ge(sem("cen"), NT * k + t + 1)
                        nc.scalar.activation(sqs[:, t, :], ps[:, 4 + t, :], ACT.Square).then_inc(sem("sq"), 1)
                    if t:
                        act.wait_ge(sem("var"), NT * k + t)
                        nc.scalar.activation(rss[:, t - 1, :], ps[:, t - 1, :], ACT.Ln, bias=eps).then_inc(sem("lv"), 1)
                        act.wait_ge(sem("lv"), NT * k + t)
                        nc.scalar.activation(rss[:, t - 1, :], rss[:, t - 1, :], ACT.Exp, scale=-0.5).then_inc(sem("rs"), 1)

            logexp = "natural_log_exp_and_others"
            nc.scalar.preload_act_table_set(logexp)
            act.wait_ge(sem("in_vec"), 16)
            act.wait_ge(sem("wq_scaled"), 2)
            split(0, "bq0", "bk0")
            act.wait_ge(sem("vaug0"), 2)
            for j in range(4):
                act.wait_ge(sem("v"), j + 1)
                nc.scalar.activation(vaug[:, 4 * j:4 * j + 4, :, 0:HD],
                                     ps[:, j, :].rearrange("p (c h d) -> p c h d", c=4, h=NH), ACT.Copy).then_inc(sem("vev0"), 1)
            act.wait_ge(sem("in_cst"), 16)
            nc.scalar.activation(identb[:, :], ident, ACT.Copy).then_inc(sem("identb"), 1)
            act.wait_ge(sem("pbe_mm"), 1)
            nc.scalar.activation(pbe, ps[:, 6, 0:1], ACT.Identity, bias=vv("pb0")).then_inc(sem("pbe_ready"), 1)
            act.wait_ge(sem("in_u"), 16)
            for i in range(2):
                s = slice(HT * i, HT * (i + 1))
                nc.scalar.activation(tab2f[0][:, s], u_raw[:, s], ACT.Copy).then_inc(sem("tab_hi"), 1)
            for i in range(2):
                s = slice(HT * i, HT * (i + 1))
                act.wait_ge(sem("tab_rem"), i + 1)
                nc.scalar.activation(tab2f[1][:, s], u_raw[:, s], ACT.Copy).then_inc(sem("tab_mid"), 1)

            def take0(b):
                act.wait_ge(sem("pv0"), NCH * (b + 1))
                nc.scalar.activation(oraw[:, b, :], ps[:, 6:8, :].rearrange("p s n -> p (s n)"), ACT.Copy).then_inc(sem("accev0"), 1)

            act.wait_ge(sem("tab2_ready"), 2)
            for u in range(16 * NB):
                r0, r1 = query_rows(u // 2 % 4)
                n = (r1 - r0) * QWIN_C
                bank = 2 + 2 * (u % 2)
                act.wait_ge(sem("s2_0"), u + 1)
                if u >= 4:
                    act.wait_ge(sem("pv0"), (u - 4) // 2 + 1)
                nc.scalar.activation(pa0[:, u % 4, :, 0:n], ps[:, bank:bank + 2, 0:n], ACT.Exp).then_inc(sem("exp0"), 1)
                if u % 16 == 1 and u > 16:
                    take0(u // 16 - 1)
            take0(NB - 1)

            normalise(3)
            for t in range(NT):
                act.wait_ge(sem("g1"), t + 1)
                nc.scalar.activation(g1s[:, t, :], ps[0:C // 4, 4 + t, :], ACT.Relu, bias=vv("g1b")[0:C // 4, :]).then_inc(sem("g1r"), 1)
            for t in range(NT):
                act.wait_ge(sem("g2"), t + 1)
                nc.scalar.activation(gate[:, t, :], ps[:, 4 + t, :], ACT.Sigmoid, bias=vv("g2b")).then_inc(sem("sig"), 1)
            nc.scalar.preload_act_table_set(logexp)
            norm(0)
            for t in range(NT):
                act.wait_ge(sem("conv"), t + 1)
                nc.scalar.activation(x2[:, tile(t)], ps[:, t, :], ACT.Copy).then_inc(sem("x2_ready"), 1)

            split(2, "bq2", "bk2")

            def take2(n):
                act.wait_ge(sem("pv2"), NCH * (n + 1))
                nc.scalar.activation(oraw[:, n // 2, tile(n % 2)], ps[:, 7, :], ACT.Copy).then_inc(sem("accev2"), 1)

            for u in range(32 * NB2):
                act.wait_ge(sem("s2_2"), u + 1)
                if u >= 12:
                    act.wait_ge(sem("pv2"), (u - 12) // 4 + 1)
                nc.scalar.activation(pa2[:, u % 12, :], ps[:, 4 + u % 3, :], ACT.Exp).then_inc(sem("exp2"), 1)
                if u % 32 == 3 and u > 32:
                    take2(u // 32 - 1)
            take2(NB2 - 1)

            normalise(4)
            for t in range(NT):
                act.wait_ge(sem("hb"), NT + t + 1)
                nc.scalar.activation(tmp[:, t, :], ps[:, t, :], ACT.Identity, bias=gb2, scale=vv("gamma")).then_inc(sem("gx"), 1)
            norm(1)

            for t in range(NT):
                act.wait_ge(sem("fa"), t + 1)
                nc.scalar.activation(x3t[:, tile(t)], ps[:, t, :], ACT.Copy).then_inc(sem("fa_ev"), 1)
            for t in range(NT):
                act.wait_ge(sem("fc"), t + 1)
                nc.scalar.activation(zt[:, tile(t)], ps[:, t, :], ACT.Copy).then_inc(sem("fc_ev"), 1)

            def take_columns(img, half, eng_copy):
                m = 2 * img + half
                s = sf[half].rearrange("p (k i h) -> p k i h", i=IMG, h=H)
                g0 = ps[:, 4, 96 * m:96 * m + 96].rearrange("p (k h) -> p k h", h=H)
                g1 = ps[:, (5, 6, 7, 0)[m], 0:448].rearrange("p (k h) -> p k h", h=H)
                eng_copy(s[:, 0:3, img, :], g0)
                eng_copy(s[:, 3:KX, img, :], g1)

            for img in range(IMG):
                act.wait_ge(sem("fd"), 4)
                take_columns(img, 0, lambda o, i: nc.scalar.activation(o, i, ACT.Copy).then_inc(sem("fdA"), 1))

            def shrink_in(q):
                half, (o, n) = q // 3, ftiles[q % 3]
                act.wait_ge(sem("ad"), q + 1)
                if q > 1:
                    act.wait_ge(sem("yf"), q - 1)
                nc.scalar.activation(tsh[:, q % 2, 0:n], ps[:, 6 + q % 2, 0:n], ACT.Identity, bias=vv(f"ab2_{half}")).then_inc(sem("tsh"), 1)

            for q in range(6):
                half, (o, n) = q // 3, ftiles[q % 3]
                for m in range(0, 8, 2):
                    act.wait_ge(sem("au"), 8 * q + m + 1)
                    if q > 1:
                        act.wait_ge(sem("ad"), q - 1)
                    nc.scalar.activation(hid[:, q % 2, m, 0:n], ps[:, (8 * q + m) % 6, 0:n], ACT.Relu,
                                         bias=vv(f"ab1_{8 * half + m}")).then_inc(sem("ahA"), 1)
                if q:
                    shrink_in(q - 1)
            shrink_in(5)
            for i in range(5):
                act.wait_ge(sem("ba"), i + 1)
                n = 256 if i == 4 else 512
                for o in range(2):
                    nc.scalar.activation(yt[:, o, 256 * i:256 * i + n // 2].rearrange("p (m c) -> p m c", c=16),
                                         ps[:, i, 0:n].rearrange("p (m o c) -> p m o c", o=2, c=16)[:, :, o, :],
                                         ACT.Copy).then_inc(sem("ba_ev"), 1)
            for t in range(NT):
                act.wait_ge(sem("bc"), t + 1)
                nc.scalar.activation(zt2[:, tile(t)], ps[:, t, :], ACT.Copy).then_inc(sem("bc_ev"), 1)
            norm(2)

            act.wait_ge(sem("gw"), 1)
            nc.scalar.activation(cw, ps[:, 0, 0:256], ACT.Copy).then_inc(sem("gw_ev"), 1)
            nc.scalar.activation(cwb, ps[:, 1, 0:256], ACT.Copy).then_inc(sem("gw_ev"), 1)
            for j in range(8):
                act.wait_ge(sem("kc"), j + 1)
                nc.scalar.activation(ksq[:, 512 * j:512 * j + 512], kc[:, 2 * j:2 * j + 2, :].rearrange("p t n -> p (t n)"), ACT.Square).then_inc(sem("ksq"), 1)
            for i in range(2):
                s = slice(128 * i, 128 * i + 128)
                act.wait_ge(sem("kvar"), 4 * (i + 1))
                nc.scalar.activation(rsk[:, s], rsk[:, s], ACT.Ln, bias=eps, scale=1.0 / DH_G).then_inc(sem("klv"), 1)
                act.wait_ge(sem("klv"), i + 1)
                nc.scalar.activation(rsk[:, s], rsk[:, s], ACT.Exp, scale=-0.5).then_inc(sem("krs"), 1)
            for img in range(IMG):
                act.wait_ge(sem("kw"), img + 1)
                nc.scalar.activation(kws[:, img, :], ps[:, 6, 128 * img:128 * img + 128], ACT.Copy).then_inc(sem("kw_ev"), 1)
                act.wait_ge(sem("km"), img + 1)
                nc.scalar.activation(ms[:, img, :], ps[:, 7, 128 * img:128 * img + 128], ACT.Copy).then_inc(sem("km_ev"), 1)
                nc.scalar.activation(bvecs[:, img:img + 1], ps[:, 7, 256 + img:257 + img], ACT.Identity, bias=vv("bo3")).then_inc(sem("km_ev"), 1)
            norm(3)
            for cnt in range(FF * NT):
                t, m = cnt // FF, cnt % FF
                act.wait_ge(sem("up"), cnt + 1)
                if t > 1:
                    act.wait_ge(sem("down"), t - 1)
                nc.scalar.activation(hid8[:, t % 2, m, :], ps[:, cnt % 6, :], ACT.Gelu, bias=vv(f"bup{m}")).then_inc(sem("gelu"), 1)

        @block.vector
        def _(dve):
            v = nc.vector

            def split(layer, bq, bk):
                for i in range(2 * NT + 1):
                    if i < 2 * NT:
                        t, a = i // 2, i % 2
                        dve.wait_ge(sem("hi"), 2 * NT * (layer // 2) + i + 1)
                        if i > 1:
                            dve.wait_ge(sem("mid"), 2 * NT * (layer // 2) + i - 1)
                        if i > 1:
                            dve.wait_ge(sem("split"), 2 * NT * (layer // 2) + i - 1)
                        v.scalar_tensor_tensor(rem[:, i % 2, :], ps[:, 4 + 2 * (t % 2) + a, :], vv((bq, bk)[a]),
                                               parts[:, t % 2, a, 0, :], ALU.add, ALU.subtract).then_inc(sem("rem"), 1)
                    if i:
                        t, a = (i - 1) // 2, (i - 1) % 2
                        dve.wait_ge(sem("mid"), 2 * NT * (layer // 2) + i)
                        v.tensor_tensor(parts[:, t % 2, a, 2, :], rem[:, (i - 1) % 2, :], parts[:, t % 2, a, 1, :],
                                        ALU.subtract).then_inc(sem("split"), 1)

            def maxima(layer, base, nu, k, done):
                dve.wait_ge(sem(f"p1_taken{layer}"), base + nu - 1)
                v.tensor_scalar(mcat[:, 0:k], mx[:, 0:k], -1.0, None, ALU.mult).then_inc(sem(f"mhi{layer}"), 1)
                dve.wait_ge(sem(f"mhi{layer}"), done + 1)
                v.scalar_tensor_tensor(mcat[:, k:2 * k], mx[:, 0:k], -1.0, mcat[:, 0:k], ALU.mult, ALU.subtract)\
                    .then_inc(sem(f"mcat{layer}"), 1)
                dve.wait_ge(sem(f"s1_{layer}"), base + nu)
                if done:
                    dve.wait_ge(sem(f"mrow{layer}"), (32 if layer == 0 else 128) * done)
                bank = (base + nu - 1) % 2 * (1 if layer == 0 else 2)
                v.tensor_copy(mt[0:2 * k, :], ps[0:2 * k, bank, 0:64].bitcast(BF16)).then_inc(sem(f"p1_taken{layer}"), 1)

            def normalised(layer):
                for i in range(2 * NT):
                    dve.wait_ge(sem("rec"), 2 * NT * (layer - 3) + i + 1)
                    v.tensor_tensor(og[:, i, :], oraw[:, 2 * (i // 4) + i % 2, tile(i // 2 % 2)], rec[:, i, :], ALU.mult)\
                        .then_inc(sem("og"), 1)

            def norm(k, g, b, out, per=1):
                for t in range(NT):
                    dve.wait_ge(sem("rs"), NT * k + t + 1)
                    v.scalar_tensor_tensor(t1s[:, t, :], ps[:, 4 + t, :], vv(g), rss[:, t, :], ALU.mult, ALU.mult).then_inc(sem("ng"), 1)
                    dve.wait_ge(sem("ng"), NT * k + t + 1)
                    dst, src = out(t), t1s[:, t, :]
                    if len(dst.shape) == 3:
                        src = src.rearrange("p (r c) -> p r c", c=W)
                    v.tensor_scalar(dst, src, vv(b), None, ALU.add).then_inc(sem("lnout"), 1)

            dve.wait_ge(sem("in_w0"), 16)
            dve.wait_ge(sem("in_vec"), 16)
            scale = float(HD) ** -0.5
            v.tensor_scalar(ww(w0, W0A, "wq"), ww(w0, W0A, "wq"), scale, None, ALU.mult).then_inc(sem("wq_scaled"), 1)
            v.tensor_scalar(vv("bq0"), vv("bq0"), scale, None, ALU.mult).then_inc(sem("wq_scaled"), 1)
            v.tensor_scalar(gb2, vv("bv2"), vv("gamma"), None, ALU.mult).then_inc(sem("gb2"), 1)
            split(0, "bq0", "bk0")
            for i in range(2):
                s = slice(HT * i, HT * (i + 1))
                dve.wait_ge(sem("tab_hi"), i + 1)
                v.tensor_tensor(u_raw[:, s], u_raw[:, s], tab2f[0][:, s], ALU.subtract).then_inc(sem("tab_rem"), 1)
            for i in range(2):
                s = slice(HT * i, HT * (i + 1))
                dve.wait_ge(sem("tab_mid"), i + 1)
                v.tensor_tensor(tab2f[2][:, s], u_raw[:, s], tab2f[1][:, s], ALU.subtract).then_inc(sem("tab2_ready"), 1)

            dve.wait_ge(sem("in_tab1"), 16)
            for b in range(NB):
                for r in range(U0 - 1):
                    i = U0 * b + r
                    qb, h = r // HG, r % HG
                    k0, k1 = key_rows(qb)
                    n = (k1 - k0) * W
                    o = (k0 - QROWS * qb + K // 2) * CCOLS
                    dve.wait_ge(sem("s1_0"), i + 1)
                    if i > 1:
                        dve.wait_ge(sem("p1_taken0"), i - 1)
                    if r == 0:
                        if b:
                            dve.wait_ge(sem("mcat0"), b)
                    v.tensor_tensor_reduce(junk[:, i % 2, 0:n].rearrange("p (f n) -> p f n", f=2),
                                           ps[:, i % 2, 0:n].rearrange("p (f n) -> p f n", f=2),
                                           tab1[:, HG * (b % NG) + h, :, o:o + n // 2],
                                           1.0, -3.0e38, ALU.add, ALU.max, mx[:, 8 * h + qb:8 * h + qb + 1])\
                        .then_inc(sem("p1_taken0"), 1)
                maxima(0, U0 * b, U0, 32, b)

            normalised(3)
            for t in range(NT):
                dve.wait_ge(sem("hb"), t + 1)
                dve.wait_ge(sem("sig"), t + 1)
                v.scalar_tensor_tensor(tmp[:, t, :], ps[:, t, :], pbe, gate[:, t, :], ALU.add, ALU.mult).then_inc(sem("yg"), 1)
                dve.wait_ge(sem("yg"), t + 1)
                v.tensor_tensor(ysum[:, t, :], tmp[:, t, :], xt[:, tile(t)], ALU.add).then_inc(sem("y3"), 1)
            dve.wait_ge(sem("pad0"), 1)
            norm(0, "lng0", "lnb0", lambda t: pad[:, t // 2, 1 + 16 * (t % 2):17 + 16 * (t % 2), 1:1 + W])

            split(2, "bq2", "bk2")
            dve.wait_ge(sem("vaug2"), 1)
            for j in range(4):
                dve.wait_ge(sem("v"), NT + j + 1)
                for i in range(4):
                    c = 4 * (j % 2) + i
                    v.tensor_scalar(vaug[:, 4 * j + i, :, 0:HD], ps[:, j, 128 * i:128 * i + 128].rearrange("p (h d) -> p h d", h=NH),
                                    cc("mult")[:, c:c + 1], None, ALU.mult).then_inc(sem("vev2"), 1)
            for n in range(NB2):
                for r in range(U2 - 1):
                    i = U2 * n + r
                    qt, h = r // HG, r % HG
                    bank = 2 * (i % 2)
                    dve.wait_ge(sem("s1_2"), i + 1)
                    if r == 0:
                        if n:
                            dve.wait_ge(sem("mcat2"), n)
                    v.tensor_reduce(mx[:, 4 * h + qt:4 * h + qt + 1], ps[:, bank:bank + 2, :], AXIS.XY, ALU.max)\
                        .then_inc(sem("p1_taken2"), 1)
                maxima(2, U2 * n, U2, 16, n)

            normalised(4)
            for t in range(NT):
                dve.wait_ge(sem("gx"), t + 1)
                v.tensor_tensor(xt[:, tile(t)], tmp[:, t, :], x2[:, tile(t)], ALU.add).then_inc(sem("x3_ready"), 1)
            norm(1, "n1g", "n1b", lambda t: x3n[:, tile(t)])

            for t in range(NT):
                dve.wait_ge(sem("fb"), t + 1)
                dst = a1.rearrange("p (i j h f) -> p i j h f", i=IMG, j=8, h=H)[:, t // 2, :, 16 * (t % 2):16 * (t % 2) + 16, :]
                v.tensor_copy(dst, ps[:, 4 + t, :].rearrange("p (h j f) -> p j h f", j=8, f=4)).then_inc(sem("fb_ev"), 1)
            for img in range(IMG):
                dve.wait_ge(sem("fd"), 4)
                m = 2 * img + 1
                s = sf[1].rearrange("p (k i h) -> p k i h", i=IMG, h=H)
                v.tensor_copy(s[:, 3:KX, img, :], ps[:, (5, 6, 7, 0)[m], 0:448].rearrange("p (k h) -> p k h", h=H)).then_inc(sem("fdD"), 1)
            dve.wait_ge(sem("fdA"), 4)
            for img in range(IMG):
                m = 2 * img + 1
                v.tensor_copy(s[:, 0:3, img, :], ps[:, 4, 96 * m:96 * m + 96].rearrange("p (k h) -> p k h", h=H)).then_inc(sem("fdD"), 1)

            def shrink(q):
                half, (o, n) = q // 3, ftiles[q % 3]
                dve.wait_ge(sem("tsh"), q + 1)
                v.tensor_scalar(csh[:, q % 2, 0:n], tsh[:, q % 2, 0:n], 0.01, -0.01, ALU.min, ALU.max).then_inc(sem("csh"), 1)
                dve.wait_ge(sem("csh"), q + 1)
                v.tensor_tensor(yf[half][:, o:o + n], tsh[:, q % 2, 0:n], csh[:, q % 2, 0:n], ALU.subtract).then_inc(sem("yf"), 1)

            for q in range(6):
                half, (o, n) = q // 3, ftiles[q % 3]
                for m in range(1, 8, 2):
                    dve.wait_ge(sem("au"), 8 * q + m + 1)
                    if q > 1:
                        dve.wait_ge(sem("ad"), q - 1)
                    v.tensor_scalar(hid[:, q % 2, m, 0:n], ps[:, (8 * q + m) % 6, 0:n], vv(f"ab1_{8 * half + m}"), 0.0,
                                    ALU.add, ALU.max).then_inc(sem("ahD"), 1)
                if q:
                    shrink(q - 1)
            shrink(5)
            zv = zf.rearrange("p (i h f) -> p i f h", i=IMG, f=W)
            for kp in range(9):
                dve.wait_ge(sem("bb"), kp + 1)
                n, f0, fn = (128, 0, 2) if kp == 0 else (128, 30, 2) if kp == 8 else (256, 4 * kp - 2, 4)
                v.tensor_copy(zv[:, :, f0:f0 + fn, :], ps[:, 5 + kp % 3, 0:n].rearrange("p (i f h) -> p i f h", i=IMG, h=H))\
                    .then_inc(sem("bb_ev"), 1)
            for t in range(NT):
                dve.wait_ge(sem("bd"), t + 1)
                v.tensor_tensor(x4[:, tile(t)], ps[:, 4 + t, :], x3n[:, tile(t)], ALU.add).then_inc(sem("x4a"), 1)
                dve.wait_ge(sem("x4a"), t + 1)
                v.tensor_tensor(x4[:, tile(t)], x4[:, tile(t)], xt[:, tile(t)], ALU.add).then_inc(sem("x4_ready"), 1)
            norm(2, "n2g", "n2b", lambda t: h5[:, tile(t)])

            for a, b in enumerate(("bk3", "bv3")):
                v.tensor_scalar(cbs[:, 128 * a:128 * a + 128], cc("cenhead"), vv(b), None, ALU.mult).then_inc(sem("cbs"), 1)
            dve.wait_ge(sem("gw_ev"), 2)
            bias2 = cwb.unsqueeze(1).to_broadcast([C, 2, 256])
            for j in range(8):
                dve.wait_ge(sem("gk"), j + 1)
                v.tensor_tensor(kc[:, 2 * j:2 * j + 2, :], ps[:, j, :].rearrange("p (t n) -> p t n", t=2), bias2, ALU.add).then_inc(sem("kc"), 1)
            for j in range(8):
                dve.wait_ge(sem("ksq"), j + 1)
                v.tensor_reduce(rsk[:, 32 * j:32 * j + 32], ksq[:, 512 * j:512 * j + 512].rearrange("p (g d) -> p g d", d=DH_G),
                                AXIS.X, ALU.add).then_inc(sem("kvar"), 1)
            for j in range(8):
                dve.wait_ge(sem("krs"), j // 4 + 1)
                kv_ = kc[:, 2 * j:2 * j + 2, :].rearrange("p t (g d) -> p (t g) d", d=DH_G)
                v.tensor_tensor(kv_, kv_, rsk[:, 32 * j:32 * j + 32].unsqueeze(2).to_broadcast([C, 32, DH_G]), ALU.mult)\
                    .then_inc(sem("kn"), 1)
            done = [0]

            def step(ins):
                done[0] += 1
                ins.then_inc(sem("kvchain"), 1)
                dve.wait_ge(sem("kvchain"), done[0])

            lkg, lkb = ww(r_tab, W3A, "lkg"), ww(r_tab, W3A, "lkb")
            for img in range(IMG):
                dve.wait_ge(sem("kv"), img + 1)
                step(v.tensor_copy(sv, ps[:, 3 * img + 1, 0:1]))
                step(v.tensor_tensor(kvx[:, 0, :], ps[:, 3 * img, 0:128], lkg, ALU.mult))
                step(v.scalar_tensor_tensor(kvx[:, 1, :], lkb, sv, kvx[:, 0, :], ALU.mult, ALU.add))
                step(v.tensor_tensor(kvx[:, 2, :], ps[:, 3 * img + 2, 0:128], lkg, ALU.mult))
                step(v.scalar_tensor_tensor(kvx[:, 3, :], lkb, float(TOK), kvx[:, 2, :], ALU.mult, ALU.add))
                step(v.tensor_scalar(kvx[:, 4, :], kvx[:, 1, :], vv("lvg"), None, ALU.mult))
                step(v.scalar_tensor_tensor(kvx[:, 5, :], kvx[:, 3, :], vv("lvb"), kvx[:, 4, :], ALU.mult, ALU.add))
                v.tensor_tensor(kvt[:, img, :], kvx[:, 5, :], cc("kvmask"), ALU.mult).then_inc(sem("kvt"), 1)
            for t in range(NT):
                dve.wait_ge(sem("att"), t + 1)
                v.scalar_tensor_tensor(xt[:, tile(t)], ps[:, t, :], bvecs[:, t // 2:t // 2 + 1], h5[:, tile(t)], ALU.add, ALU.add)\
                    .then_inc(sem("x6_ready"), 1)
            norm(3, "n3g", "n3b", lambda t: x7[:, tile(t)])
            for t in range(NT):
                dve.wait_ge(sem("down"), t + 1)
                v.scalar_tensor_tensor(x2[:, tile(t)], ps[:, 6 + t % 2, :], vv("bdn"), x7[:, tile(t)], ALU.add, ALU.add)\
                    .then_inc(sem("y_ready"), 1)

        @block.gpsimd
        def _(pool):
            g = nc.gpsimd
            g.memset(zerob[:, :], 0.0).then_inc(sem("zeros"), 1)
            g.memset(eps, 1e-5).then_inc(sem("zeros"), 1)
            g.memset(vaug[:, :, :, :], 0.0).then_inc(sem("vaug0"), 1)
            pool.wait_ge(sem("vaug0"), 1)
            g.memset(vaug[:, :, :, HD:HD + 1], 1.0).then_inc(sem("vaug0"), 1)
            g.memset(ones[:, :], 1.0).then_inc(sem("zeros"), 1)
            g.memset(pad[:, :, :, :], 0.0).then_inc(sem("pad0"), 1)
            pool.wait_ge(sem("in_cst"), 16)
            pool.wait_ge(sem("in_vec"), 16)
            for i in range(9):
                if i == 4:
                    g.tensor_copy(kd[:, i, :], ident).then_inc(sem("kd"), 1)
                else:
                    g.tensor_scalar(kd[:, i, :], ident, vv(f"kc{i}"), None, ALU.mult).then_inc(sem("kd"), 1)
            pool.wait_ge(sem("pv0"), NCH * NB)
            g.tensor_copy(vaug[:, :, :, HD].rearrange("p (i c) h -> p i c h", i=IMG),
                          cc("mult").unsqueeze(1).unsqueeze(3).to_broadcast([C, IMG, NCH, NH])).then_inc(sem("vaug2"), 1)
            pool.wait_ge(sem("in_w3"), 16)
            for half in range(2):
                g.tensor_scalar(aw1[:, half, 0, :, :], aw1[:, half, 0, :, :], cc("sign"), None, ALU.mult).then_inc(sem("aw1s"), 1)
            pool.wait_ge(sem("aw1s"), 2)
            for half in range(2):
                g.tensor_scalar(aw2[:, half, 1, :, 0:16], aw2[:, half, 1, :, 0:16], -1.0, None, ALU.mult).then_inc(sem("aw_signed"), 1)
    return


def bias_tables(rpb):
    n, k = NH, K - 1
    s = window(W)
    t1 = np.zeros((QROWS, W, n, KWIN, W), rpb.dtype)
    for r in range(QROWS):
        for v in range(KWIN):
            dr = v - K // 2 - r + k
            if not 0 <= dr <= 2 * k:
                continue
            for q in range(W):
                t1[r, q, :, v, :] = NEG
                t1[r, q, :, v, s[q]:s[q] + K] = rpb[:, dr, s[q] - q + k:s[q] - q + k + K]
    t1 = t1.reshape(QROWS, W, n, KWIN, 2, CCOLS).transpose(0, 1, 2, 4, 3, 5)
    t2 = np.zeros((CROWS, CCOLS, n, 2, QWIN_R, QWIN_C), rpb.dtype)
    for half in range(2):
        c0, c1 = query_cols(half)
        for kc in range(CCOLS):
            key = CCOLS * half + kc
            for j, q in enumerate(range(c0, c1)):
                inside = s[q] <= key < s[q] + K
                for r in range(CROWS):
                    for u in range(QWIN_R):
                        dr = r - (u - K // 2) + k
                        if 0 <= dr <= 2 * k:
                            t2[r, kc, :, half, u, j] = rpb[:, dr, key - q + k] if inside else NEG
    return t1.reshape(128, -1), t2.reshape(128, -1)


def pack(**a):
    f = np.float32
    heads = np.zeros((NG, 128, C), f)
    for g in range(NG):
        for h in range(HG):
            heads[g, 32 * h:32 * h + HD] = a["L0_conv_proj_w"][64 * g + HD * h:64 * g + HD * (h + 1)]

    def column(x):
        out = np.zeros((C, 1), f)
        out[:x.size, 0] = x
        return out

    def every(x):
        return np.broadcast_to(x.reshape(1, -1), (C, x.size)).astype(f)

    qkv_b = a["L0_conv_qkv_b"]
    kern = a["L1_conv_kernel"].reshape(9, C)
    b1 = a["L3_conv_afno_b1"]
    b2 = a["L3_conv_afno_b2"].reshape(2, 2, 4, 2, BS)
    v = {"bq0": column(qkv_b[0:C]), "bk0": column(qkv_b[C:2 * C]), "bv0": column(qkv_b[2 * C:]),
         "pb0": column(a["L0_conv_proj_b"]), "lng0": column(a["L0_conv_ln_g"]), "lnb0": column(a["L0_conv_ln_b"]),
         "g1b": column(a["L0_conv_g1_b"]), "g2b": every(a["L0_conv_g2_b"]),
         "bq2": column(a["L2_conv_bq"]), "bk2": column(a["L2_conv_bk"]), "bv2": column(a["L2_conv_bv"]),
         "gamma": every(a["L2_conv_gamma"]), "bq3": column(a["L3_conv_bq"]), "bk3": column(a["L3_conv_bk"]),
         "bv3": column(a["L3_conv_bv"]), "bo3": column(a["L3_conv_bo"]), "bdn": column(a["L3_conv_b_down"]),
         "lvg": column(a["L3_conv_lnv_g"].reshape(-1)), "lvb": column(a["L3_conv_lnv_b"].reshape(-1))}
    for i in range(1, 4):
        v[f"n{i}g"], v[f"n{i}b"] = column(a[f"L3_conv_n{i}_g"]), column(a[f"L3_conv_n{i}_b"])
    for i in range(9):
        v[f"kc{i}"] = column(kern[i])
    for i in range(FF):
        v[f"bup{i}"] = column(a["L3_conv_b_up"][128 * i:128 * i + 128])
    for half in range(2):
        for t in range(2):
            for p in range(4):
                v[f"ab1_{8 * half + 4 * t + p}"] = column(b1[t, 8 * half + 2 * p:8 * half + 2 * p + 2].reshape(-1))
        v[f"ab2_{half}"] = column(b2[:, half].transpose(1, 0, 2, 3).reshape(-1))
    aw1 = np.zeros((128, 2, 2, 4, 128), f)
    aw2 = np.zeros((128, 2, 2, 4, 32), f)
    w1, w2 = a["L3_conv_afno_w1"], a["L3_conv_afno_w2"]
    E = BS * EXPF
    for half in range(2):
        for t in range(2):
            for p in range(4):
                for b in range(2):
                    n = 8 * half + 2 * p + b
                    c = HD * p + BS * b
                    for part in range(2):
                        aw1[HALF * part + c:HALF * part + c + BS, half, t, p, E * b:E * (b + 1)] = w1[part ^ t, n]
                        aw2[E * b:E * (b + 1), half, t, p, 16 * part + BS * b:16 * part + BS * (b + 1)] = w2[part ^ t, n]
    w = {"wq": a["L0_conv_qkv_w"][:, 0:C], "wk": a["L0_conv_qkv_w"][:, C:2 * C], "wv": a["L0_conv_qkv_w"][:, 2 * C:],
         "pw": a["L0_conv_proj_w"], "pwg0": heads[0], "pwg1": heads[1], "g1w": a["L0_conv_g1_w"],
         "g2w": np.concatenate([np.broadcast_to(a["L0_conv_g2_w"], (C // 4, C)), np.zeros((3 * C // 4, C), f)]),
         "wq2": a["L2_conv_Wq"], "wk2": a["L2_conv_Wk"], "wv2": a["L2_conv_Wv"],
         "wq3": a["L3_conv_wq"], "wk3": a["L3_conv_wk"], "wv3": a["L3_conv_wv"], "wo3": a["L3_conv_wo"].T,
         "lkg": every(a["L3_conv_lnk_g"]), "lkb": every(a["L3_conv_lnk_b"]),
         "aw1": aw1.reshape(128, -1), "aw2": aw2.reshape(128, -1), "wup": a["L3_conv_w_up"].T,
         "wdn": a["L3_conv_w_down"].T.reshape(FF, 128, C).transpose(1, 0, 2).reshape(128, -1)}

    def row(names):
        return np.ascontiguousarray(np.concatenate([np.asarray(w[n], f) for n, _ in names], axis=1))

    t1, t2 = bias_tables(a["L0_conv_rpb"])
    xt = a["x"].reshape(IMG, TOK, C)
    return {"xT": np.ascontiguousarray(xt.reshape(T, C).T), "xK": np.ascontiguousarray(xt[:, key_order()].reshape(T, C).T), "w0": row(W0), "w2": row(W2), "w3": row(W3),
            "vec": np.ascontiguousarray(np.concatenate([v[n] for n in VEC], axis=1)),
            "cst": CONSTS, "tab1": np.ascontiguousarray(t1), "tab2": np.ascontiguousarray(t2), "mrows": mask_rows()}


def kernel(**inputs):
    import concourse.bacc as bacc
    from concourse.bass_utils import run_bass_kernel_spmd

    arrays = pack(**{k: np.asarray(a) for k, a in inputs.items()})
    nc = bacc.Bacc("TRN2", target_bir_lowering=False, num_devices=1)
    io = {n: nc.dram_tensor(f"in_{n}", a.shape, mybir.dt.from_np(a.dtype), kind="ExternalInput").ap() for n, a in arrays.items()}
    io["out"] = nc.dram_tensor("y", (C, T), F32, kind="ExternalOutput").ap()
    build(nc, io)
    r = run_bass_kernel_spmd(nc, [{f"in_{n}": a for n, a in arrays.items()}], core_ids=[0])
    y = r.results[0]["y"]
    return np.ascontiguousarray(y.T).reshape(IMG, H, W, C)
```

```python
from contextlib import ExitStack

import numpy as np

import concourse.bass as bass
from concourse import mybir

F32 = mybir.dt.float32
BF16 = mybir.dt.bfloat16
F32R = mybir.dt.float32r
ALU = mybir.AluOpType
ACT = mybir.ActivationFunctionType
AXIS = mybir.AxisListType

C = 128
IMG, H, W = 2, 32, 32
TOK = H * W
T = IMG * TOK
TILE = 512
NT = T // TILE
NH, HD = 8, 16
HG = 4
NG = NH // HG
NB = IMG * NG
K = 7
NCH = TOK // 128
NEG = -float(2 ** 100)
RMOD = 16
R_SPLIT = 6 * HD
K1_L0 = R_SPLIT + RMOD
K2_L0 = K1_L0 + 2
K1_L2 = R_SPLIT
K2_L2 = R_SPLIT + 2
Q_PARTS = (0, 0, 0, 1, 1, 2)
K_PARTS = (0, 1, 2, 0, 1, 0)
PART_RUNS = ((0, 3), (3, 5), (5, 6))
QROWS = 4
KWIN = 10
CROWS, CCOLS = 8, 16
QWIN_R, QWIN_C = 14, 20
NB_AF, BS, EXPF = 16, 8, 8
PE_TAPS = (1, 3, 4, 5)
DVE_TAPS = (0, 2, 6, 7, 8)
HALF = C // 2
KX = W // 2 + 1
NF = KX * IMG * H
DH_G = 16
FF = 8 * C // 128


def window(n):
    return np.clip(np.arange(n) - K // 2, 0, n - K)


def key_rows(qb):
    s = window(H)
    return int(s[QROWS * qb]), int(s[QROWS * qb + QROWS - 1]) + K


def query_rows(rb):
    s = window(H)
    hit = [i for i in range(H) if s[i] < CROWS * (rb + 1) and s[i] + K > CROWS * rb]
    return hit[0], hit[-1] + 1


def query_cols(half):
    return (0, QWIN_C) if half == 0 else (W - QWIN_C, W)


def key_order():
    return np.arange(TOK).reshape(H, W // CCOLS, CCOLS).transpose(1, 0, 2).reshape(-1)


def kx_order():
    return [0, W // 2] + list(range(1, W // 2))


def shape_constants():
    c = {}
    eye = np.eye(C)
    c["ident"] = eye
    c["cen"] = eye - 1.0 / C
    c["avg"] = np.full((C, C), 1.0 / C)
    den = np.zeros((C, C))
    for h in range(HG):
        den[32 * h + HD, 32 * h:32 * h + 32] = 1.0
    c["den"] = den
    for g in range(NG):
        s = np.zeros((C, C))
        for h in range(HG):
            for j in range(HD):
                s[32 * h + j, 64 * g + HD * h + j] = 1.0
        c[f"sel{g}"] = s
    pad = K // 2
    mult = np.ones(H)
    mult[1:1 + pad] += 1
    mult[H - 1 - pad:H - 1] += 1
    c["mult"] = np.outer(mult, mult).reshape(NCH, 128).T
    head = np.kron(np.eye(C // DH_G), np.ones((DH_G, DH_G)))
    c["cenhead"] = eye - head / DH_G
    c["kvmask"] = head / TOK
    k = np.arange(W)
    n = float(W) ** -0.5
    f1 = np.zeros((W, W))
    g = np.zeros((W, W))
    for f in range(W):
        kx = (0, W // 2)[f] if f < 2 else f // 2
        im = f >= 2 and f % 2
        ang = 2 * np.pi * kx * k / W
        f1[:, f] = n * (-np.sin(ang) if im else np.cos(ang))
        g[f, :] = n * (1.0 if f < 2 else 2.0) * (-np.sin(ang) if im else np.cos(ang))
    c["f1"] = np.kron(np.eye(4), f1)
    c["g"] = np.kron(np.eye(4), g)
    ch = n * np.cos(2 * np.pi * np.outer(k, k) / H)
    sh = n * np.sin(2 * np.pi * np.outer(k, k) / H)
    d0 = np.zeros((H, 4, 2, 3, H))
    d0[:, 0, 0, 0], d0[:, 0, 1, 0] = ch, -sh
    d0[:, 1, 0, 1], d0[:, 1, 1, 1] = ch, -sh
    d0[:, 2, 0, 2], d0[:, 2, 1, 2] = ch, -sh
    d0[:, 3, 0, 2], d0[:, 3, 1, 2] = sh, ch
    c["d0"] = d0.reshape(128, -1)
    dg = np.zeros((H, 4, 2, 2, H))
    for b in range(2):
        dg[:, 2 * b, 0, b], dg[:, 2 * b, 1, b] = ch, -sh
        dg[:, 2 * b + 1, 0, b], dg[:, 2 * b + 1, 1, b] = sh, ch
    c["dg"] = dg.reshape(128, -1)
    e0 = np.zeros((2, 2, IMG, H, IMG, 2, H))
    eg = np.zeros((2, 2, IMG, H, IMG, 4, H))
    for i in range(IMG):
        for b in range(2):
            e0[0, b, i, :, i, b], e0[1, b, i, :, i, b] = ch, -sh
            eg[0, b, i, :, i, 2 * b], eg[0, b, i, :, i, 2 * b + 1] = ch, sh
            eg[1, b, i, :, i, 2 * b], eg[1, b, i, :, i, 2 * b + 1] = -sh, ch
    for p in range(2):
        c[f"e0{p}"] = e0[p].reshape(128, -1)
        c[f"eg{p}"] = eg[p].reshape(128, -1)
    c["sign"] = np.where(np.arange(C) < HALF, 1.0, -1.0)[:, None]
    return c


def place_constants():
    at, parts, n = {}, [], 0
    for name, a in shape_constants().items():
        at[name] = (n, a.shape[1])
        parts.append(a.astype(np.float32))
        n += a.shape[1]
    return at, np.ascontiguousarray(np.concatenate(parts, axis=1))


CAT, CONSTS = place_constants()


def mask_rows():
    row = np.arange(TOK) // W
    s = window(H)
    k = (row[key_order()][None] % RMOD == np.arange(RMOD)[:, None]).astype(np.float32)
    q = np.full((RMOD, TOK), NEG, np.float32)
    for t in range(TOK):
        for r in range(s[row[t]], s[row[t]] + K):
            q[r % RMOD, t] = 0.0
    one = np.ones((2, TOK), np.float32)
    m = np.concatenate([k, one, q], axis=0)
    return np.repeat(m[:, None], HG, axis=1).astype(mybir.dt.np(BF16))


VEC = ["bq0", "bk0", "pb0", "lng0", "lnb0", "g1b", "g2b"] + [f"kc{i}" for i in range(9)] + \
      ["bq2", "bk2", "bv2", "gamma", "n1g", "n1b", "n2g", "n2b", "n3g", "n3b", "bq3", "bk3", "bv3", "bo3", "bdn",
       "lvg", "lvb"] + [f"bup{i}" for i in range(FF)] + [f"ab1_{i}" for i in range(16)] + ["ab2_0", "ab2_1", "bv0"]
VAT = {n: i for i, n in enumerate(VEC)}
W0 = [("wq", C), ("wk", C), ("wv", C), ("pw", C), ("pwg0", C), ("pwg1", C), ("g1w", C // 4), ("g2w", C)]
W2 = [("wq2", C), ("wk2", C), ("wv2", C)]
W3 = [("wq3", C), ("wk3", C), ("wv3", C), ("wo3", C), ("lkg", C), ("lkb", C), ("aw1", 2048), ("aw2", 512),
      ("wup", 1024), ("wdn", 1024)]


def places(ws):
    at, n = {}, 0
    for name, w in ws:
        at[name] = (n, w)
        n += w
    return at, n



def build(nc, io):
    W0A, W0N = places(W0)
    W2A, W2N = places(W2)
    W3A, W3N = places(W3)
    ctx = ExitStack()
    with ctx:
        start = {}

        def sb(name, shape, dt=F32):
            start[name] = (nc.sbuf_base + 31) // 32 * 32
            return ctx.enter_context(nc.sbuf_tensor(name, shape, dt))

        def rounded(name, region, column, shape):
            return nc.alloc_sbuf_tensor_at(name, shape, F32R, offset=start[region] + 4 * column)

        sems = {}

        def sem(name):
            if name not in sems:
                sems[name] = ctx.enter_context(nc.semaphore(name))
            return sems[name]

        ps = ctx.enter_context(nc.psum_tensor("ps", [128, 8, TILE], F32))

        cst = sb("cst", [C, CONSTS.shape[1]])
        vec = sb("vec", [C, len(VEC)])
        w0 = sb("w0", [C, W0N])
        w2 = sb("w2", [C, W2N])
        kd = sb("kd", [C, 9, C])
        identb = sb("identb", [C, C], BF16)
        identr = sb("identr", [C, C], F32R)
        zerob = sb("zerob", [C, TILE], BF16)
        ones = sb("ones", [C, C])
        small = sb("small", [C, 16])
        eps, pbe, gb2, sv, bvec = (small[:, i:i + 1] for i in (0, 1, 2, 3, 4))
        bvecs = small[:, 4:6]
        xt = sb("xt", [C, T])
        pad = sb("pad", [C, IMG, H + 2, W + 2])
        x2 = sb("x2", [C, T])
        vaug = sb("vaug", [C, IMG * NCH, NH, 32])
        mx = sb("mx", [C, 32])
        mcat = sb("mcat", [C, 64], BF16)
        mt = sb("mt", [64, C], BF16)
        r_tab = sb("r_tab", [C, 9088])
        r_stk = sb("r_stk", [C, 12288])
        r_prt = sb("r_prt", [C, 4480])
        r_p = sb("r_p", [C, 6144])
        r_o = sb("r_o", [C, 4096])

        def cc(name):
            o, n = CAT[name]
            return cst[:, o:o + n]

        def vv(name, n=1):
            return vec[:, VAT[name]:VAT[name] + n]

        def ww(t, at, name):
            o, n = at[name]
            return t[:, o:o + n]

        ident, cen, avg, dens = cc("ident"), cc("cen"), cc("avg"), cc("den")
        TAB1 = NH * KWIN * W
        TW = 2 * QWIN_R * QWIN_C
        HT = NH // 2 * TW
        tab1 = r_tab[:, 0:TAB1].rearrange("p (n f v c) -> p n f (v c)", n=NH, f=2, c=CCOLS)
        tab2f = [rounded("tab2hi", "r_tab", TAB1, [C, NH * TW])[:, :], rounded("tab2lo", "r_prt", 0, [C, NH * TW])[:, :]]
        tab2 = [a.rearrange("p (n f u c) -> p n f (u c)", n=NH, f=2, c=QWIN_C) for a in tab2f]
        u_raw = r_p[:, 0:NH * TW]
        stk = r_stk[:, :].bitcast(BF16).rearrange("p (s a h n) -> p s a h n", s=3, a=2, h=HG)
        parts = r_prt[:, 0:3072].bitcast(BF16).rearrange("p (b a r n) -> p b a r n", b=2, a=2, r=3)
        rem = r_prt[:, 3072:4096].rearrange("p (b n) -> p b n", b=2)
        NP0 = QWIN_R * QWIN_C
        pa0 = r_p[:, 0:8 * NP0].rearrange("p (s h n) -> p s h n", s=4, h=2)
        junk = r_p[:, NH * TW:NH * TW + 2 * KWIN * W].rearrange("p (s n) -> p s n", s=2)
        pa2 = r_p[:, :].rearrange("p (s n) -> p s n", s=12)
        oraw = r_o[:, :].rearrange("p (b n) -> p b n", b=NB)
        rec = r_stk[:, 0:4096].rearrange("p (i n) -> p i n", n=TILE)
        og = r_stk[:, 4096:8192].rearrange("p (i n) -> p i n", n=TILE)
        gate = r_tab[:, TAB1 + NH * TW:TAB1 + NH * TW + T].rearrange("p (t n) -> p t n", n=TILE)
        ysum = r_stk[:, 10240:12288].rearrange("p (t n) -> p t n", n=TILE)
        g1s = r_o[0:C // 4, 0:T].rearrange("p (t n) -> p t n", n=TILE)
        sqs = r_p[:, 0:2048].rearrange("p (t n) -> p t n", n=TILE)
        rss = r_p[:, 2048:4096].rearrange("p (t n) -> p t n", n=TILE)
        t1s = r_p[:, 4096:6144].rearrange("p (t n) -> p t n", n=TILE)
        tmp = r_prt[:, 0:2048].rearrange("p (t n) -> p t n", n=TILE)
        x3n = r_o[:, 0:2048]
        x4 = r_o[:, 2048:4096]
        x3t = r_stk[:, 0:2048]
        a1 = r_stk[:, 2048:4096]
        zt = r_stk[:, 4096:6144]
        sf = [r_stk[:, 6144 + i * NF:6144 + (i + 1) * NF] for i in range(2)]
        yf = [r_stk[:, 8320 + i * NF:8320 + (i + 1) * NF] for i in range(2)]
        yt = r_stk[:, 0:2304].rearrange("p (o n) -> p o n", o=2)
        zf = r_stk[:, 2304:4352]
        zt2 = r_stk[:, 4352:6400]
        h5 = r_stk[:, 6400:8448]
        FT = 384
        ftiles = [(o, min(FT, NF - o)) for o in range(0, NF, FT)]
        hid = r_p[:, :].rearrange("p (b m n) -> p b m n", b=2, m=8)
        tsh = r_prt[:, 0:2 * FT].rearrange("p (b n) -> p b n", b=2)
        csh = r_prt[:, 2 * FT:4 * FT].rearrange("p (b n) -> p b n", b=2)
        cw = r_prt[:, 0:256]
        cwb = r_prt[:, 256:512]
        cbs = r_prt[:, 512:768]
        kvt = r_prt[:, 768:768 + 2 * C].rearrange("p (i n) -> p i n", i=IMG)
        kws = r_prt[:, 1024:1024 + 2 * C].rearrange("p (i n) -> p i n", i=IMG)
        ms = r_prt[:, 1280:1280 + 2 * C].rearrange("p (i n) -> p i n", i=IMG)
        kvx = r_prt[:, 1536:1536 + 6 * C].rearrange("p (i n) -> p i n", n=C)
        rsk = r_prt[:, 2304:2560]
        kc = r_p[:, 0:4096].rearrange("p (t n) -> p t n", t=16)
        ksq = r_stk[:, 0:4096]
        x7 = r_o[:, 0:2048]
        HRING, GRING, LAG = 8, 4, 4
        whi, wlo = rounded("whi", "vaug", 0, [C, 2048]), rounded("wlo", "vaug", 2048, [C, 2048])
        x7hi, x7lo = rounded("x7hi", "r_o", 2048, [C, T]), rounded("x7lo", "r_prt", 0, [C, T])
        hidhi, hidlo = (rounded(n, "r_stk", HRING * TILE * i, [C, HRING, TILE]) for i, n in enumerate(("hidhi", "hidlo")))
        hidraw = r_stk[:, 8192:8192 + GRING * TILE].rearrange("p (s n) -> p s n", n=TILE)
        aw1 = ww(r_tab, W3A, "aw1").rearrange("p (f t m n) -> p f t m n", f=2, t=2, m=4)
        aw2 = ww(r_tab, W3A, "aw2").rearrange("p (f t m n) -> p f t m n", f=2, t=2, m=4)

        scr = nc.dram_tensor("scr", (2, 2, 3, IMG, C, TOK), BF16, kind="Internal").ap()
        block = ctx.enter_context(nc.Block())

        def tile(t):
            return slice(t * TILE, (t + 1) * TILE)

        def mm(out, lhsT, rhs, start=True, stop=True, **kw):
            return nc.tensor.matmul(out, lhsT, rhs, start=start, stop=stop, **kw)

        seg = {}
        for rb in range(H // CROWS):
            a, b = query_rows(rb)
            seg[rb] = [(s, max(a, 16 * s), min(b, 16 * s + 16)) for s in range(2) if max(a, 16 * s) < min(b, 16 * s + 16)]
        U0 = TOK // 128 * HG + 1
        U2 = TILE // 128 * HG + 1
        LEAD0, LEAD2 = 6, 5
        NB2 = 2 * NB

        @block.sync
        def _(sp):
            sp.dma_start(w0[:, :], io["w0"]).then_inc(sem("in_w0"), 16)
            sp.dma_start(vec[:, :], io["vec"]).then_inc(sem("in_vec"), 16)
            for t in range(2):
                sp.dma_start(xt[:, tile(t)], io["xT"][:, tile(t)]).then_inc(sem(f"in_x{t}"), 16)
            sp.dma_start(x2[:, 0:TOK], io["xK"][:, 0:TOK]).then_inc(sem("in_xK0"), 16)
            for t in range(2, 4):
                sp.dma_start(xt[:, tile(t)], io["xT"][:, tile(t)]).then_inc(sem(f"in_x{t}"), 16)
            sp.dma_start(x2[:, TOK:T], io["xK"][:, TOK:T]).then_inc(sem("in_xK1"), 16)
            sp.dma_start(stk[96:96 + RMOD + 2, :, 1].rearrange("p s h n -> p s (h n)"),
                         io["mrows"][0:RMOD + 2].rearrange("p h n -> p (h n)").unsqueeze(1).to_broadcast([RMOD + 2, 3, HG * TOK]))\
                .then_inc(sem("in_mask"), 16)
            sp.dma_start(stk[96:96 + RMOD, :, 0].rearrange("p s h n -> p s (h n)"),
                         io["mrows"][RMOD + 2:2 * RMOD + 2].rearrange("p h n -> p (h n)").unsqueeze(1).to_broadcast([RMOD, 3, HG * TOK]))\
                .then_inc(sem("in_mask"), 16)

            def load_stack(layer, b):
                img, g, s = b // NG, b % NG, b % 3
                for lo, hi in PART_RUNS:
                    n = hi - lo
                    for a in range(2):
                        rows = slice(HD * g * HG, HD * (g + 1) * HG)
                        src = scr[layer // 2, a, :, img, rows, :].rearrange("r (j h) n -> r j (h n)", h=HG)
                        first = (Q_PARTS, K_PARTS)[a][lo]
                        src = src[first:first + n] if a else src[first:first + 1].to_broadcast([n, HD, HG * TOK])
                        sp.dma_start(stk[HD * lo:HD * hi, s, a].rearrange("p h n -> p (h n)"), src).then_inc(sem(f"stk{layer}_{b}"), 16)

            def store_parts(layer, t):
                for a in range(2):
                    sp.wait_ge(sem("split"), 2 * NT * (layer // 2) + 2 * t + a + 1)
                    sp.dma_start(scr[layer // 2, a, :, t // 2].rearrange("r p n -> p r n")[:, :, tile(t % 2)],
                                 parts[:, t % 2, a]).then_inc(sem(f"parts_out{layer}_{t}"), 16)

            def image_stored(layer, img):
                sp.wait_ge(sem(f"parts_out{layer}_{2 * img}"), 32)
                sp.wait_ge(sem(f"parts_out{layer}_{2 * img + 1}"), 32)

            store_parts(0, 0)
            store_parts(0, 1)
            sp.dma_start(r_tab[:, 0:TAB1], io["tab1"]).then_inc(sem("in_tab1"), 16)
            image_stored(0, 0)
            load_stack(0, 0)
            store_parts(0, 2)
            sp.dma_start(cst[:, :], io["cst"]).then_inc(sem("in_cst"), 16)
            store_parts(0, 3)
            load_stack(0, 1)
            sp.dma_start(u_raw, io["tab2"]).then_inc(sem("in_u"), 16)
            image_stored(0, 1)
            load_stack(0, 2)
            sp.dma_start(w2[:, :], io["w2"]).then_inc(sem("in_w2"), 16)
            for b in range(NB):
                sp.wait_ge(sem("p1_taken0"), U0 * (b + 1))
                for part in range(2):
                    sp.dma_start(stk[K1_L0 + part:K1_L0 + part + 1, b % 3, 0].rearrange("p h (a n) -> p (h a) n", n=128),
                                 mt[32 * part:32 * part + 32, :]).then_inc(sem("mrow0"), 16)
                if b == 1:
                    sp.wait_ge(sem("pv0"), NCH)
                    load_stack(0, 3)
            sp.wait_ge(sem("pv0"), NCH * NB)
            sp.dma_start(r_tab[:, 0:W3N], io["w3"]).then_inc(sem("in_w3"), 16)

            sp.wait_ge(sem("og"), 8)
            sp.wait_ge(sem("lnout"), NT)
            sp.dma_start(stk[96:98, :, 1].rearrange("p s h n -> p s (h n)"),
                         io["mrows"][RMOD:RMOD + 2].rearrange("p h n -> p (h n)").unsqueeze(1).to_broadcast([2, 3, HG * TOK]))\
                .then_inc(sem("in_ones"), 16)
            for t in range(NT):
                store_parts(2, t)
                if t % 2:
                    image_stored(2, t // 2)
                    load_stack(2, 2 * (t // 2))
                    if t == 1:
                        load_stack(2, 1)
            for n in range(NB2):
                b, qh = n // 2, n % 2
                sp.wait_ge(sem("p1_taken2"), U2 * (n + 1))
                for h in range(HG):
                    sp.dma_start(stk[K1_L2:K1_L2 + 2, b % 3, 0, h, tile(qh)], mt[8 * h:8 * h + 8, :]).then_inc(sem("mrow2"), 16)
                if n == 2:
                    sp.wait_ge(sem("pv2"), 2 * NCH)
                    load_stack(2, 3)
            for t in range(NT):
                sp.wait_ge(sem("y_ready"), t + 1)
                sp.dma_start(io["out"][:, tile(t)], x2[:, tile(t)]).then_inc(sem("out"), 16)
            sp.wait_ge(sem("out"), 16 * NT)

        @block.tensor
        def _(pe):
            def project(layer, src, keys, w, at, suffix):
                for t in range(NT):
                    if layer == 0:
                        pe.wait_ge(sem(f"in_x{t}"), 16)
                        pe.wait_ge(sem("wq_scaled"), 2)
                    for a, name in enumerate(("wq", "wk")):
                        if t >= 2:
                            pe.wait_ge(sem("rem"), 2 * NT * (layer // 2) + 2 * (t - 2) + a + 1)
                        if a and layer == 0 and t % 2 == 0:
                            pe.wait_ge(sem(f"in_xK{t // 2}"), 16)
                        mm(ps[:, 4 + 2 * (t % 2) + a, :], ww(w, at, name + suffix), (src, keys)[a][:, tile(t)]).then_inc(sem("qk"), 1)
                for j in range(4):
                    for i in range(4):
                        c = 4 * j + i
                        last = mm(ps[:, j, 128 * i:128 * i + 128], keys[:, 128 * c:128 * c + 128], ww(w, at, "wv" + suffix))
                    last.then_inc(sem("v"), 1)

            def heads_back(layer, wa, wb):
                for i in range(2 * NT):
                    t, g = i // 2, i % 2
                    mm(ps[:, i, :], dens, oraw[:, 2 * (t // 2) + g, tile(t % 2)]).then_inc(sem("den"), 1)
                for t in range(NT):
                    pe.wait_ge(sem("og"), 2 * NT * (layer - 3) + 2 * t + 2)
                    mm(ps[:, t, :], wa, og[:, 2 * t, :], stop=False)
                    mm(ps[:, t, :], wb, og[:, 2 * t + 1, :], start=False).then_inc(sem("hb"), 1)

            def norm(k, src, ready, per=1):
                for t in range(NT):
                    pe.wait_ge(sem(ready), per * (t + 1))
                    mm(ps[:, 4 + t, :], cen, src(t)).then_inc(sem("cen"), 1)
                    if t:
                        pe.wait_ge(sem("sq"), NT * k + t)
                        mm(ps[:, t - 1, :], avg, sqs[:, t - 1, :]).then_inc(sem("var"), 1)
                pe.wait_ge(sem("sq"), NT * k + NT)
                mm(ps[:, NT - 1, :], avg, sqs[:, NT - 1, :]).then_inc(sem("var"), 1)

            pe.wait_ge(sem("in_w0"), 16)
            project(0, xt, x2, w0, W0A, "")
            pe.wait_ge(sem("in_vec"), 16)
            pe.wait_ge(sem("rem"), 2 * NT)
            for t in range(NT):
                mm(ps[0:C // 4, 4 + t, :], ww(w0, W0A, "g1w"), xt[:, tile(t)]).then_inc(sem("g1"), 1)

            def l0_first(i):
                b, r = i // U0, i % U0
                bank = i % 2
                if i > 1:
                    pe.wait_ge(sem("p1_taken0"), i - 1)
                if r == 0:
                    pe.wait_ge(sem(f"stk0_{b}"), 6 * 16)
                    pe.wait_ge(sem("in_mask"), 32)
                if r < U0 - 1:
                    qb, h = r // HG, r % HG
                    k0, k1 = key_rows(qb)
                    mm(ps[:, bank, 0:(k1 - k0) * W].rearrange("p (f n) -> p f n", f=2), stk[0:K1_L0, b % 3, 0, h, 128 * qb:128 * qb + 128],
                       stk[0:K1_L0, b % 3, 1, h].rearrange("p (f n) -> p f n", f=2)[:, :, k0 * CCOLS:k1 * CCOLS]).then_inc(sem("s1_0"), 1)
                else:
                    pe.wait_ge(sem("mcat0"), b + 1)
                    pe.wait_ge(sem("identb"), 1)
                    nc.tensor.transpose(ps[0:64, bank, 0:64].bitcast(BF16), mcat[:, :], identb[:, :]).then_inc(sem("s1_0"), 1)

            def l0_second(u, between):
                b, c, pair = u // 16, u // 2 % 8, u % 2
                rb, half = c % 4, c // 4
                r0, r1 = query_rows(rb)
                c0, c1 = query_cols(half)
                n = (r1 - r0) * QWIN_C
                bank = 2 + 2 * (u % 2)
                if u % 16 == 0:
                    pe.wait_ge(sem("mrow0"), 32 * (b + 1))
                if u > 1:
                    pe.wait_ge(sem("exp0"), u - 1)
                u0 = (r0 - CROWS * rb + K // 2) * QWIN_C
                for hh in range(2):
                    h = 2 * pair + hh
                    qv = stk[0:K2_L0, b % 3, 0, h].rearrange("p (r c) -> p r c", c=W)
                    out = ps[:, bank + hh, 0:n]
                    mm(out.rearrange("p (r c) -> p r c", c=QWIN_C), stk[0:K2_L0, b % 3, 1, h, 128 * c:128 * c + 128],
                       qv[:, r0:r1, c0:c1], stop=False)
                    mm(out, identr[:, :], tab2[0][:, HG * (b % NG) + h, half, u0:u0 + n], start=False, stop=False)
                    last = mm(out, identr[:, :], tab2[1][:, HG * (b % NG) + h, half, u0:u0 + n], start=False)
                    if hh == 0:
                        between()
                last.then_inc(sem("s2_0"), 1)

            def l0_values(cc_):
                b, c = cc_ // NCH, cc_ % NCH
                rb, half = c % 4, c // 4
                r0, _ = query_rows(rb)
                c0, c1 = query_cols(half)
                if c == 0:
                    if b:
                        pe.wait_ge(sem("accev0"), b)
                    for s in range(2):
                        mm(ps[:, 6 + s, :], zerob[:, 0:C], zerob[:, :])
                pe.wait_ge(sem("exp0"), 2 * cc_ + 2)
                for s, a, z in seg[rb]:
                    for h in range(HG):
                        out = ps[32 * h:32 * h + 32, 6 + s, :].rearrange("p (r c) -> p r c", c=W)[:, a - 16 * s:z - 16 * s, c0:c1]
                        last = mm(out, vaug[:, b // NG * NCH + c, HG * (b % NG) + h, :],
                                  pa0[:, (2 * cc_ + h // 2) % 4, h % 2, (a - r0) * QWIN_C:(z - r0) * QWIN_C]
                                  .rearrange("p (r c) -> p r c", c=QWIN_C),
                                  start=False, stop=True, skip_group_check=True)
                last.then_inc(sem("pv0"), 1)

            pe.wait_ge(sem("vev0"), 4)
            mm(ps[:, 3, 0:1], ww(w0, W0A, "pw"), vv("bv0")).then_inc(sem("pbe_mm"), 1)
            issued = 0

            def first_up_to(limit):
                nonlocal issued
                while issued < min(limit, NB * U0):
                    l0_first(issued)
                    issued += 1

            for s in range(NB * NCH):
                base = U0 + LEAD0 + s * U0 // NCH
                if s == 0:
                    first_up_to(U0)
                    for t in range(NT):
                        pe.wait_ge(sem("g1r"), t + 1)
                        mm(ps[:, 4 + t, :], ww(w0, W0A, "g2w")[0:C // 4, :], g1s[:, t, :]).then_inc(sem("g2"), 1)
                    pe.wait_ge(sem("sig"), NT)
                    pe.wait_ge(sem("tab2_ready"), 2)
                    pe.wait_ge(sem("identr"), 1)
                    pe.wait_ge(sem("pbe_ready"), 1)
                    pe.wait_ge(sem("zeros"), 3)
                first_up_to(base + 1)
                l0_second(2 * s, lambda: first_up_to(base + 2))
                first_up_to(base + 3)
                l0_second(2 * s + 1, lambda: first_up_to(base + 4))
                if s:
                    l0_values(s - 1)
            l0_values(NB * NCH - 1)
            pe.wait_ge(sem("accev0"), NB)

            heads_back(3, ww(w0, W0A, "pwg0"), ww(w0, W0A, "pwg1"))
            norm(0, lambda t: ysum[:, t, :], "y3")

            pe.wait_ge(sem("kd"), 9)
            for t in range(NT):
                img, r0 = t // 2, 16 * (t % 2)
                pe.wait_ge(sem("lnout"), 2 * (img + 1))
                for i in PE_TAPS:
                    dy, dx = i // 3, i % 3
                    last = mm(ps[:, t, :], kd[:, i, :], pad[:, img, r0 + dy:r0 + dy + 16, dx:dx + W],
                              start=i == PE_TAPS[0], stop=i == PE_TAPS[-1])
                last.then_inc(sem("conv"), 1)

            pe.wait_ge(sem("in_w2"), 16)
            pe.wait_ge(sem("x2_ready"), NT)
            pe.wait_ge(sem("lnout"), NT)
            project(2, x2, x2, w2, W2A, "2")

            def l2_first(i):
                n, r = i // U2, i % U2
                b, qh = n // 2, n % 2
                bank = 2 * (i % 2)
                if i > 1:
                    pe.wait_ge(sem("p1_taken2"), i - 1)
                if n % 2 == 0 and r == 0:
                    pe.wait_ge(sem(f"stk2_{b}"), 6 * 16)
                if r < U2 - 1:
                    qt, h = r // HG, r % HG
                    q0 = qh * TILE + 128 * qt
                    for kh in range(2):
                        last = mm(ps[:, bank + kh, :], stk[0:K1_L2, b % 3, 0, h, q0:q0 + 128],
                                  stk[0:K1_L2, b % 3, 1, h, tile(kh)])
                    last.then_inc(sem("s1_2"), 1)
                else:
                    pe.wait_ge(sem("mcat2"), n + 1)
                    nc.tensor.transpose(ps[0:32, bank, 0:64].bitcast(BF16), mcat[:, 0:32], identb[:, :]).then_inc(sem("s1_2"), 1)

            def l2_second(u):
                n, c, h = u // 32, u // 4 % 8, u % 4
                b, qh = n // 2, n % 2
                if u % 32 == 0:
                    pe.wait_ge(sem("mrow2"), 64 * (n + 1))
                    pe.wait_ge(sem("in_ones"), 16)
                if u > 2:
                    pe.wait_ge(sem("exp2"), u - 2)
                mm(ps[:, 4 + u % 3, :], stk[0:K2_L2, b % 3, 1, h, 128 * c:128 * c + 128],
                   stk[0:K2_L2, b % 3, 0, h, tile(qh)]).then_inc(sem("s2_2"), 1)

            def l2_values(cc_):
                n, c = cc_ // NCH, cc_ % NCH
                b = n // 2
                if c == 0:
                    if n:
                        pe.wait_ge(sem("accev2"), n)
                pe.wait_ge(sem("exp2"), 4 * cc_ + 4)
                for h in range(HG):
                    last = mm(ps[32 * h:32 * h + 32, 7, :], vaug[:, b // NG * NCH + c, HG * (b % NG) + h, :],
                              pa2[:, (4 * cc_ + h) % 12, :], start=c == 0, stop=c == NCH - 1)
                last.then_inc(sem("pv2"), 1)

            pe.wait_ge(sem("vev2"), 16)
            pe.wait_ge(sem("split"), 2 * NT + 2 * NT)
            issued = 0
            for s in range(NB2 * NCH):
                upto = min(U2 + LEAD2 + (s + 1) * U2 // NCH, NB2 * U2)
                if s == 0:
                    while issued < U2:
                        l2_first(issued)
                        issued += 1
                for h in range(HG):
                    if h % 2 == 0 and issued < upto:
                        l2_first(issued)
                        issued += 1
                    while h == 3 and issued < upto:
                        l2_first(issued)
                        issued += 1
                    l2_second(4 * s + h)
                if s:
                    l2_values(s - 1)
            l2_values(NB2 * NCH - 1)
            pe.wait_ge(sem("accev2"), NB2)

            heads_back(4, cc("sel0"), cc("sel1"))
            norm(1, lambda t: xt[:, tile(t)], "x3_ready")

            for t in range(NT):
                pe.wait_ge(sem("lnout"), NT + t + 1)
                for i in range(4):
                    last = nc.tensor.transpose(ps[:, t, 128 * i:128 * i + 128], x3n[:, t * TILE + 128 * i:t * TILE + 128 * i + 128], ident)
                last.then_inc(sem("fa"), 1)
            for t in range(NT):
                pe.wait_ge(sem("fa_ev"), t + 1)
                for i in range(4):
                    last = mm(ps[:, 4 + t, 128 * i:128 * i + 128], x3t[:, t * TILE + 128 * i:t * TILE + 128 * i + 128], cc("f1"))
                last.then_inc(sem("fb"), 1)
            for q in range(4):
                pe.wait_ge(sem("fb_ev"), 2 * (q // 2) + 2)
                for i in range(4):
                    last = nc.tensor.transpose(ps[:, q, 128 * i:128 * i + 128], a1[:, q * TILE + 128 * i:q * TILE + 128 * i + 128], ident)
                last.then_inc(sem("fc"), 1)
            pe.wait_ge(sem("fb_ev"), 4)
            d0 = cc("d0").rearrange("p (o n) -> p o n", o=2)
            dg = cc("dg").rearrange("p (o n) -> p o n", o=2)
            for m in range(4):
                img, half = m // 2, m % 2
                pe.wait_ge(sem("fc_ev"), 2 * img + 2)
                bank = (5, 6, 7, 0)[m]
                if m == 3:
                    pe.wait_ge(sem("fc_ev"), 4)
                for ro in range(2):
                    o = slice(64 * ro, 64 * ro + 64)
                    for j in range(8):
                        wgt = zt[:, (8 * img + j) * C + 64 * half:(8 * img + j) * C + 64 * half + 64]
                        if j == 0:
                            last = mm(ps[o, 4, 96 * m:96 * m + 96], wgt, d0[:, ro, :])
                        else:
                            last = mm(ps[o, bank, 64 * (j - 1):64 * j], wgt, dg[:, ro, :])
                last.then_inc(sem("fd"), 1)

            pe.wait_ge(sem("in_w3"), 16)
            pe.wait_ge(sem("aw_signed"), 2)
            pe.wait_ge(sem("fdA"), 4)
            pe.wait_ge(sem("fdD"), 4)

            def af_up(q):
                half, (o, n) = q // 3, ftiles[q % 3]
                for m in range(8):
                    cnt = 8 * q + m
                    if cnt >= 6:
                        pe.wait_ge(sem("ahA" if cnt % 2 == 0 else "ahD"), (cnt - 6) // 2 + 1)
                    mm(ps[:, cnt % 6, 0:n], aw1[:, half, m // 4, m % 4, :], sf[half][:, o:o + n])\
                        .then_inc(sem("au"), 1)

            def af_down(q):
                half, (o, n) = q // 3, ftiles[q % 3]
                pe.wait_ge(sem("ahA"), 4 * (q + 1))
                pe.wait_ge(sem("ahD"), 4 * (q + 1))
                if q > 1:
                    pe.wait_ge(sem("tsh"), q - 1)
                for t in range(2):
                    for p in range(4):
                        last = mm(ps[32 * p:32 * p + 32, 6 + q % 2, 0:n], aw2[:, half, t, p, :],
                                  hid[:, q % 2, 4 * t + p, 0:n], start=t == 0, stop=t == 1)
                last.then_inc(sem("ad"), 1)

            for q in range(6):
                af_up(q)
                if q:
                    af_down(q - 1)
            af_down(5)

            pe.wait_ge(sem("ahA"), 24)
            pe.wait_ge(sem("ahD"), 24)
            for i in range(18):
                kp, half = i // 2, i % 2
                pe.wait_ge(sem("yf"), 6 if half else 3)
                o = min(128 * kp, NF - 128)
                last = nc.tensor.transpose(ps[:, i // 4, 128 * (i % 4):128 * (i % 4) + 128], yf[half][:, o:o + 128], ident)
                if i % 4 == 3 or i == 17:
                    last.then_inc(sem("ba"), 1)
            for kp in range(9):
                pe.wait_ge(sem("ba_ev"), 2 * (kp // 2 + 1))
                if kp == 0:
                    pe.wait_ge(sem("tsh"), 6)
                if kp > 2:
                    pe.wait_ge(sem("bb_ev"), kp - 2)
                bank = 5 + kp % 3
                rows = slice(64, 128) if kp == 8 else slice(0, 128)
                for half in range(2):
                    for part in range(2):
                        e = cc(f"e0{part}" if kp == 0 else f"eg{part}").rearrange("p (i f h) -> p i f h", i=IMG, h=H)
                        if kp == 8:
                            e = e[:, :, 2:4, :]
                        n = 128 if kp in (0, 8) else 256
                        last = mm(ps[64 * half:64 * half + 64, bank, 0:n], yt[rows, part, 64 * (2 * kp + half):64 * (2 * kp + half) + 64], e[rows], start=part == 0, stop=part == 1)
                last.then_inc(sem("bb"), 1)
            for q in range(4):
                pe.wait_ge(sem("bb_ev"), 9)
                pe.wait_ge(sem("ba_ev"), 10)
                for i in range(4):
                    last = nc.tensor.transpose(ps[:, q, 128 * i:128 * i + 128], zf[:, q * TILE + 128 * i:q * TILE + 128 * i + 128], ident)
                last.then_inc(sem("bc"), 1)
            for t in range(NT):
                pe.wait_ge(sem("bc_ev"), t + 1)
                for i in range(4):
                    last = mm(ps[:, 4 + t, 128 * i:128 * i + 128], zt2[:, t * TILE + 128 * i:t * TILE + 128 * i + 128], cc("g"))
                last.then_inc(sem("bd"), 1)
            norm(2, lambda t: x4[:, tile(t)], "x4_ready")

            pe.wait_ge(sem("lnout"), 2 * NT + NT)
            for a, name in enumerate(("wk3", "wv3")):
                mm(ps[:, 0, 128 * a:128 * a + 128], ww(r_tab, W3A, name), cc("cenhead"))
            pe.wait_ge(sem("cbs"), 2)
            mm(ps[:, 1, 0:256], ones[:, :], cbs).then_inc(sem("gw"), 1)
            for j in range(8):
                if j == 0:
                    pe.wait_ge(sem("gw_ev"), 2)
                for i in range(2):
                    tk = 2 * j + i
                    last = mm(ps[:, j, 256 * i:256 * i + 256], h5[:, 128 * tk:128 * tk + 128], cw)
                last.then_inc(sem("gk"), 1)
            for img in range(IMG):
                for i in range(8):
                    pe.wait_ge(sem("kn"), 4 * img + i // 2 + 1)
                    tk = 8 * img + i
                    if i == 0:
                        pe.wait_ge(sem("kc"), 8)
                    st, sp_ = i == 0, i == 7
                    mm(ps[:, 3 * img, 0:128], kc[:, tk, 128:256], kc[:, tk, 0:128], start=st, stop=sp_)
                    mm(ps[:, 3 * img + 1, 0:1], kc[:, tk, 128:256], ones[:, 0:1], start=st, stop=sp_)
                    last = mm(ps[:, 3 * img + 2, 0:128], ones[:, :], kc[:, tk, 0:128], start=st, stop=sp_)
                last.then_inc(sem("kv"), 1)
            for img in range(IMG):
                pe.wait_ge(sem("kvt"), img + 1)
                mm(ps[:, 6, 128 * img:128 * img + 128], kvt[:, img, :], ww(r_tab, W3A, "wo3")).then_inc(sem("kw"), 1)
                pe.wait_ge(sem("kw_ev"), img + 1)
                mm(ps[:, 7, 128 * img:128 * img + 128], ww(r_tab, W3A, "wq3"), kws[:, img, :])
                mm(ps[:, 7, 256 + img:257 + img], kws[:, img, :], vv("bq3")).then_inc(sem("km"), 1)
                pe.wait_ge(sem("km_ev"), 2 * img + 2)
            for t in range(NT):
                if t == 0:
                    pe.wait_ge(sem("kvt"), IMG)
                mm(ps[:, t, :], ms[:, t // 2, :], h5[:, tile(t)]).then_inc(sem("att"), 1)
            norm(3, lambda t: xt[:, tile(t)], "x6_ready")

            def three(out, w, x, start, stop):
                mm(out, w[0], x[0], start=start, stop=False)
                mm(out, w[0], x[1], start=False, stop=False)
                return mm(out, w[1], x[0], start=False, stop=stop)

            def up(cnt):
                t, m = cnt // FF, cnt % FF
                if cnt > 5:
                    pe.wait_ge(sem("gelu"), cnt - 5)
                s_ = slice(128 * m, 128 * m + 128)
                three(ps[:, cnt % 6, :], (whi[:, s_], wlo[:, s_]), (x7hi[:, tile(t)], x7lo[:, tile(t)]), True, True)\
                    .then_inc(sem("up"), 1)

            def down(cnt):
                t, m = cnt // FF, cnt % FF
                pe.wait_ge(sem("hidlo"), cnt + 1)
                if t > 1 and m == 0:
                    pe.wait_ge(sem("y_ready"), t - 1)
                s_ = slice(1024 + 128 * m, 1024 + 128 * m + 128)
                three(ps[:, 6 + t % 2, :], (whi[:, s_], wlo[:, s_]), (hidhi[:, cnt % HRING, :], hidlo[:, cnt % HRING, :]), m == 0, m == FF - 1)\
                    .then_inc(sem("down"), 1)

            pe.wait_ge(sem("wsplit"), 2)
            for cnt in range(FF * NT + LAG):
                if cnt < FF * NT:
                    if cnt % FF == 0:
                        pe.wait_ge(sem("x7lo"), cnt // FF + 1)
                    up(cnt)
                if cnt >= LAG:
                    down(cnt - LAG)

        @block.scalar
        def _(act):
            def split(layer, bq, bk):
                for i in range(2 * NT + 1):
                    if i < 2 * NT:
                        t, a = i // 2, i % 2
                        act.wait_ge(sem("qk"), 2 * NT * (layer // 2) + i + 1)
                        if t >= 2:
                            act.wait_ge(sem(f"parts_out{layer}_{t - 2}"), 32)
                        nc.scalar.activation(parts[:, t % 2, a, 0, :], ps[:, 4 + 2 * (t % 2) + a, :], ACT.Identity,
                                             bias=vv((bq, bk)[a])).then_inc(sem("hi"), 1)
                    if i:
                        t, a = (i - 1) // 2, (i - 1) % 2
                        act.wait_ge(sem("rem"), 2 * NT * (layer // 2) + i)
                        nc.scalar.activation(parts[:, t % 2, a, 1, :], rem[:, (i - 1) % 2, :], ACT.Copy).then_inc(sem("mid"), 1)

            def normalise(layer):
                for i in range(2 * NT + 1):
                    if i < 2 * NT:
                        act.wait_ge(sem("den"), 2 * NT * (layer - 3) + i + 1)
                        nc.scalar.activation(rec[:, i, :], ps[:, i, :], ACT.Ln).then_inc(sem("lnd"), 1)
                    if i:
                        act.wait_ge(sem("lnd"), 2 * NT * (layer - 3) + i)
                        nc.scalar.activation(rec[:, i - 1, :], rec[:, i - 1, :], ACT.Exp, scale=-1.0).then_inc(sem("rec"), 1)

            def norm(k):
                for t in range(NT + 1):
                    if t < NT:
                        act.wait_ge(sem("cen"), NT * k + t + 1)
                        nc.scalar.activation(sqs[:, t, :], ps[:, 4 + t, :], ACT.Square).then_inc(sem("sq"), 1)
                    if t:
                        act.wait_ge(sem("var"), NT * k + t)
                        nc.scalar.activation(rss[:, t - 1, :], ps[:, t - 1, :], ACT.Ln, bias=eps).then_inc(sem("lv"), 1)
                        act.wait_ge(sem("lv"), NT * k + t)
                        nc.scalar.activation(rss[:, t - 1, :], rss[:, t - 1, :], ACT.Exp, scale=-0.5).then_inc(sem("rs"), 1)

            logexp = "natural_log_exp_and_others"
            nc.scalar.preload_act_table_set(logexp)
            act.wait_ge(sem("in_vec"), 16)
            act.wait_ge(sem("wq_scaled"), 2)
            split(0, "bq0", "bk0")
            act.wait_ge(sem("vaug0"), 2)
            for j in range(4):
                act.wait_ge(sem("v"), j + 1)
                nc.scalar.activation(vaug[:, 4 * j:4 * j + 4, :, 0:HD],
                                     ps[:, j, :].rearrange("p (c h d) -> p c h d", c=4, h=NH), ACT.Copy).then_inc(sem("vev0"), 1)
            act.wait_ge(sem("in_cst"), 16)
            nc.scalar.activation(identb[:, :], ident, ACT.Copy).then_inc(sem("identb"), 1)
            nc.scalar.activation(identr[:, :], ident, ACT.Copy).then_inc(sem("identr"), 1)
            act.wait_ge(sem("pbe_mm"), 1)
            nc.scalar.activation(pbe, ps[:, 3, 0:1], ACT.Identity, bias=vv("pb0")).then_inc(sem("pbe_ready"), 1)
            act.wait_ge(sem("in_u"), 16)
            for i in range(2):
                s = slice(HT * i, HT * (i + 1))
                nc.scalar.activation(tab2f[0][:, s], u_raw[:, s], ACT.Copy).then_inc(sem("tab_hi"), 1)
            for t in range(NT):
                act.wait_ge(sem("g1"), t + 1)
                nc.scalar.activation(g1s[:, t, :], ps[0:C // 4, 4 + t, :], ACT.Relu, bias=vv("g1b")[0:C // 4, :]).then_inc(sem("g1r"), 1)
            for t in range(NT):
                act.wait_ge(sem("g2"), t + 1)
                nc.scalar.activation(gate[:, t, :], ps[:, 4 + t, :], ACT.Sigmoid, bias=vv("g2b")).then_inc(sem("sig"), 1)
            nc.scalar.preload_act_table_set(logexp)

            def take0(b):
                act.wait_ge(sem("pv0"), NCH * (b + 1))
                nc.scalar.activation(oraw[:, b, :], ps[:, 6:8, :].rearrange("p s n -> p (s n)"), ACT.Copy).then_inc(sem("accev0"), 1)

            act.wait_ge(sem("tab2_ready"), 2)
            for u in range(16 * NB):
                r0, r1 = query_rows(u // 2 % 4)
                n = (r1 - r0) * QWIN_C
                bank = 2 + 2 * (u % 2)
                act.wait_ge(sem("s2_0"), u + 1)
                if u >= 4:
                    act.wait_ge(sem("pv0"), (u - 4) // 2 + 1)
                nc.scalar.activation(pa0[:, u % 4, :, 0:n], ps[:, bank:bank + 2, 0:n], ACT.Exp).then_inc(sem("exp0"), 1)
                if u % 16 == 1 and u > 16:
                    take0(u // 16 - 1)
            take0(NB - 1)

            normalise(3)
            norm(0)

            split(2, "bq2", "bk2")

            def take2(n):
                act.wait_ge(sem("pv2"), NCH * (n + 1))
                nc.scalar.activation(oraw[:, n // 2, tile(n % 2)], ps[:, 7, :], ACT.Copy).then_inc(sem("accev2"), 1)

            for u in range(32 * NB2):
                act.wait_ge(sem("s2_2"), u + 1)
                if u >= 12:
                    act.wait_ge(sem("pv2"), (u - 12) // 4 + 1)
                nc.scalar.activation(pa2[:, u % 12, :], ps[:, 4 + u % 3, :], ACT.Exp).then_inc(sem("exp2"), 1)
                if u % 32 == 3 and u > 32:
                    take2(u // 32 - 1)
            take2(NB2 - 1)

            normalise(4)
            for t in range(NT):
                act.wait_ge(sem("hb"), NT + t + 1)
                nc.scalar.activation(tmp[:, t, :], ps[:, t, :], ACT.Identity, bias=gb2, scale=vv("gamma")).then_inc(sem("gx"), 1)
            norm(1)

            for t in range(NT):
                act.wait_ge(sem("fa"), t + 1)
                nc.scalar.activation(x3t[:, tile(t)], ps[:, t, :], ACT.Copy).then_inc(sem("fa_ev"), 1)
            for t in range(NT):
                act.wait_ge(sem("fc"), t + 1)
                nc.scalar.activation(zt[:, tile(t)], ps[:, t, :], ACT.Copy).then_inc(sem("fc_ev"), 1)

            def take_columns(img, half, eng_copy):
                m = 2 * img + half
                s = sf[half].rearrange("p (k i h) -> p k i h", i=IMG, h=H)
                g0 = ps[:, 4, 96 * m:96 * m + 96].rearrange("p (k h) -> p k h", h=H)
                g1 = ps[:, (5, 6, 7, 0)[m], 0:448].rearrange("p (k h) -> p k h", h=H)
                eng_copy(s[:, 0:3, img, :], g0)
                eng_copy(s[:, 3:KX, img, :], g1)

            for img in range(IMG):
                act.wait_ge(sem("fd"), 4)
                take_columns(img, 0, lambda o, i: nc.scalar.activation(o, i, ACT.Copy).then_inc(sem("fdA"), 1))

            def shrink_in(q):
                half, (o, n) = q // 3, ftiles[q % 3]
                act.wait_ge(sem("ad"), q + 1)
                if q > 1:
                    act.wait_ge(sem("yf"), q - 1)
                nc.scalar.activation(tsh[:, q % 2, 0:n], ps[:, 6 + q % 2, 0:n], ACT.Identity, bias=vv(f"ab2_{half}")).then_inc(sem("tsh"), 1)

            for q in range(6):
                half, (o, n) = q // 3, ftiles[q % 3]
                for m in range(0, 8, 2):
                    act.wait_ge(sem("au"), 8 * q + m + 1)
                    if q > 1:
                        act.wait_ge(sem("ad"), q - 1)
                    nc.scalar.activation(hid[:, q % 2, m, 0:n], ps[:, (8 * q + m) % 6, 0:n], ACT.Relu,
                                         bias=vv(f"ab1_{8 * half + m}")).then_inc(sem("ahA"), 1)
                if q:
                    shrink_in(q - 1)
            shrink_in(5)
            for i in range(5):
                act.wait_ge(sem("ba"), i + 1)
                n = 256 if i == 4 else 512
                for o in range(2):
                    nc.scalar.activation(yt[:, o, 256 * i:256 * i + n // 2].rearrange("p (m c) -> p m c", c=16),
                                         ps[:, i, 0:n].rearrange("p (m o c) -> p m o c", o=2, c=16)[:, :, o, :],
                                         ACT.Copy).then_inc(sem("ba_ev"), 1)
            for t in range(NT):
                act.wait_ge(sem("bc"), t + 1)
                nc.scalar.activation(zt2[:, tile(t)], ps[:, t, :], ACT.Copy).then_inc(sem("bc_ev"), 1)
            norm(2)

            act.wait_ge(sem("gw"), 1)
            nc.scalar.activation(cw, ps[:, 0, 0:256], ACT.Copy).then_inc(sem("gw_ev"), 1)
            nc.scalar.activation(cwb, ps[:, 1, 0:256], ACT.Copy).then_inc(sem("gw_ev"), 1)
            for j in range(8):
                act.wait_ge(sem("kc"), j + 1)
                nc.scalar.activation(ksq[:, 512 * j:512 * j + 512], kc[:, 2 * j:2 * j + 2, :].rearrange("p t n -> p (t n)"), ACT.Square).then_inc(sem("ksq"), 1)
            for i in range(2):
                s = slice(128 * i, 128 * i + 128)
                act.wait_ge(sem("kvar"), 4 * (i + 1))
                nc.scalar.activation(rsk[:, s], rsk[:, s], ACT.Ln, bias=eps, scale=1.0 / DH_G).then_inc(sem("klv"), 1)
                act.wait_ge(sem("klv"), i + 1)
                nc.scalar.activation(rsk[:, s], rsk[:, s], ACT.Exp, scale=-0.5).then_inc(sem("krs"), 1)
            for img in range(IMG):
                act.wait_ge(sem("kw"), img + 1)
                nc.scalar.activation(kws[:, img, :], ps[:, 6, 128 * img:128 * img + 128], ACT.Copy).then_inc(sem("kw_ev"), 1)
                act.wait_ge(sem("km"), img + 1)
                nc.scalar.activation(ms[:, img, :], ps[:, 7, 128 * img:128 * img + 128], ACT.Copy).then_inc(sem("km_ev"), 1)
                nc.scalar.activation(bvecs[:, img:img + 1], ps[:, 7, 256 + img:257 + img], ACT.Identity, bias=vv("bo3")).then_inc(sem("km_ev"), 1)
            norm(3)
            for cnt in range(FF * NT):
                act.wait_ge(sem("up"), cnt + 1)
                if cnt >= GRING:
                    act.wait_ge(sem("hidlo"), cnt - GRING + 1)
                nc.scalar.activation(hidraw[:, cnt % GRING, :], ps[:, cnt % 6, :], ACT.Gelu, bias=vv(f"bup{cnt % FF}")).then_inc(sem("gelu"), 1)

        @block.vector
        def _(dve):
            v = nc.vector

            def split(layer, bq, bk):
                for i in range(2 * NT + 1):
                    if i < 2 * NT:
                        t, a = i // 2, i % 2
                        dve.wait_ge(sem("hi"), 2 * NT * (layer // 2) + i + 1)
                        if i > 1:
                            dve.wait_ge(sem("mid"), 2 * NT * (layer // 2) + i - 1)
                        if i > 1:
                            dve.wait_ge(sem("split"), 2 * NT * (layer // 2) + i - 1)
                        v.scalar_tensor_tensor(rem[:, i % 2, :], ps[:, 4 + 2 * (t % 2) + a, :], vv((bq, bk)[a]),
                                               parts[:, t % 2, a, 0, :], ALU.add, ALU.subtract).then_inc(sem("rem"), 1)
                    if i:
                        t, a = (i - 1) // 2, (i - 1) % 2
                        dve.wait_ge(sem("mid"), 2 * NT * (layer // 2) + i)
                        v.tensor_tensor(parts[:, t % 2, a, 2, :], rem[:, (i - 1) % 2, :], parts[:, t % 2, a, 1, :],
                                        ALU.subtract).then_inc(sem("split"), 1)

            def maxima(layer, base, nu, k, done):
                if layer == 0:
                    hi, lo, m = mcat[:, 0:k], mcat[:, k:2 * k], mx[:, 0:k]
                else:
                    both = mcat[:, 0:2 * k].rearrange("p (h r a) -> p r h a", h=HG, r=2)
                    hi, lo, m = both[:, 0], both[:, 1], mx[:, 0:k].rearrange("p (h a) -> p h a", h=HG)
                dve.wait_ge(sem(f"p1_taken{layer}"), base + nu - 1)
                v.tensor_scalar(hi, m, -1.0, None, ALU.mult).then_inc(sem(f"mhi{layer}"), 1)
                dve.wait_ge(sem(f"mhi{layer}"), done + 1)
                v.scalar_tensor_tensor(lo, m, -1.0, hi, ALU.mult, ALU.subtract)\
                    .then_inc(sem(f"mcat{layer}"), 1)
                dve.wait_ge(sem(f"s1_{layer}"), base + nu)
                if done:
                    dve.wait_ge(sem(f"mrow{layer}"), (32 if layer == 0 else 64) * done)
                bank = (base + nu - 1) % 2 * (1 if layer == 0 else 2)
                v.tensor_copy(mt[0:2 * k, :], ps[0:2 * k, bank, 0:64].bitcast(BF16)).then_inc(sem(f"p1_taken{layer}"), 1)

            def normalised(layer):
                for i in range(2 * NT):
                    dve.wait_ge(sem("rec"), 2 * NT * (layer - 3) + i + 1)
                    v.tensor_tensor(og[:, i, :], oraw[:, 2 * (i // 4) + i % 2, tile(i // 2 % 2)], rec[:, i, :], ALU.mult)\
                        .then_inc(sem("og"), 1)

            def norm(k, g, b, out, per=1):
                for t in range(NT):
                    dve.wait_ge(sem("rs"), NT * k + t + 1)
                    v.scalar_tensor_tensor(t1s[:, t, :], ps[:, 4 + t, :], vv(g), rss[:, t, :], ALU.mult, ALU.mult).then_inc(sem("ng"), 1)
                    dve.wait_ge(sem("ng"), NT * k + t + 1)
                    dst, src = out(t), t1s[:, t, :]
                    if len(dst.shape) == 3:
                        src = src.rearrange("p (r c) -> p r c", c=W)
                    v.tensor_scalar(dst, src, vv(b), None, ALU.add).then_inc(sem("lnout"), 1)

            dve.wait_ge(sem("in_w0"), 16)
            dve.wait_ge(sem("in_vec"), 16)
            scale = float(HD) ** -0.5
            v.tensor_scalar(ww(w0, W0A, "wq"), ww(w0, W0A, "wq"), scale, None, ALU.mult).then_inc(sem("wq_scaled"), 1)
            v.tensor_scalar(vv("bq0"), vv("bq0"), scale, None, ALU.mult).then_inc(sem("wq_scaled"), 1)
            v.tensor_scalar(gb2, vv("bv2"), vv("gamma"), None, ALU.mult).then_inc(sem("gb2"), 1)
            split(0, "bq0", "bk0")
            dve.wait_ge(sem("in_tab1"), 16)
            for b in range(NB):
                for r in range(U0 - 1):
                    i = U0 * b + r
                    qb, h = r // HG, r % HG
                    k0, k1 = key_rows(qb)
                    n = (k1 - k0) * W
                    o = (k0 - QROWS * qb + K // 2) * CCOLS
                    dve.wait_ge(sem("s1_0"), i + 1)
                    if i > 1:
                        dve.wait_ge(sem("p1_taken0"), i - 1)
                    if r == 0:
                        if b:
                            dve.wait_ge(sem("mcat0"), b)
                    v.tensor_tensor_reduce(junk[:, i % 2, 0:n].rearrange("p (f n) -> p f n", f=2),
                                           ps[:, i % 2, 0:n].rearrange("p (f n) -> p f n", f=2),
                                           tab1[:, HG * (b % NG) + h, :, o:o + n // 2],
                                           1.0, -3.0e38, ALU.add, ALU.max, mx[:, 8 * h + qb:8 * h + qb + 1])\
                        .then_inc(sem("p1_taken0"), 1)
                maxima(0, U0 * b, U0, 32, b)
                if b == 0:
                    for t in range(NT):
                        dve.wait_ge(sem(f"parts_out0_{t}"), 32)
                    for i in range(2):
                        s = slice(HT * i, HT * (i + 1))
                        dve.wait_ge(sem("tab_hi"), i + 1)
                        v.tensor_tensor(tab2f[1][:, s], u_raw[:, s], tab2f[0][:, s].bitcast(F32), ALU.subtract).then_inc(sem("tab2_ready"), 1)

            normalised(3)
            for t in range(NT):
                dve.wait_ge(sem("hb"), t + 1)
                dve.wait_ge(sem("sig"), t + 1)
                v.scalar_tensor_tensor(tmp[:, t, :], ps[:, t, :], pbe, gate[:, t, :], ALU.add, ALU.mult).then_inc(sem("yg"), 1)
                dve.wait_ge(sem("yg"), t + 1)
                v.tensor_tensor(ysum[:, t, :], tmp[:, t, :], xt[:, tile(t)], ALU.add).then_inc(sem("y3"), 1)
            dve.wait_ge(sem("pad0"), 1)
            norm(0, "lng0", "lnb0", lambda t: pad[:, t // 2, 1 + 16 * (t % 2):17 + 16 * (t % 2), 1:1 + W])
            steps = 0
            for img in range(IMG):
                dve.wait_ge(sem("lnout"), 2 * (img + 1))
                for j, i in enumerate(DVE_TAPS):
                    for t in (2 * img, 2 * img + 1):
                        r0 = 16 * (t % 2) + i // 3
                        src = pad[:, img, r0:r0 + 16, i % 3:i % 3 + W]
                        dst = x2[:, tile(t)].rearrange("p (r c) -> p r c", c=W)
                        if j == 0:
                            v.tensor_scalar(dst, src, vv(f"kc{i}"), None, ALU.mult).then_inc(sem("tap"), 1)
                        else:
                            dve.wait_ge(sem("tap"), steps - 1)
                            v.scalar_tensor_tensor(dst, src, vv(f"kc{i}"), dst, ALU.mult, ALU.add).then_inc(sem("tap"), 1)
                        steps += 1
                for t in (2 * img, 2 * img + 1):
                    dve.wait_ge(sem("tap"), steps)
                    dve.wait_ge(sem("conv"), t + 1)
                    v.tensor_tensor(x2[:, tile(t)], ps[:, t, :], x2[:, tile(t)], ALU.add).then_inc(sem("x2_ready"), 1)

            split(2, "bq2", "bk2")
            dve.wait_ge(sem("vaug2"), 1)
            for j in range(4):
                dve.wait_ge(sem("v"), NT + j + 1)
                for i in range(4):
                    c = 4 * (j % 2) + i
                    v.tensor_scalar(vaug[:, 4 * j + i, :, 0:HD], ps[:, j, 128 * i:128 * i + 128].rearrange("p (h d) -> p h d", h=NH),
                                    cc("mult")[:, c:c + 1], None, ALU.mult).then_inc(sem("vev2"), 1)
            for n in range(NB2):
                for r in range(U2 - 1):
                    i = U2 * n + r
                    qt, h = r // HG, r % HG
                    bank = 2 * (i % 2)
                    dve.wait_ge(sem("s1_2"), i + 1)
                    if r == 0:
                        if n:
                            dve.wait_ge(sem("mcat2"), n)
                    v.tensor_reduce(mx[:, 4 * h + qt:4 * h + qt + 1], ps[:, bank:bank + 2, :], AXIS.XY, ALU.max)\
                        .then_inc(sem("p1_taken2"), 1)
                maxima(2, U2 * n, U2, 16, n)

            normalised(4)
            for t in range(NT):
                dve.wait_ge(sem("gx"), t + 1)
                v.tensor_tensor(xt[:, tile(t)], tmp[:, t, :], x2[:, tile(t)], ALU.add).then_inc(sem("x3_ready"), 1)
            norm(1, "n1g", "n1b", lambda t: x3n[:, tile(t)])

            for t in range(NT):
                dve.wait_ge(sem("fb"), t + 1)
                dst = a1.rearrange("p (i j h f) -> p i j h f", i=IMG, j=8, h=H)[:, t // 2, :, 16 * (t % 2):16 * (t % 2) + 16, :]
                v.tensor_copy(dst, ps[:, 4 + t, :].rearrange("p (h j f) -> p j h f", j=8, f=4)).then_inc(sem("fb_ev"), 1)
            for img in range(IMG):
                dve.wait_ge(sem("fd"), 4)
                m = 2 * img + 1
                s = sf[1].rearrange("p (k i h) -> p k i h", i=IMG, h=H)
                v.tensor_copy(s[:, 3:KX, img, :], ps[:, (5, 6, 7, 0)[m], 0:448].rearrange("p (k h) -> p k h", h=H)).then_inc(sem("fdD"), 1)
            dve.wait_ge(sem("fdA"), 4)
            for img in range(IMG):
                m = 2 * img + 1
                v.tensor_copy(s[:, 0:3, img, :], ps[:, 4, 96 * m:96 * m + 96].rearrange("p (k h) -> p k h", h=H)).then_inc(sem("fdD"), 1)

            def shrink(q):
                half, (o, n) = q // 3, ftiles[q % 3]
                dve.wait_ge(sem("tsh"), q + 1)
                v.tensor_scalar(csh[:, q % 2, 0:n], tsh[:, q % 2, 0:n], 0.01, -0.01, ALU.min, ALU.max).then_inc(sem("csh"), 1)
                dve.wait_ge(sem("csh"), q + 1)
                v.tensor_tensor(yf[half][:, o:o + n], tsh[:, q % 2, 0:n], csh[:, q % 2, 0:n], ALU.subtract).then_inc(sem("yf"), 1)

            for q in range(6):
                half, (o, n) = q // 3, ftiles[q % 3]
                for m in range(1, 8, 2):
                    dve.wait_ge(sem("au"), 8 * q + m + 1)
                    if q > 1:
                        dve.wait_ge(sem("ad"), q - 1)
                    v.tensor_scalar(hid[:, q % 2, m, 0:n], ps[:, (8 * q + m) % 6, 0:n], vv(f"ab1_{8 * half + m}"), 0.0,
                                    ALU.add, ALU.max).then_inc(sem("ahD"), 1)
                if q:
                    shrink(q - 1)
            shrink(5)
            zv = zf.rearrange("p (i h f) -> p i f h", i=IMG, f=W)
            for kp in range(9):
                dve.wait_ge(sem("bb"), kp + 1)
                n, f0, fn = (128, 0, 2) if kp == 0 else (128, 30, 2) if kp == 8 else (256, 4 * kp - 2, 4)
                v.tensor_copy(zv[:, :, f0:f0 + fn, :], ps[:, 5 + kp % 3, 0:n].rearrange("p (i f h) -> p i f h", i=IMG, h=H))\
                    .then_inc(sem("bb_ev"), 1)
            for t in range(NT):
                dve.wait_ge(sem("bd"), t + 1)
                v.tensor_tensor(x4[:, tile(t)], ps[:, 4 + t, :], x3n[:, tile(t)], ALU.add).then_inc(sem("x4a"), 1)
                dve.wait_ge(sem("x4a"), t + 1)
                v.tensor_tensor(x4[:, tile(t)], x4[:, tile(t)], xt[:, tile(t)], ALU.add).then_inc(sem("x4_ready"), 1)
            norm(2, "n2g", "n2b", lambda t: h5[:, tile(t)])

            for a, b in enumerate(("bk3", "bv3")):
                v.tensor_scalar(cbs[:, 128 * a:128 * a + 128], cc("cenhead"), vv(b), None, ALU.mult).then_inc(sem("cbs"), 1)
            dve.wait_ge(sem("gw_ev"), 2)
            bias2 = cwb.unsqueeze(1).to_broadcast([C, 2, 256])
            for j in range(8):
                dve.wait_ge(sem("gk"), j + 1)
                v.tensor_tensor(kc[:, 2 * j:2 * j + 2, :], ps[:, j, :].rearrange("p (t n) -> p t n", t=2), bias2, ALU.add).then_inc(sem("kc"), 1)
            for j in range(8):
                dve.wait_ge(sem("ksq"), j + 1)
                v.tensor_reduce(rsk[:, 32 * j:32 * j + 32], ksq[:, 512 * j:512 * j + 512].rearrange("p (g d) -> p g d", d=DH_G),
                                AXIS.X, ALU.add).then_inc(sem("kvar"), 1)
            for j in range(8):
                dve.wait_ge(sem("krs"), j // 4 + 1)
                kv_ = kc[:, 2 * j:2 * j + 2, :].rearrange("p t (g d) -> p (t g) d", d=DH_G)
                v.tensor_tensor(kv_, kv_, rsk[:, 32 * j:32 * j + 32].unsqueeze(2).to_broadcast([C, 32, DH_G]), ALU.mult)\
                    .then_inc(sem("kn"), 1)
            done = [0]

            def step(ins):
                done[0] += 1
                ins.then_inc(sem("kvchain"), 1)
                dve.wait_ge(sem("kvchain"), done[0])

            lkg, lkb = ww(r_tab, W3A, "lkg"), ww(r_tab, W3A, "lkb")
            for img in range(IMG):
                dve.wait_ge(sem("kv"), img + 1)
                step(v.tensor_copy(sv, ps[:, 3 * img + 1, 0:1]))
                step(v.tensor_tensor(kvx[:, 0, :], ps[:, 3 * img, 0:128], lkg, ALU.mult))
                step(v.scalar_tensor_tensor(kvx[:, 1, :], lkb, sv, kvx[:, 0, :], ALU.mult, ALU.add))
                step(v.tensor_tensor(kvx[:, 2, :], ps[:, 3 * img + 2, 0:128], lkg, ALU.mult))
                step(v.scalar_tensor_tensor(kvx[:, 3, :], lkb, float(TOK), kvx[:, 2, :], ALU.mult, ALU.add))
                step(v.tensor_scalar(kvx[:, 4, :], kvx[:, 1, :], vv("lvg"), None, ALU.mult))
                step(v.scalar_tensor_tensor(kvx[:, 5, :], kvx[:, 3, :], vv("lvb"), kvx[:, 4, :], ALU.mult, ALU.add))
                v.tensor_tensor(kvt[:, img, :], kvx[:, 5, :], cc("kvmask"), ALU.mult).then_inc(sem("kvt"), 1)
            for t in range(NT):
                dve.wait_ge(sem("att"), t + 1)
                v.scalar_tensor_tensor(xt[:, tile(t)], ps[:, t, :], bvecs[:, t // 2:t // 2 + 1], h5[:, tile(t)], ALU.add, ALU.add)\
                    .then_inc(sem("x6_ready"), 1)
            norm(3, "n3g", "n3b", lambda t: x7[:, tile(t)])
            for t in range(NT):
                dve.wait_ge(sem("lnout"), 3 * NT + t + 1)
                v.tensor_copy(x7hi[:, tile(t)], x7[:, tile(t)]).then_inc(sem("x7hi"), 1)
                dve.wait_ge(sem("x7hi"), t + 1)
                v.tensor_tensor(x7lo[:, tile(t)], x7[:, tile(t)], x7hi[:, tile(t)].bitcast(F32), ALU.subtract).then_inc(sem("x7lo"), 1)

            def finish(t):
                dve.wait_ge(sem("down"), FF * (t + 1))
                v.scalar_tensor_tensor(x2[:, tile(t)], ps[:, 6 + t % 2, :], vv("bdn"), x7[:, tile(t)], ALU.add, ALU.add)\
                    .then_inc(sem("y_ready"), 1)

            for cnt in range(FF * NT):
                s, g = cnt % HRING, cnt % GRING
                dve.wait_ge(sem("gelu"), cnt + 1)
                if cnt >= HRING:
                    dve.wait_ge(sem("down"), cnt - HRING + 1)
                v.tensor_copy(hidhi[:, s, :], hidraw[:, g, :]).then_inc(sem("hidhi"), 1)
                dve.wait_ge(sem("hidhi"), cnt + 1)
                v.tensor_tensor(hidlo[:, s, :], hidraw[:, g, :], hidhi[:, s, :].bitcast(F32), ALU.subtract).then_inc(sem("hidlo"), 1)
                if cnt >= FF and cnt % FF == LAG + 1:
                    finish(cnt // FF - 1)
            finish(NT - 1)

        @block.gpsimd
        def _(pool):
            g = nc.gpsimd
            g.memset(zerob[:, :], 0.0).then_inc(sem("zeros"), 1)
            g.memset(eps, 1e-5).then_inc(sem("zeros"), 1)
            g.memset(vaug[:, :, :, :], 0.0).then_inc(sem("vaug0"), 1)
            pool.wait_ge(sem("vaug0"), 1)
            g.memset(vaug[:, :, :, HD:HD + 1], 1.0).then_inc(sem("vaug0"), 1)
            g.memset(ones[:, :], 1.0).then_inc(sem("zeros"), 1)
            g.memset(pad[:, :, :, :], 0.0).then_inc(sem("pad0"), 1)
            pool.wait_ge(sem("in_cst"), 16)
            pool.wait_ge(sem("in_vec"), 16)
            for i in range(9):
                if i == 4:
                    g.tensor_copy(kd[:, i, :], ident).then_inc(sem("kd"), 1)
                else:
                    g.tensor_scalar(kd[:, i, :], ident, vv(f"kc{i}"), None, ALU.mult).then_inc(sem("kd"), 1)
            pool.wait_ge(sem("pv0"), NCH * NB)
            g.tensor_copy(vaug[:, :, :, HD].rearrange("p (i c) h -> p i c h", i=IMG),
                          cc("mult").unsqueeze(1).unsqueeze(3).to_broadcast([C, IMG, NCH, NH])).then_inc(sem("vaug2"), 1)
            pool.wait_ge(sem("in_w3"), 16)
            for half in range(2):
                g.tensor_scalar(aw1[:, half, 0, :, :], aw1[:, half, 0, :, :], cc("sign"), None, ALU.mult).then_inc(sem("aw1s"), 1)
            pool.wait_ge(sem("aw1s"), 2)
            for half in range(2):
                g.tensor_scalar(aw2[:, half, 1, :, 0:16], aw2[:, half, 1, :, 0:16], -1.0, None, ALU.mult).then_inc(sem("aw_signed"), 1)
            pool.wait_ge(sem("pv2"), NCH * NB2)
            o = W3A["wup"][0]
            g.tensor_copy(whi[:, :], r_tab[:, o:o + 2048]).then_inc(sem("wsplit"), 1)
            pool.wait_ge(sem("wsplit"), 1)
            g.tensor_tensor(wlo[:, :], r_tab[:, o:o + 2048], whi[:, :].bitcast(F32), ALU.subtract).then_inc(sem("wsplit"), 1)
    return


def bias_tables(rpb):
    n, k = NH, K - 1
    s = window(W)
    t1 = np.zeros((QROWS, W, n, KWIN, W), rpb.dtype)
    for r in range(QROWS):
        for v in range(KWIN):
            dr = v - K // 2 - r + k
            if not 0 <= dr <= 2 * k:
                continue
            for q in range(W):
                t1[r, q, :, v, :] = NEG
                t1[r, q, :, v, s[q]:s[q] + K] = rpb[:, dr, s[q] - q + k:s[q] - q + k + K]
    t1 = t1.reshape(QROWS, W, n, KWIN, 2, CCOLS).transpose(0, 1, 2, 4, 3, 5)
    t2 = np.zeros((CROWS, CCOLS, n, 2, QWIN_R, QWIN_C), rpb.dtype)
    for half in range(2):
        c0, c1 = query_cols(half)
        for kc in range(CCOLS):
            key = CCOLS * half + kc
            for j, q in enumerate(range(c0, c1)):
                inside = s[q] <= key < s[q] + K
                for r in range(CROWS):
                    for u in range(QWIN_R):
                        dr = r - (u - K // 2) + k
                        if 0 <= dr <= 2 * k:
                            t2[r, kc, :, half, u, j] = rpb[:, dr, key - q + k] if inside else NEG
    return t1.reshape(128, -1), t2.reshape(128, -1)


def pack(**a):
    f = np.float32
    heads = np.zeros((NG, 128, C), f)
    for g in range(NG):
        for h in range(HG):
            heads[g, 32 * h:32 * h + HD] = a["L0_conv_proj_w"][64 * g + HD * h:64 * g + HD * (h + 1)]

    def column(x):
        out = np.zeros((C, 1), f)
        out[:x.size, 0] = x
        return out

    def every(x):
        return np.broadcast_to(x.reshape(1, -1), (C, x.size)).astype(f)

    qkv_b = a["L0_conv_qkv_b"]
    kern = a["L1_conv_kernel"].reshape(9, C)
    b1 = a["L3_conv_afno_b1"]
    b2 = a["L3_conv_afno_b2"].reshape(2, 2, 4, 2, BS)
    qk = np.arange(C).reshape(NG, HG, HD).transpose(0, 2, 1).reshape(-1)
    v = {"bq0": column(qkv_b[0:C][qk]), "bk0": column(qkv_b[C:2 * C][qk]), "bv0": column(qkv_b[2 * C:]),
         "pb0": column(a["L0_conv_proj_b"]), "lng0": column(a["L0_conv_ln_g"]), "lnb0": column(a["L0_conv_ln_b"]),
         "g1b": column(a["L0_conv_g1_b"]), "g2b": every(a["L0_conv_g2_b"]),
         "bq2": column(a["L2_conv_bq"][qk]), "bk2": column(a["L2_conv_bk"][qk]), "bv2": column(a["L2_conv_bv"]),
         "gamma": every(a["L2_conv_gamma"]), "bq3": column(a["L3_conv_bq"]), "bk3": column(a["L3_conv_bk"]),
         "bv3": column(a["L3_conv_bv"]), "bo3": column(a["L3_conv_bo"]), "bdn": column(a["L3_conv_b_down"]),
         "lvg": column(a["L3_conv_lnv_g"].reshape(-1)), "lvb": column(a["L3_conv_lnv_b"].reshape(-1))}
    for i in range(1, 4):
        v[f"n{i}g"], v[f"n{i}b"] = column(a[f"L3_conv_n{i}_g"]), column(a[f"L3_conv_n{i}_b"])
    for i in range(9):
        v[f"kc{i}"] = column(kern[i])
    for i in range(FF):
        v[f"bup{i}"] = column(a["L3_conv_b_up"][128 * i:128 * i + 128])
    for half in range(2):
        for t in range(2):
            for p in range(4):
                v[f"ab1_{8 * half + 4 * t + p}"] = column(b1[t, 8 * half + 2 * p:8 * half + 2 * p + 2].reshape(-1))
        v[f"ab2_{half}"] = column(b2[:, half].transpose(1, 0, 2, 3).reshape(-1))
    aw1 = np.zeros((128, 2, 2, 4, 128), f)
    aw2 = np.zeros((128, 2, 2, 4, 32), f)
    w1, w2 = a["L3_conv_afno_w1"], a["L3_conv_afno_w2"]
    E = BS * EXPF
    for half in range(2):
        for t in range(2):
            for p in range(4):
                for b in range(2):
                    n = 8 * half + 2 * p + b
                    c = HD * p + BS * b
                    for part in range(2):
                        aw1[HALF * part + c:HALF * part + c + BS, half, t, p, E * b:E * (b + 1)] = w1[part ^ t, n]
                        aw2[E * b:E * (b + 1), half, t, p, 16 * part + BS * b:16 * part + BS * (b + 1)] = w2[part ^ t, n]
    w = {"wq": a["L0_conv_qkv_w"][:, 0:C][:, qk], "wk": a["L0_conv_qkv_w"][:, C:2 * C][:, qk], "wv": a["L0_conv_qkv_w"][:, 2 * C:],
         "pw": a["L0_conv_proj_w"], "pwg0": heads[0], "pwg1": heads[1], "g1w": a["L0_conv_g1_w"],
         "g2w": np.concatenate([np.broadcast_to(a["L0_conv_g2_w"], (C // 4, C)), np.zeros((3 * C // 4, C), f)]),
         "wq2": a["L2_conv_Wq"][:, qk], "wk2": a["L2_conv_Wk"][:, qk], "wv2": a["L2_conv_Wv"],
         "wq3": a["L3_conv_wq"], "wk3": a["L3_conv_wk"], "wv3": a["L3_conv_wv"], "wo3": a["L3_conv_wo"].T,
         "lkg": every(a["L3_conv_lnk_g"]), "lkb": every(a["L3_conv_lnk_b"]),
         "aw1": aw1.reshape(128, -1), "aw2": aw2.reshape(128, -1), "wup": a["L3_conv_w_up"].T,
         "wdn": a["L3_conv_w_down"].T.reshape(FF, 128, C).transpose(1, 0, 2).reshape(128, -1)}

    def row(names):
        return np.ascontiguousarray(np.concatenate([np.asarray(w[n], f) for n, _ in names], axis=1))

    t1, t2 = bias_tables(a["L0_conv_rpb"])
    xt = a["x"].reshape(IMG, TOK, C)
    return {"xT": np.ascontiguousarray(xt.reshape(T, C).T), "xK": np.ascontiguousarray(xt[:, key_order()].reshape(T, C).T), "w0": row(W0), "w2": row(W2), "w3": row(W3),
            "vec": np.ascontiguousarray(np.concatenate([v[n] for n in VEC], axis=1)),
            "cst": CONSTS, "tab1": np.ascontiguousarray(t1), "tab2": np.ascontiguousarray(t2), "mrows": mask_rows()}


def kernel(**inputs):
    import concourse.bacc as bacc
    from concourse.bass_utils import run_bass_kernel_spmd

    arrays = pack(**{k: np.asarray(a) for k, a in inputs.items()})
    nc = bacc.Bacc("TRN2", target_bir_lowering=False, num_devices=1)
    io = {n: nc.dram_tensor(f"in_{n}", a.shape, mybir.dt.from_np(a.dtype), kind="ExternalInput").ap() for n, a in arrays.items()}
    io["out"] = nc.dram_tensor("y", (C, T), F32, kind="ExternalOutput").ap()
    build(nc, io)
    r = run_bass_kernel_spmd(nc, [{f"in_{n}": a for n, a in arrays.items()}], core_ids=[0])
    y = r.results[0]["y"]
    return np.ascontiguousarray(y.T).reshape(IMG, H, W, C)
```

```python
from contextlib import ExitStack

import numpy as np

import concourse.bass as bass
from concourse import mybir

F32 = mybir.dt.float32
BF16 = mybir.dt.bfloat16
F32R = mybir.dt.float32r
ALU = mybir.AluOpType
ACT = mybir.ActivationFunctionType
AXIS = mybir.AxisListType

C = 128
IMG, H, W = 2, 32, 32
TOK = H * W
T = IMG * TOK
TILE = 512
NT = T // TILE
NH, HD = 8, 16
HG = 4
NG = NH // HG
NB = IMG * NG
K = 7
NCH = TOK // 128
NEG = -float(2 ** 100)
RMOD = 16
R_SPLIT = 6 * HD
K1_L0 = R_SPLIT + RMOD
K2_L0 = K1_L0 + 2
K1_L2 = R_SPLIT
K2_L2 = R_SPLIT + 2
Q_PARTS = (0, 0, 0, 1, 1, 2)
K_PARTS = (0, 1, 2, 0, 1, 0)
PART_RUNS = ((0, 3), (3, 5), (5, 6))
QROWS = 4
KWIN = 10
CROWS, CCOLS = 8, 16
QWIN_R, QWIN_C = 14, 20
NB_AF, BS, EXPF = 16, 8, 8
PE_TAPS = (1, 3, 4, 5, 7)
DVE_TAPS = (0, 2, 6, 8)
HALF = C // 2
KX = W // 2 + 1
NF = KX * IMG * H
DH_G = 16
FF = 8 * C // 128


def window(n):
    return np.clip(np.arange(n) - K // 2, 0, n - K)


def key_rows(qb):
    s = window(H)
    return int(s[QROWS * qb]), int(s[QROWS * qb + QROWS - 1]) + K


def query_rows(rb):
    s = window(H)
    hit = [i for i in range(H) if s[i] < CROWS * (rb + 1) and s[i] + K > CROWS * rb]
    return hit[0], hit[-1] + 1


def query_cols(half):
    return (0, QWIN_C) if half == 0 else (W - QWIN_C, W)


def key_order():
    return np.arange(TOK).reshape(H, W // CCOLS, CCOLS).transpose(1, 0, 2).reshape(-1)


def kx_order():
    return [0, W // 2] + list(range(1, W // 2))


def shape_constants():
    c = {}
    eye = np.eye(C)
    c["ident"] = eye
    c["cen"] = eye - 1.0 / C
    c["avg"] = np.full((C, C), 1.0 / C)
    den = np.zeros((C, C))
    for h in range(HG):
        den[32 * h + HD, 32 * h:32 * h + 32] = 1.0
    c["den"] = den
    for g in range(NG):
        s = np.zeros((C, C))
        for h in range(HG):
            for j in range(HD):
                s[32 * h + j, 64 * g + HD * h + j] = 1.0
        c[f"sel{g}"] = s
    pad = K // 2
    mult = np.ones(H)
    mult[1:1 + pad] += 1
    mult[H - 1 - pad:H - 1] += 1
    c["mult"] = np.outer(mult, mult).reshape(NCH, 128).T
    head = np.kron(np.eye(C // DH_G), np.ones((DH_G, DH_G)))
    c["cenhead"] = eye - head / DH_G
    c["kvmask"] = head / TOK
    k = np.arange(W)
    n = float(W) ** -0.5
    f1 = np.zeros((W, W))
    g = np.zeros((W, W))
    for f in range(W):
        kx = (0, W // 2)[f] if f < 2 else f // 2
        im = f >= 2 and f % 2
        ang = 2 * np.pi * kx * k / W
        f1[:, f] = n * (-np.sin(ang) if im else np.cos(ang))
        g[f, :] = n * (1.0 if f < 2 else 2.0) * (-np.sin(ang) if im else np.cos(ang))
    c["f1"] = np.kron(np.eye(4), f1)
    c["g"] = np.kron(np.eye(4), g)
    ch = n * np.cos(2 * np.pi * np.outer(k, k) / H)
    sh = n * np.sin(2 * np.pi * np.outer(k, k) / H)
    d0 = np.zeros((H, 4, 2, 3, H))
    d0[:, 0, 0, 0], d0[:, 0, 1, 0] = ch, -sh
    d0[:, 1, 0, 1], d0[:, 1, 1, 1] = ch, -sh
    d0[:, 2, 0, 2], d0[:, 2, 1, 2] = ch, -sh
    d0[:, 3, 0, 2], d0[:, 3, 1, 2] = sh, ch
    c["d0"] = d0.reshape(128, -1)
    dg = np.zeros((H, 4, 2, 2, H))
    for b in range(2):
        dg[:, 2 * b, 0, b], dg[:, 2 * b, 1, b] = ch, -sh
        dg[:, 2 * b + 1, 0, b], dg[:, 2 * b + 1, 1, b] = sh, ch
    c["dg"] = dg.reshape(128, -1)
    e0 = np.zeros((2, 2, IMG, H, IMG, 2, H))
    eg = np.zeros((2, 2, IMG, H, IMG, 4, H))
    for i in range(IMG):
        for b in range(2):
            e0[0, b, i, :, i, b], e0[1, b, i, :, i, b] = ch, -sh
            eg[0, b, i, :, i, 2 * b], eg[0, b, i, :, i, 2 * b + 1] = ch, sh
            eg[1, b, i, :, i, 2 * b], eg[1, b, i, :, i, 2 * b + 1] = -sh, ch
    for p in range(2):
        c[f"e0{p}"] = e0[p].reshape(128, -1)
        c[f"eg{p}"] = eg[p].reshape(128, -1)
    c["sign"] = np.where(np.arange(C) < HALF, 1.0, -1.0)[:, None]
    return c


def place_constants():
    at, parts, n = {}, [], 0
    for name, a in shape_constants().items():
        at[name] = (n, a.shape[1])
        parts.append(a.astype(np.float32))
        n += a.shape[1]
    return at, np.ascontiguousarray(np.concatenate(parts, axis=1))


CAT, CONSTS = place_constants()


def mask_rows():
    row = np.arange(TOK) // W
    s = window(H)
    k = (row[key_order()][None] % RMOD == np.arange(RMOD)[:, None]).astype(np.float32)
    q = np.full((RMOD, TOK), NEG, np.float32)
    for t in range(TOK):
        for r in range(s[row[t]], s[row[t]] + K):
            q[r % RMOD, t] = 0.0
    one = np.ones((2, TOK), np.float32)
    m = np.concatenate([k, one, q], axis=0)
    return np.repeat(m[:, None], HG, axis=1).astype(mybir.dt.np(BF16))


VEC = ["bq0", "bk0", "pb0", "lng0", "lnb0", "g1b", "g2b"] + [f"kc{i}" for i in range(9)] + \
      ["bq2", "bk2", "bv2", "gamma", "n1g", "n1b", "n2g", "n2b", "n3g", "n3b", "bq3", "bk3", "bv3", "bo3", "bdn",
       "lvg", "lvb"] + [f"bup{i}" for i in range(FF)] + [f"ab1_{i}" for i in range(16)] + ["ab2_0", "ab2_1", "bv0"]
VAT = {n: i for i, n in enumerate(VEC)}
W0 = [("wq", C), ("wk", C), ("wv", C), ("pw", C), ("pwg0", C), ("pwg1", C), ("g1w", C // 4), ("g2w", C)]
W2 = [("wq2", C), ("wk2", C), ("wv2", C)]
W3 = [("wq3", C), ("wk3", C), ("wv3", C), ("wo3", C), ("lkg", C), ("lkb", C), ("aw1", 2048), ("aw2", 512),
      ("wup", 1024), ("wdn", 1024)]


def places(ws):
    at, n = {}, 0
    for name, w in ws:
        at[name] = (n, w)
        n += w
    return at, n



def build(nc, io):
    W0A, W0N = places(W0)
    W2A, W2N = places(W2)
    W3A, W3N = places(W3)
    ctx = ExitStack()
    with ctx:
        start = {}

        def sb(name, shape, dt=F32):
            start[name] = (nc.sbuf_base + 31) // 32 * 32
            return ctx.enter_context(nc.sbuf_tensor(name, shape, dt))

        def rounded(name, region, column, shape):
            return nc.alloc_sbuf_tensor_at(name, shape, F32R, offset=start[region] + 4 * column)

        sems = {}

        def sem(name):
            if name not in sems:
                sems[name] = ctx.enter_context(nc.semaphore(name))
            return sems[name]

        ps = ctx.enter_context(nc.psum_tensor("ps", [128, 8, TILE], F32))

        cst = sb("cst", [C, CONSTS.shape[1]])
        vec = sb("vec", [C, len(VEC)])
        w0 = sb("w0", [C, W0N])
        w2 = sb("w2", [C, W2N])
        kd = sb("kd", [C, 9, C])
        identb = sb("identb", [C, C], BF16)
        identr = sb("identr", [C, C], F32R)
        zerob = sb("zerob", [C, TILE], BF16)
        ones = sb("ones", [C, C])
        small = sb("small", [C, 16])
        eps, pbe, gb2, sv = (small[:, i:i + 1] for i in range(4))
        bvecs = small[:, 4:6]
        xt = sb("xt", [C, T])
        pad = sb("pad", [C, IMG, H + 2, W + 2])
        x2 = sb("x2", [C, T])
        vaug = sb("vaug", [C, IMG * NCH, NH, 32])
        mx = sb("mx", [C, 32])
        mcat = sb("mcat", [C, 64], BF16)
        mt = sb("mt", [64, C], BF16)
        r_tab = sb("r_tab", [C, 9088])
        r_stk = sb("r_stk", [C, 12288])
        r_prt = sb("r_prt", [C, 4480])
        r_p = sb("r_p", [C, 6144])
        r_o = sb("r_o", [C, 4096])

        def cc(name):
            o, n = CAT[name]
            return cst[:, o:o + n]

        def vv(name, n=1):
            return vec[:, VAT[name]:VAT[name] + n]

        def ww(t, at, name):
            o, n = at[name]
            return t[:, o:o + n]

        ident, cen, avg, dens = cc("ident"), cc("cen"), cc("avg"), cc("den")
        TAB1 = NH * KWIN * W
        TW = 2 * QWIN_R * QWIN_C
        HT = NH // 2 * TW
        tab1 = r_tab[:, 0:TAB1].rearrange("p (n f v c) -> p n f (v c)", n=NH, f=2, c=CCOLS)
        tab2f = [rounded("tab2hi", "r_tab", TAB1, [C, NH * TW])[:, :], rounded("tab2lo", "r_prt", 0, [C, NH * TW])[:, :]]
        tab2 = [a.rearrange("p (n f u c) -> p n f (u c)", n=NH, f=2, c=QWIN_C) for a in tab2f]
        u_raw = r_p[:, 0:NH * TW]
        stk = r_stk[:, :].bitcast(BF16).rearrange("p (s a h n) -> p s a h n", s=3, a=2, h=HG)
        parts = [r[:, 0:3072].bitcast(BF16).rearrange("p (b a r n) -> p b a r n", b=2, a=2, r=3) for r in (r_prt, r_o)]
        rem = r_prt[:, 3072:4096].rearrange("p (b n) -> p b n", b=2)
        NP0 = QWIN_R * QWIN_C
        pa0 = r_p[:, 0:8 * NP0].rearrange("p (s h n) -> p s h n", s=4, h=2)
        junk = r_p[:, NH * TW:NH * TW + 2 * KWIN * W].rearrange("p (s n) -> p s n", s=2)
        pa2 = r_p[:, :].rearrange("p (s n) -> p s n", s=12)
        oraw = r_o[:, :].rearrange("p (b n) -> p b n", b=NB)

        def piece(region, column):
            return region[:, column:column + TILE]

        def rec(i):
            return piece(r_stk, (8192 if i < 4 else -2048) + TILE * i)

        og = r_stk[:, 4096:8192].rearrange("p (i n) -> p i n", n=TILE)
        gate = r_tab[:, TAB1 + NH * TW:TAB1 + NH * TW + T].rearrange("p (t n) -> p t n", n=TILE)
        ysum = r_stk[:, 10240:12288].rearrange("p (t n) -> p t n", n=TILE)
        g1s = x2[0:C // 4, :].rearrange("p (t n) -> p t n", n=TILE)

        def sqs(k, t):
            return piece(r_p, (2560, 3072, 0, 512)[t] if k == 0 else TILE * t)

        def rss(k, t):
            return piece(r_p, (3584, 4096, 1024, 1536)[t] if k == 0 else 2048 + TILE * t)

        def t1s(k, t):
            return piece(r_p, (4608, 5120, 2048, 5632)[t] if k == 0 else 4096 + TILE * t)

        def cen_bank(k, t):
            return 0 if k == 0 and t < 2 else 4 + t

        def var_bank(k, t):
            return 1 if k == 0 and t < 2 else t

        def den_bank(layer, i):
            return i % 2 if layer == 3 and i < 4 else i

        tmp = r_prt[:, 0:2048].rearrange("p (t n) -> p t n", n=TILE)
        x3n = r_o[:, 0:2048]
        x4 = r_o[:, 2048:4096]
        x3t = r_stk[:, 0:2048]
        a1 = r_stk[:, 2048:4096]
        zt = r_stk[:, 4096:6144]
        sf = [r_stk[:, 6144 + i * NF:6144 + (i + 1) * NF] for i in range(2)]
        yf = [r_stk[:, 8320 + i * NF:8320 + (i + 1) * NF] for i in range(2)]
        yt = r_stk[:, 0:2304].rearrange("p (o n) -> p o n", o=2)
        zf = r_stk[:, 2304:4352]
        zt2 = r_stk[:, 4352:6400]
        h5 = r_stk[:, 6400:8448]
        FT = 384
        ftiles = [(o, min(FT, NF - o)) for o in range(0, NF, FT)]
        hid = r_p[:, :].rearrange("p (b m n) -> p b m n", b=2, m=8)
        tsh = r_prt[:, 0:2 * FT].rearrange("p (b n) -> p b n", b=2)
        csh = r_prt[:, 2 * FT:4 * FT].rearrange("p (b n) -> p b n", b=2)
        cw = r_prt[:, 0:256]
        cwb = r_prt[:, 256:512]
        cbs = r_prt[:, 512:768]
        kvt = r_prt[:, 768:768 + 2 * C].rearrange("p (i n) -> p i n", i=IMG)
        kws = r_prt[:, 1024:1024 + 2 * C].rearrange("p (i n) -> p i n", i=IMG)
        ms = r_prt[:, 1280:1280 + 2 * C].rearrange("p (i n) -> p i n", i=IMG)
        kvx = r_prt[:, 1536:1536 + 6 * C].rearrange("p (i n) -> p i n", n=C)
        rsk = r_prt[:, 2304:2560]
        kc = r_p[:, 0:32 * (C + 1)].rearrange("p (t a n) -> p t a n", a=2, n=C + 1)
        kcm = r_p[:, 0:32 * (C + 1)].rearrange("p (m n) -> p m n", n=C + 1)
        ksum = r_prt[:, 2560:2560 + 2 * C].rearrange("p (i n) -> p i n", i=IMG)
        ksq = r_stk[:, 0:4096]
        x7 = r_o[:, 0:2048]
        HRING, GRING, LAG = 8, 4, 4
        whi, wlo = rounded("whi", "vaug", 0, [C, 2048]), rounded("wlo", "vaug", 2048, [C, 2048])
        x7hi, x7lo = rounded("x7hi", "r_o", 2048, [C, T]), rounded("x7lo", "r_prt", 0, [C, T])
        hidhi, hidlo = (rounded(n, "r_stk", HRING * TILE * i, [C, HRING, TILE]) for i, n in enumerate(("hidhi", "hidlo")))
        hidraw = r_stk[:, 8192:8192 + GRING * TILE].rearrange("p (s n) -> p s n", n=TILE)
        aw1 = ww(r_tab, W3A, "aw1").rearrange("p (f t m n) -> p f t m n", f=2, t=2, m=4)
        aw2 = ww(r_tab, W3A, "aw2").rearrange("p (f t m n) -> p f t m n", f=2, t=2, m=4)

        scr = nc.dram_tensor("scr", (2, 2, 3, IMG, C, TOK), BF16, kind="Internal").ap()
        block = ctx.enter_context(nc.Block())

        def tile(t):
            return slice(t * TILE, (t + 1) * TILE)

        def mm(out, lhsT, rhs, start=True, stop=True, **kw):
            return nc.tensor.matmul(out, lhsT, rhs, start=start, stop=stop, **kw)

        seg = {}
        for rb in range(H // CROWS):
            a, b = query_rows(rb)
            seg[rb] = [(s, max(a, 16 * s), min(b, 16 * s + 16)) for s in range(2) if max(a, 16 * s) < min(b, 16 * s + 16)]
        U0 = TOK // 128 * HG + 1
        U2 = TILE // 128 * HG + 1
        LEAD0, LEAD2 = 6, 6
        NB2 = 2 * NB
        MAX_DELAY = 5

        def l2_bank(u):
            tail = u - NCH * HG * (NB2 - 1)
            return 4 + u % 3 if tail < 0 else tail % 7

        @block.sync
        def _(sp):
            sp.dma_start(w0[:, :], io["w0"]).then_inc(sem("in_w0"), 16)
            sp.dma_start(vec[:, :], io["vec"]).then_inc(sem("in_vec"), 16)
            for t in range(2):
                sp.dma_start(xt[:, tile(t)], io["xT"][:, tile(t)]).then_inc(sem(f"in_x{t}"), 16)
            sp.dma_start(x2[:, 0:TOK], io["xK"][:, 0:TOK]).then_inc(sem("in_xK0"), 16)
            for t in range(2, 4):
                sp.dma_start(xt[:, tile(t)], io["xT"][:, tile(t)]).then_inc(sem(f"in_x{t}"), 16)
            sp.dma_start(x2[:, TOK:T], io["xK"][:, TOK:T]).then_inc(sem("in_xK1"), 16)
            sp.dma_start(stk[96:96 + RMOD + 2, :, 1].rearrange("p s h n -> p s (h n)"),
                         io["mrows"][0:RMOD + 2].rearrange("p h n -> p (h n)").unsqueeze(1).to_broadcast([RMOD + 2, 3, HG * TOK]))\
                .then_inc(sem("in_mask"), 16)
            sp.dma_start(stk[96:96 + RMOD, :, 0].rearrange("p s h n -> p s (h n)"),
                         io["mrows"][RMOD + 2:2 * RMOD + 2].rearrange("p h n -> p (h n)").unsqueeze(1).to_broadcast([RMOD, 3, HG * TOK]))\
                .then_inc(sem("in_mask"), 16)

            def load_stack(layer, b):
                img, g, s = b // NG, b % NG, b % 3
                for lo, hi in PART_RUNS:
                    n = hi - lo
                    for a in range(2):
                        rows = slice(HD * g * HG, HD * (g + 1) * HG)
                        src = scr[layer // 2, a, :, img, rows, :].rearrange("r (j h) n -> r j (h n)", h=HG)
                        first = (Q_PARTS, K_PARTS)[a][lo]
                        src = src[first:first + n] if a else src[first:first + 1].to_broadcast([n, HD, HG * TOK])
                        sp.dma_start(stk[HD * lo:HD * hi, s, a].rearrange("p h n -> p (h n)"), src).then_inc(sem(f"stk{layer}_{b}"), 16)

            def store_parts(layer, t):
                for a in range(2):
                    sp.wait_ge(sem("split"), 2 * NT * (layer // 2) + 2 * t + a + 1)
                    sp.dma_start(scr[layer // 2, a, :, t // 2].rearrange("r p n -> p r n")[:, :, tile(t % 2)],
                                 parts[t // 2][:, t % 2, a]).then_inc(sem(f"parts_out{layer}_{t}"), 16)

            def image_stored(layer, img):
                sp.wait_ge(sem(f"parts_out{layer}_{2 * img}"), 32)
                sp.wait_ge(sem(f"parts_out{layer}_{2 * img + 1}"), 32)

            store_parts(0, 0)
            store_parts(0, 1)
            sp.dma_start(r_tab[:, 0:TAB1], io["tab1"]).then_inc(sem("in_tab1"), 16)
            image_stored(0, 0)
            load_stack(0, 0)
            store_parts(0, 2)
            sp.dma_start(cst[:, :], io["cst"]).then_inc(sem("in_cst"), 16)
            store_parts(0, 3)
            sp.dma_start(u_raw, io["tab2"]).then_inc(sem("in_u"), 16)
            load_stack(0, 1)
            image_stored(0, 1)
            load_stack(0, 2)
            sp.dma_start(w2[:, :], io["w2"]).then_inc(sem("in_w2"), 16)
            for b in range(NB):
                sp.wait_ge(sem("p1_taken0"), U0 * (b + 1))
                for part in range(2):
                    sp.dma_start(stk[K1_L0 + part:K1_L0 + part + 1, b % 3, 0].rearrange("p h (a n) -> p (h a) n", n=128),
                                 mt[32 * part:32 * part + 32, :]).then_inc(sem("mrow0"), 16)
                if b == 1:
                    sp.wait_ge(sem("pv0"), NCH)
                    load_stack(0, 3)
            sp.wait_ge(sem("pv0"), NCH * NB)
            sp.dma_start(r_tab[:, 0:W3N], io["w3"]).then_inc(sem("in_w3"), 16)

            sp.wait_ge(sem("og"), 8)
            sp.wait_ge(sem("lnout"), NT)
            sp.dma_start(stk[96:98, :, 1].rearrange("p s h n -> p s (h n)"),
                         io["mrows"][RMOD:RMOD + 2].rearrange("p h n -> p (h n)").unsqueeze(1).to_broadcast([2, 3, HG * TOK]))\
                .then_inc(sem("in_ones"), 16)
            for t in range(NT):
                store_parts(2, t)
                if t % 2:
                    image_stored(2, t // 2)
                    load_stack(2, 2 * (t // 2))
                    if t == 1:
                        load_stack(2, 1)
            for n in range(NB2):
                b, qh = n // 2, n % 2
                sp.wait_ge(sem("p1_taken2"), U2 * (n + 1))
                for h in range(HG):
                    sp.dma_start(stk[K1_L2:K1_L2 + 2, b % 3, 0, h, tile(qh)], mt[8 * h:8 * h + 8, :]).then_inc(sem("mrow2"), 16)
                if n == 2:
                    sp.wait_ge(sem("pv2"), 2 * NCH)
                    load_stack(2, 3)
            for t in range(NT):
                sp.wait_ge(sem("y_ready"), t + 1)
                sp.dma_start(io["out"][:, tile(t)], x2[:, tile(t)]).then_inc(sem("out"), 16)
            sp.wait_ge(sem("out"), 16 * NT)

        @block.tensor
        def _(pe):
            def project(layer, src, keys, w, at, suffix, tiles):
                for t in tiles:
                    if layer == 0:
                        pe.wait_ge(sem(f"in_x{t}"), 16)
                        pe.wait_ge(sem("wq_scaled"), 2)
                    for a, name in enumerate(("wq", "wk")):
                        if t >= 2:
                            pe.wait_ge(sem("rem"), 2 * NT * (layer // 2) + 2 * (t - 2) + a + 1)
                        if a and layer == 0 and t % 2 == 0:
                            pe.wait_ge(sem(f"in_xK{t // 2}"), 16)
                        mm(ps[:, 4 + 2 * (t % 2) + a, :], ww(w, at, name + suffix), (src, keys)[a][:, tile(t)]).then_inc(sem("qk"), 1)

            def values(keys, w, at, suffix, bank):
                for j in range(4):
                    if bank:
                        pe.wait_ge(sem("rem"), 2 * NT + NT + j + 1)
                    for i in range(4):
                        c = 4 * j + i
                        last = mm(ps[:, bank + j, 128 * i:128 * i + 128], keys[:, 128 * c:128 * c + 128], ww(w, at, "wv" + suffix))
                    last.then_inc(sem("v"), 1)

            def denominator(layer, i):
                t, g = i // 2, i % 2
                if layer == 3 and 2 <= i < 4:
                    pe.wait_ge(sem("lnd"), i - 1)
                mm(ps[:, den_bank(layer, i), :], dens, oraw[:, 2 * (t // 2) + g, tile(t % 2)]).then_inc(sem("den"), 1)

            def heads(layer, t, wa, wb):
                pe.wait_ge(sem("og"), 2 * NT * (layer - 3) + 2 * t + 2)
                mm(ps[:, t, :], wa, og[:, 2 * t, :], stop=False)
                mm(ps[:, t, :], wb, og[:, 2 * t + 1, :], start=False).then_inc(sem("hb"), 1)

            def centre(k, t, src, ready):
                pe.wait_ge(sem(ready), t + 1)
                mm(ps[:, cen_bank(k, t), :], cen, src(t)).then_inc(sem("cen"), 1)

            def variance(k, t):
                pe.wait_ge(sem("sq"), NT * k + t + 1)
                mm(ps[:, var_bank(k, t), :], avg, sqs(k, t)).then_inc(sem("var"), 1)

            def norm(k, src, ready):
                for t in range(NT):
                    centre(k, t, src, ready)
                    if t:
                        variance(k, t - 1)
                variance(k, NT - 1)

            pe.wait_ge(sem("in_w0"), 16)
            project(0, xt, x2, w0, W0A, "", range(NT))
            values(x2, w0, W0A, "", 0)
            pe.wait_ge(sem("in_vec"), 16)
            pe.wait_ge(sem("rem"), 2 * NT)
            for t in range(NT):
                mm(ps[0:C // 4, 4 + t, :], ww(w0, W0A, "g1w"), xt[:, tile(t)]).then_inc(sem("g1"), 1)

            def l0_first(i):
                b, r = i // U0, i % U0
                bank = i % 2
                if i > 1:
                    pe.wait_ge(sem("p1_taken0"), i - 1)
                if r == 0:
                    pe.wait_ge(sem(f"stk0_{b}"), 6 * 16)
                    pe.wait_ge(sem("in_mask"), 32)
                if r < U0 - 1:
                    qb, h = r // HG, r % HG
                    k0, k1 = key_rows(qb)
                    mm(ps[:, bank, 0:(k1 - k0) * W].rearrange("p (f n) -> p f n", f=2), stk[0:K1_L0, b % 3, 0, h, 128 * qb:128 * qb + 128],
                       stk[0:K1_L0, b % 3, 1, h].rearrange("p (f n) -> p f n", f=2)[:, :, k0 * CCOLS:k1 * CCOLS]).then_inc(sem("s1_0"), 1)
                else:
                    pe.wait_ge(sem("mcat0"), b + 1)
                    pe.wait_ge(sem("identb"), 1)
                    nc.tensor.transpose(ps[0:64, bank, 0:64].bitcast(BF16), mcat[:, :], identb[:, :]).then_inc(sem("s1_0"), 1)

            def l0_second(u, between):
                b, c, pair = u // 16, u // 2 % 8, u % 2
                rb, half = c % 4, c // 4
                r0, r1 = query_rows(rb)
                c0, c1 = query_cols(half)
                n = (r1 - r0) * QWIN_C
                bank = 2 + 2 * (u % 2)
                if u % 16 == 0:
                    pe.wait_ge(sem("mrow0"), 32 * (b + 1))
                    pe.wait_ge(sem("tab2_ready"), b % NG + 1)
                if u > 1:
                    pe.wait_ge(sem("exp0"), u - 1)
                u0 = (r0 - CROWS * rb + K // 2) * QWIN_C
                for hh in range(2):
                    h = 2 * pair + hh
                    qv = stk[0:K2_L0, b % 3, 0, h].rearrange("p (r c) -> p r c", c=W)
                    out = ps[:, bank + hh, 0:n]
                    mm(out.rearrange("p (r c) -> p r c", c=QWIN_C), stk[0:K2_L0, b % 3, 1, h, 128 * c:128 * c + 128],
                       qv[:, r0:r1, c0:c1], stop=False)
                    mm(out, identr[:, :], tab2[0][:, HG * (b % NG) + h, half, u0:u0 + n], start=False, stop=False)
                    last = mm(out, identr[:, :], tab2[1][:, HG * (b % NG) + h, half, u0:u0 + n], start=False)
                    if hh == 0:
                        between()
                last.then_inc(sem("s2_0"), 1)

            def l0_values(cc_):
                b, c = cc_ // NCH, cc_ % NCH
                rb, half = c % 4, c // 4
                r0, _ = query_rows(rb)
                c0, c1 = query_cols(half)
                if c == 0:
                    if b:
                        pe.wait_ge(sem("accev0"), b)
                    for s in range(2):
                        mm(ps[:, 6 + s, :], zerob[:, 0:C], zerob[:, :])
                pe.wait_ge(sem("exp0"), 2 * cc_ + 2)
                for s, a, z in seg[rb]:
                    for h in range(HG):
                        out = ps[32 * h:32 * h + 32, 6 + s, :].rearrange("p (r c) -> p r c", c=W)[:, a - 16 * s:z - 16 * s, c0:c1]
                        last = mm(out, vaug[:, b // NG * NCH + c, HG * (b % NG) + h, :],
                                  pa0[:, (2 * cc_ + h // 2) % 4, h % 2, (a - r0) * QWIN_C:(z - r0) * QWIN_C]
                                  .rearrange("p (r c) -> p r c", c=QWIN_C),
                                  start=False, stop=True, skip_group_check=True)
                last.then_inc(sem("pv0"), 1)

            pe.wait_ge(sem("vev0"), 4)
            mm(ps[:, 3, 0:1], ww(w0, W0A, "pw"), vv("bv0")).then_inc(sem("pbe_mm"), 1)
            issued = 0

            def first_up_to(limit):
                nonlocal issued
                while issued < min(limit, NB * U0):
                    l0_first(issued)
                    issued += 1

            pwg = ww(w0, W0A, "pwg0"), ww(w0, W0A, "pwg1")

            def first_image(s):
                if s == 0:
                    pe.wait_ge(sem("p1_taken0"), NB * U0)
                    pe.wait_ge(sem("accev0"), NG)
                if s < 2:
                    denominator(3, 2 * s)
                    denominator(3, 2 * s + 1)
                elif s < 4:
                    pe.wait_ge(sem("lnd"), s + 1)
                    heads(3, s - 2, *pwg)
                else:
                    t = (s - 4) // 2
                    if s % 2 == 0:
                        if t:
                            pe.wait_ge(sem("ng"), t)
                        centre(0, t, lambda t: ysum[:, t, :], "y3")
                    else:
                        pe.wait_ge(sem("y3"), 2)
                        if t:
                            pe.wait_ge(sem("lv"), t)
                        variance(0, t)

            for s in range(NB * NCH):
                base = U0 + LEAD0 + s * U0 // NCH
                if s == 0:
                    for t in range(NT):
                        pe.wait_ge(sem("g1r"), t + 1)
                        mm(ps[:, 4 + t, :], ww(w0, W0A, "g2w")[0:C // 4, :], g1s[:, t, :]).then_inc(sem("g2"), 1)
                    first_up_to(U0)
                    pe.wait_ge(sem("sig"), NT)
                    pe.wait_ge(sem("identr"), 1)
                    pe.wait_ge(sem("pbe_ready"), 1)
                    pe.wait_ge(sem("zeros"), 3)
                first_up_to(base + 1)
                l0_second(2 * s, lambda: first_up_to(base + 2))
                first_up_to(base + 3)
                l0_second(2 * s + 1, lambda: first_up_to(base + 4))
                if s:
                    l0_values(s - 1)
                if s >= (NB - 1) * NCH:
                    first_image(s - (NB - 1) * NCH)
            l0_values(NB * NCH - 1)
            pe.wait_ge(sem("accev0"), NB)

            pe.wait_ge(sem("kd"), len(PE_TAPS))
            def convolve(t):
                img, r0 = t // 2, 16 * (t % 2)
                pe.wait_ge(sem("lnout"), 2 * (img + 1))
                for i in PE_TAPS:
                    dy, dx = i // 3, i % 3
                    last = mm(ps[:, t, :], kd[:, i, :], pad[:, img, r0 + dy:r0 + dy + 16, dx:dx + W],
                              start=i == PE_TAPS[0], stop=i == PE_TAPS[-1])
                last.then_inc(sem("conv"), 1)

            def project2(t):
                pe.wait_ge(sem("x2_ready"), t + 1)
                project(2, x2, x2, w2, W2A, "2", (t,))

            for i in range(4, 8):
                denominator(3, i)
            convolve(0)
            convolve(1)
            heads(3, 2, *pwg)
            heads(3, 3, *pwg)
            pe.wait_ge(sem("in_w2"), 16)
            pe.wait_ge(sem("lnd"), 6)
            project2(0)
            pe.wait_ge(sem("lnd"), 8)
            centre(0, 2, lambda t: ysum[:, t, :], "y3")
            centre(0, 3, lambda t: ysum[:, t, :], "y3")
            variance(0, 2)
            variance(0, 3)
            pe.wait_ge(sem("lnout"), NT)
            project2(1)
            convolve(2)
            convolve(3)
            project2(2)
            project2(3)
            values(x2, w2, W2A, "2", 4)

            def l2_first(i):
                n, r = i // U2, i % U2
                b, qh = n // 2, n % 2
                bank = 2 * (i % 2)
                if i > 1:
                    pe.wait_ge(sem("p1_taken2"), i - 1)
                if n % 2 == 0 and r == 0:
                    pe.wait_ge(sem(f"stk2_{b}"), 6 * 16)
                if r < U2 - 1:
                    qt, h = r // HG, r % HG
                    q0 = qh * TILE + 128 * qt
                    for kh in range(2):
                        last = mm(ps[:, bank + kh, :], stk[0:K1_L2, b % 3, 0, h, q0:q0 + 128],
                                  stk[0:K1_L2, b % 3, 1, h, tile(kh)])
                    last.then_inc(sem("s1_2"), 1)
                else:
                    pe.wait_ge(sem("mcat2"), n + 1)
                    nc.tensor.transpose(ps[0:32, bank, 0:64].bitcast(BF16), mcat[:, 0:32], identb[:, :]).then_inc(sem("s1_2"), 1)

            def l2_second(u):
                n, c, h = u // 32, u // 4 % 8, u % 4
                b, qh = n // 2, n % 2
                if u % 32 == 0:
                    pe.wait_ge(sem("mrow2"), 64 * (n + 1))
                    pe.wait_ge(sem("in_ones"), 16)
                tail = u - NCH * HG * (NB2 - 1)
                if tail == 0:
                    pe.wait_ge(sem("p1_taken2"), NB2 * U2)
                if tail >= 0:
                    pe.wait_ge(sem("exp2"), u - 6 if tail > 6 or tail < 4 else u - tail)
                elif u > 2:
                    pe.wait_ge(sem("exp2"), u - 2)
                mm(ps[:, l2_bank(u), :], stk[0:K2_L2, b % 3, 1, h, 128 * c:128 * c + 128],
                   stk[0:K2_L2, b % 3, 0, h, tile(qh)]).then_inc(sem("s2_2"), 1)

            def l2_values(cc_):
                n, c = cc_ // NCH, cc_ % NCH
                b = n // 2
                if c == 0:
                    if n:
                        pe.wait_ge(sem("accev2"), n)
                pe.wait_ge(sem("exp2"), 4 * cc_ + 4)
                for h in range(HG):
                    last = mm(ps[32 * h:32 * h + 32, 7, :], vaug[:, b // NG * NCH + c, HG * (b % NG) + h, :],
                              pa2[:, (4 * cc_ + h) % 12, :], start=c == 0, stop=c == NCH - 1)
                last.then_inc(sem("pv2"), 1)

            issued = last_unit = 0
            for s in range(NB2 * NCH):
                upto = min(U2 + LEAD2 + (s + 1) * U2 // NCH, NB2 * U2)
                if s == 0:
                    while issued < U2:
                        l2_first(issued)
                        issued += 1
                    pe.wait_ge(sem("vev2"), 16)
                for h in range(HG):
                    while h != 1 and issued < upto and (issued % U2 < U2 - 1 or 4 * s + h >= last_unit + MAX_DELAY):
                        l2_first(issued)
                        issued += 1
                        last_unit = 4 * s + h
                        if h != 3:
                            break
                    l2_second(4 * s + h)
                if s:
                    l2_values(s - 1)
            l2_values(NB2 * NCH - 1)
            pe.wait_ge(sem("accev2"), NB2)

            for i in range(2 * NT):
                denominator(4, i)
            for t in range(NT):
                heads(4, t, cc("sel0"), cc("sel1"))
            norm(1, lambda t: xt[:, tile(t)], "x3_ready")

            for t in range(NT):
                pe.wait_ge(sem("lnout"), NT + t + 1)
                for i in range(4):
                    last = nc.tensor.transpose(ps[:, t, 128 * i:128 * i + 128], x3n[:, t * TILE + 128 * i:t * TILE + 128 * i + 128], ident)
                last.then_inc(sem("fa"), 1)
            for t in range(NT):
                pe.wait_ge(sem("fa_ev"), t + 1)
                for i in range(4):
                    last = mm(ps[:, 4 + t, 128 * i:128 * i + 128], x3t[:, t * TILE + 128 * i:t * TILE + 128 * i + 128], cc("f1"))
                last.then_inc(sem("fb"), 1)
            for q in range(4):
                pe.wait_ge(sem("fb_ev"), 2 * (q // 2) + 2)
                for i in range(4):
                    last = nc.tensor.transpose(ps[:, q, 128 * i:128 * i + 128], a1[:, q * TILE + 128 * i:q * TILE + 128 * i + 128], ident)
                last.then_inc(sem("fc"), 1)
            pe.wait_ge(sem("fb_ev"), 4)
            d0 = cc("d0").rearrange("p (o n) -> p o n", o=2)
            dg = cc("dg").rearrange("p (o n) -> p o n", o=2)
            for m in range(4):
                img, half = m // 2, m % 2
                pe.wait_ge(sem("fc_ev"), 2 * img + 2)
                bank = (5, 6, 7, 0)[m]
                if m == 3:
                    pe.wait_ge(sem("fc_ev"), 4)
                for ro in range(2):
                    o = slice(64 * ro, 64 * ro + 64)
                    for j in range(8):
                        wgt = zt[:, (8 * img + j) * C + 64 * half:(8 * img + j) * C + 64 * half + 64]
                        if j == 0:
                            last = mm(ps[o, 4, 96 * m:96 * m + 96], wgt, d0[:, ro, :])
                        else:
                            last = mm(ps[o, bank, 64 * (j - 1):64 * j], wgt, dg[:, ro, :])
                last.then_inc(sem("fd"), 1)

            pe.wait_ge(sem("in_w3"), 16)
            pe.wait_ge(sem("aw_signed"), 2)
            pe.wait_ge(sem("fdA"), 4)
            pe.wait_ge(sem("fdD"), 4)

            def af_up(q):
                half, (o, n) = q // 3, ftiles[q % 3]
                for m in range(8):
                    cnt = 8 * q + m
                    if cnt >= 6:
                        pe.wait_ge(sem("ahA" if cnt % 2 == 0 else "ahD"), (cnt - 6) // 2 + 1)
                    mm(ps[:, cnt % 6, 0:n], aw1[:, half, m // 4, m % 4, :], sf[half][:, o:o + n])\
                        .then_inc(sem("au"), 1)

            def af_down(q):
                half, (o, n) = q // 3, ftiles[q % 3]
                pe.wait_ge(sem("ahA"), 4 * (q + 1))
                pe.wait_ge(sem("ahD"), 4 * (q + 1))
                if q > 1:
                    pe.wait_ge(sem("tsh"), q - 1)
                for t in range(2):
                    for p in range(4):
                        last = mm(ps[32 * p:32 * p + 32, 6 + q % 2, 0:n], aw2[:, half, t, p, :],
                                  hid[:, q % 2, 4 * t + p, 0:n], start=t == 0, stop=t == 1)
                last.then_inc(sem("ad"), 1)

            for q in range(6):
                af_up(q)
                if q:
                    af_down(q - 1)
            af_down(5)

            pe.wait_ge(sem("ahA"), 24)
            pe.wait_ge(sem("ahD"), 24)
            for i in range(18):
                kp, half = i // 2, i % 2
                pe.wait_ge(sem("yf"), 6 if half else 3)
                o = min(128 * kp, NF - 128)
                last = nc.tensor.transpose(ps[:, i // 4, 128 * (i % 4):128 * (i % 4) + 128], yf[half][:, o:o + 128], ident)
                if i % 4 == 3 or i == 17:
                    last.then_inc(sem("ba"), 1)
            for kp in range(9):
                pe.wait_ge(sem("ba_ev"), 2 * (kp // 2 + 1))
                if kp == 0:
                    pe.wait_ge(sem("tsh"), 6)
                if kp > 2:
                    pe.wait_ge(sem("bb_ev"), kp - 2)
                bank = 5 + kp % 3
                rows = slice(64, 128) if kp == 8 else slice(0, 128)
                for half in range(2):
                    for part in range(2):
                        e = cc(f"e0{part}" if kp == 0 else f"eg{part}").rearrange("p (i f h) -> p i f h", i=IMG, h=H)
                        if kp == 8:
                            e = e[:, :, 2:4, :]
                        n = 128 if kp in (0, 8) else 256
                        last = mm(ps[64 * half:64 * half + 64, bank, 0:n], yt[rows, part, 64 * (2 * kp + half):64 * (2 * kp + half) + 64], e[rows], start=part == 0, stop=part == 1)
                last.then_inc(sem("bb"), 1)
            for q in range(4):
                pe.wait_ge(sem("bb_ev"), 9)
                pe.wait_ge(sem("ba_ev"), 10)
                for i in range(4):
                    last = nc.tensor.transpose(ps[:, q, 128 * i:128 * i + 128], zf[:, q * TILE + 128 * i:q * TILE + 128 * i + 128], ident)
                last.then_inc(sem("bc"), 1)
            for t in range(NT):
                pe.wait_ge(sem("bc_ev"), t + 1)
                for i in range(4):
                    last = mm(ps[:, 4 + t, 128 * i:128 * i + 128], zt2[:, t * TILE + 128 * i:t * TILE + 128 * i + 128], cc("g"))
                last.then_inc(sem("bd"), 1)
            norm(2, lambda t: x4[:, tile(t)], "x4_ready")

            pe.wait_ge(sem("lnout"), 2 * NT + NT)
            for a, name in enumerate(("wk3", "wv3")):
                mm(ps[:, 0, 128 * a:128 * a + 128], ww(r_tab, W3A, name), cc("cenhead"))
            pe.wait_ge(sem("cbs"), 2)
            mm(ps[:, 1, 0:256], ones[:, :], cbs).then_inc(sem("gw"), 1)
            for j in range(8):
                if j == 0:
                    pe.wait_ge(sem("gw_ev"), 2)
                for i in range(2):
                    tk = 2 * j + i
                    last = mm(ps[:, j, 256 * i:256 * i + 256], h5[:, 128 * tk:128 * tk + 128], cw)
                last.then_inc(sem("gk"), 1)
            pe.wait_ge(sem("kc_ones"), 1)
            pe.wait_ge(sem("kc"), 8)
            for img in range(IMG):
                for i in range(8):
                    pe.wait_ge(sem("kn"), 4 * img + i // 2 + 1)
                    tk = 8 * img + i
                    mm(ps[:, 3 * img, 0:C + 1], kc[:, tk, 1, 0:C], kc[:, tk, 0, :], start=i == 0, stop=i == 7)
                pe.wait_ge(sem("ksum"), img + 1)
                mm(ps[:, 3 * img + 2, 0:128], ones[:, :], ksum[:, img, :]).then_inc(sem("kv"), 1)
            for img in range(IMG):
                pe.wait_ge(sem("kvt"), img + 1)
                mm(ps[:, 6, 128 * img:128 * img + 128], kvt[:, img, :], ww(r_tab, W3A, "wo3")).then_inc(sem("kw"), 1)
                pe.wait_ge(sem("kw_ev"), img + 1)
                mm(ps[:, 7, 128 * img:128 * img + 128], ww(r_tab, W3A, "wq3"), kws[:, img, :])
                mm(ps[:, 7, 256 + img:257 + img], kws[:, img, :], vv("bq3")).then_inc(sem("km"), 1)
                pe.wait_ge(sem("km_ev"), 2 * img + 2)
            for t in range(NT):
                if t == 0:
                    pe.wait_ge(sem("kvt"), IMG)
                mm(ps[:, t, :], ms[:, t // 2, :], h5[:, tile(t)]).then_inc(sem("att"), 1)
            norm(3, lambda t: xt[:, tile(t)], "x6_ready")

            def three(out, w, x, start, stop):
                mm(out, w[0], x[0], start=start, stop=False)
                mm(out, w[0], x[1], start=False, stop=False)
                return mm(out, w[1], x[0], start=False, stop=stop)

            def up(cnt):
                t, m = cnt // FF, cnt % FF
                if cnt > 5:
                    pe.wait_ge(sem("gelu"), cnt - 5)
                s_ = slice(128 * m, 128 * m + 128)
                three(ps[:, cnt % 6, :], (whi[:, s_], wlo[:, s_]), (x7hi[:, tile(t)], x7lo[:, tile(t)]), True, True)\
                    .then_inc(sem("up"), 1)

            def down(cnt):
                t, m = cnt // FF, cnt % FF
                pe.wait_ge(sem("hidlo"), cnt + 1)
                if t > 1 and m == 0:
                    pe.wait_ge(sem("y_ready"), t - 1)
                s_ = slice(1024 + 128 * m, 1024 + 128 * m + 128)
                three(ps[:, 6 + t % 2, :], (whi[:, s_], wlo[:, s_]), (hidhi[:, cnt % HRING, :], hidlo[:, cnt % HRING, :]), m == 0, m == FF - 1)\
                    .then_inc(sem("down"), 1)

            pe.wait_ge(sem("wsplit"), 2)
            for cnt in range(FF * NT + LAG):
                if cnt < FF * NT:
                    if cnt % FF == 0:
                        pe.wait_ge(sem("x7lo"), cnt // FF + 1)
                    up(cnt)
                if cnt >= LAG:
                    down(cnt - LAG)

        @block.scalar
        def _(act):
            def split(layer, bq, bk, tiles):
                first, end = 2 * tiles[0], 2 * tiles[-1] + 2
                for i in range(first, end + 1):
                    if i < end:
                        t, a = i // 2, i % 2
                        act.wait_ge(sem("qk"), 2 * NT * (layer // 2) + i + 1)
                        nc.scalar.activation(parts[t // 2][:, t % 2, a, 0, :], ps[:, 4 + 2 * (t % 2) + a, :], ACT.Identity,
                                             bias=vv((bq, bk)[a])).then_inc(sem("hi"), 1)
                    if i > first:
                        t, a = (i - 1) // 2, (i - 1) % 2
                        act.wait_ge(sem("rem"), 2 * NT * (layer // 2) + i)
                        nc.scalar.activation(parts[t // 2][:, t % 2, a, 1, :], rem[:, (i - 1) % 2, :], ACT.Copy).then_inc(sem("mid"), 1)

            def normalise(layer, items):
                for i in range(items[0], items[-1] + 2):
                    if i <= items[-1]:
                        act.wait_ge(sem("den"), 2 * NT * (layer - 3) + i + 1)
                        nc.scalar.activation(rec(i), ps[:, den_bank(layer, i), :], ACT.Ln).then_inc(sem("lnd"), 1)
                    if i > items[0]:
                        act.wait_ge(sem("lnd"), 2 * NT * (layer - 3) + i)
                        nc.scalar.activation(rec(i - 1), rec(i - 1), ACT.Exp, scale=-1.0).then_inc(sem("rec"), 1)

            def square(k, t):
                act.wait_ge(sem("cen"), NT * k + t + 1)
                nc.scalar.activation(sqs(k, t), ps[:, cen_bank(k, t), :], ACT.Square).then_inc(sem("sq"), 1)

            def deviation(k, t):
                act.wait_ge(sem("var"), NT * k + t + 1)
                nc.scalar.activation(rss(k, t), ps[:, var_bank(k, t), :], ACT.Ln, bias=eps).then_inc(sem("lv"), 1)
                act.wait_ge(sem("lv"), NT * k + t + 1)
                nc.scalar.activation(rss(k, t), rss(k, t), ACT.Exp, scale=-0.5).then_inc(sem("rs"), 1)

            def norm(k, tiles=range(NT)):
                for t in range(tiles[0], tiles[-1] + 2):
                    if t <= tiles[-1]:
                        square(k, t)
                    if t > tiles[0]:
                        deviation(k, t - 1)

            logexp = "natural_log_exp_and_others"
            nc.scalar.preload_act_table_set(logexp)
            act.wait_ge(sem("in_vec"), 16)
            act.wait_ge(sem("wq_scaled"), 2)
            split(0, "bq0", "bk0", range(NT))
            act.wait_ge(sem("vaug0"), 2)
            for j in range(4):
                act.wait_ge(sem("v"), j + 1)
                nc.scalar.activation(vaug[:, 4 * j:4 * j + 4, :, 0:HD],
                                     ps[:, j, :].rearrange("p (c h d) -> p c h d", c=4, h=NH), ACT.Copy).then_inc(sem("vev0"), 1)
            for t in range(NT):
                act.wait_ge(sem("g1"), t + 1)
                nc.scalar.activation(g1s[:, t, :], ps[0:C // 4, 4 + t, :], ACT.Relu, bias=vv("g1b")[0:C // 4, :]).then_inc(sem("g1r"), 1)
            for t in range(NT):
                act.wait_ge(sem("g2"), t + 1)
                nc.scalar.activation(gate[:, t, :], ps[:, 4 + t, :], ACT.Sigmoid, bias=vv("g2b")).then_inc(sem("sig"), 1)
            nc.scalar.preload_act_table_set(logexp)
            act.wait_ge(sem("in_cst"), 16)
            nc.scalar.activation(identb[:, :], ident, ACT.Copy).then_inc(sem("identb"), 1)
            nc.scalar.activation(identr[:, :], ident, ACT.Copy).then_inc(sem("identr"), 1)
            act.wait_ge(sem("pbe_mm"), 1)
            nc.scalar.activation(pbe, ps[:, 3, 0:1], ACT.Identity, bias=vv("pb0")).then_inc(sem("pbe_ready"), 1)
            act.wait_ge(sem("in_u"), 16)
            for i in range(2):
                s = slice(HT * i, HT * (i + 1))
                nc.scalar.activation(tab2f[0][:, s], u_raw[:, s], ACT.Copy).then_inc(sem("tab_hi"), 1)

            def take0(b):
                act.wait_ge(sem("pv0"), NCH * (b + 1))
                nc.scalar.activation(oraw[:, b, :], ps[:, 6:8, :].rearrange("p s n -> p (s n)"), ACT.Copy).then_inc(sem("accev0"), 1)

            act.wait_ge(sem("tab2_ready"), 1)
            for u in range(16 * NB):
                r0, r1 = query_rows(u // 2 % 4)
                n = (r1 - r0) * QWIN_C
                bank = 2 + 2 * (u % 2)
                act.wait_ge(sem("s2_0"), u + 1)
                if u >= 4:
                    act.wait_ge(sem("pv0"), (u - 4) // 2 + 1)
                nc.scalar.activation(pa0[:, u % 4, :, 0:n], ps[:, bank:bank + 2, 0:n], ACT.Exp).then_inc(sem("exp0"), 1)
                if u % 16 == 1 and u > 16:
                    take0(u // 16 - 1)
                if u > 16 * (NB - 1) and u % 2 == 0:
                    j = u // 2 - NCH * (NB - 1) - 1
                    if j < 2:
                        normalise(3, (2 * j, 2 * j + 1))
                    elif j >= 4:
                        (square, deviation)[j % 2](0, (j - 4) // 2)
            take0(NB - 1)
            deviation(0, 1)

            normalise(3, range(4, 8))
            split(2, "bq2", "bk2", (0,))
            norm(0, (2, 3))
            split(2, "bq2", "bk2", (1,))
            split(2, "bq2", "bk2", (2, 3))

            act.wait_ge(sem("vaug2"), 1)
            for j in range(4):
                act.wait_ge(sem("v"), NT + j + 1)
                for i in range(4):
                    c = 4 * (j % 2) + i
                    nc.scalar.activation(vaug[:, 4 * j + i, :, 0:HD], ps[:, 4 + j, 128 * i:128 * i + 128].rearrange("p (h d) -> p h d", h=NH),
                                         ACT.Copy, scale=cc("mult")[:, c:c + 1]).then_inc(sem("vev2"), 1)

            def take2(n):
                act.wait_ge(sem("pv2"), NCH * (n + 1))
                nc.scalar.activation(oraw[:, n // 2, tile(n % 2)], ps[:, 7, :], ACT.Copy).then_inc(sem("accev2"), 1)

            for u in range(32 * NB2):
                act.wait_ge(sem("s2_2"), u + 1)
                if u >= 12:
                    act.wait_ge(sem("pv2"), (u - 12) // 4 + 1)
                nc.scalar.activation(pa2[:, u % 12, :], ps[:, l2_bank(u), :], ACT.Exp).then_inc(sem("exp2"), 1)
                if u % 32 == 3 and u > 32:
                    take2(u // 32 - 1)
            take2(NB2 - 1)

            normalise(4, range(2 * NT))
            for t in range(NT):
                act.wait_ge(sem("hb"), NT + t + 1)
                nc.scalar.activation(tmp[:, t, :], ps[:, t, :], ACT.Identity, bias=gb2, scale=vv("gamma")).then_inc(sem("gx"), 1)
            norm(1)

            for t in range(NT):
                act.wait_ge(sem("fa"), t + 1)
                nc.scalar.activation(x3t[:, tile(t)], ps[:, t, :], ACT.Copy).then_inc(sem("fa_ev"), 1)
            for t in range(NT):
                act.wait_ge(sem("fc"), t + 1)
                nc.scalar.activation(zt[:, tile(t)], ps[:, t, :], ACT.Copy).then_inc(sem("fc_ev"), 1)

            def take_columns(img, half, eng_copy):
                m = 2 * img + half
                s = sf[half].rearrange("p (k i h) -> p k i h", i=IMG, h=H)
                g0 = ps[:, 4, 96 * m:96 * m + 96].rearrange("p (k h) -> p k h", h=H)
                g1 = ps[:, (5, 6, 7, 0)[m], 0:448].rearrange("p (k h) -> p k h", h=H)
                eng_copy(s[:, 0:3, img, :], g0)
                eng_copy(s[:, 3:KX, img, :], g1)

            for img in range(IMG):
                act.wait_ge(sem("fd"), 4)
                take_columns(img, 0, lambda o, i: nc.scalar.activation(o, i, ACT.Copy).then_inc(sem("fdA"), 1))

            def shrink_in(q):
                half, (o, n) = q // 3, ftiles[q % 3]
                act.wait_ge(sem("ad"), q + 1)
                if q > 1:
                    act.wait_ge(sem("yf"), q - 1)
                nc.scalar.activation(tsh[:, q % 2, 0:n], ps[:, 6 + q % 2, 0:n], ACT.Identity, bias=vv(f"ab2_{half}")).then_inc(sem("tsh"), 1)

            for q in range(6):
                half, (o, n) = q // 3, ftiles[q % 3]
                for m in range(0, 8, 2):
                    act.wait_ge(sem("au"), 8 * q + m + 1)
                    if q > 1:
                        act.wait_ge(sem("ad"), q - 1)
                    nc.scalar.activation(hid[:, q % 2, m, 0:n], ps[:, (8 * q + m) % 6, 0:n], ACT.Relu,
                                         bias=vv(f"ab1_{8 * half + m}")).then_inc(sem("ahA"), 1)
                if q:
                    shrink_in(q - 1)
            shrink_in(5)
            for i in range(5):
                act.wait_ge(sem("ba"), i + 1)
                n = 256 if i == 4 else 512
                for o in range(2):
                    nc.scalar.activation(yt[:, o, 256 * i:256 * i + n // 2].rearrange("p (m c) -> p m c", c=16),
                                         ps[:, i, 0:n].rearrange("p (m o c) -> p m o c", o=2, c=16)[:, :, o, :],
                                         ACT.Copy).then_inc(sem("ba_ev"), 1)
            for t in range(NT):
                act.wait_ge(sem("bc"), t + 1)
                nc.scalar.activation(zt2[:, tile(t)], ps[:, t, :], ACT.Copy).then_inc(sem("bc_ev"), 1)
            norm(2)

            act.wait_ge(sem("gw"), 1)
            nc.scalar.activation(cw, ps[:, 0, 0:256], ACT.Copy).then_inc(sem("gw_ev"), 1)
            nc.scalar.activation(cwb, ps[:, 1, 0:256], ACT.Copy).then_inc(sem("gw_ev"), 1)
            for j in range(8):
                act.wait_ge(sem("kc"), j + 1)
                nc.scalar.activation(ksq[:, 512 * j:512 * j + 512].rearrange("p (m n) -> p m n", n=C), kcm[:, 4 * j:4 * j + 4, 0:C], ACT.Square).then_inc(sem("ksq"), 1)
            for i in range(2):
                s = slice(128 * i, 128 * i + 128)
                act.wait_ge(sem("kvar"), 4 * (i + 1))
                nc.scalar.activation(rsk[:, s], rsk[:, s], ACT.Ln, bias=eps, scale=1.0 / DH_G).then_inc(sem("klv"), 1)
                act.wait_ge(sem("klv"), i + 1)
                nc.scalar.activation(rsk[:, s], rsk[:, s], ACT.Exp, scale=-0.5).then_inc(sem("krs"), 1)
            for img in range(IMG):
                act.wait_ge(sem("kw"), img + 1)
                nc.scalar.activation(kws[:, img, :], ps[:, 6, 128 * img:128 * img + 128], ACT.Copy).then_inc(sem("kw_ev"), 1)
                act.wait_ge(sem("km"), img + 1)
                nc.scalar.activation(ms[:, img, :], ps[:, 7, 128 * img:128 * img + 128], ACT.Copy).then_inc(sem("km_ev"), 1)
                nc.scalar.activation(bvecs[:, img:img + 1], ps[:, 7, 256 + img:257 + img], ACT.Identity, bias=vv("bo3")).then_inc(sem("km_ev"), 1)
            norm(3)
            for cnt in range(FF * NT):
                act.wait_ge(sem("up"), cnt + 1)
                if cnt >= GRING:
                    act.wait_ge(sem("hidlo"), cnt - GRING + 1)
                nc.scalar.activation(hidraw[:, cnt % GRING, :], ps[:, cnt % 6, :], ACT.Gelu, bias=vv(f"bup{cnt % FF}")).then_inc(sem("gelu"), 1)

        @block.vector
        def _(dve):
            v = nc.vector

            def split(layer, bq, bk, tiles):
                for i in range(2 * tiles[0], 2 * tiles[-1] + 2):
                    t, a = i // 2, i % 2
                    dve.wait_ge(sem("hi"), 2 * NT * (layer // 2) + i + 1)
                    if i > 1:
                        dve.wait_ge(sem("mid"), 2 * NT * (layer // 2) + i - 1)
                        dve.wait_ge(sem("split"), 2 * NT * (layer // 2) + i - 1)
                    v.scalar_tensor_tensor(rem[:, i % 2, :], ps[:, 4 + 2 * (t % 2) + a, :], vv((bq, bk)[a]),
                                           parts[t // 2][:, t % 2, a, 0, :], ALU.add, ALU.subtract).then_inc(sem("rem"), 1)

            def maxima(layer, base, nu, k, done):
                if layer == 0:
                    hi, lo, m = mcat[:, 0:k], mcat[:, k:2 * k], mx[:, 0:k]
                else:
                    both = mcat[:, 0:2 * k].rearrange("p (h r a) -> p r h a", h=HG, r=2)
                    hi, lo, m = both[:, 0], both[:, 1], mx[:, 0:k].rearrange("p (h a) -> p h a", h=HG)
                dve.wait_ge(sem(f"p1_taken{layer}"), base + nu - 1)
                v.tensor_scalar(hi, m, -1.0, None, ALU.mult).then_inc(sem(f"mhi{layer}"), 1)
                dve.wait_ge(sem(f"mhi{layer}"), done + 1)
                v.scalar_tensor_tensor(lo, m, -1.0, hi, ALU.mult, ALU.subtract)\
                    .then_inc(sem(f"mcat{layer}"), 1)
                dve.wait_ge(sem(f"s1_{layer}"), base + nu)
                if done:
                    dve.wait_ge(sem(f"mrow{layer}"), (32 if layer == 0 else 64) * done)
                bank = (base + nu - 1) % 2 * (1 if layer == 0 else 2)
                v.tensor_copy(mt[0:2 * k, :], ps[0:2 * k, bank, 0:64].bitcast(BF16)).then_inc(sem(f"p1_taken{layer}"), 1)

            def normalised(layer, items):
                for i in items:
                    dve.wait_ge(sem("rec"), 2 * NT * (layer - 3) + i + 1)
                    v.tensor_tensor(og[:, i, :], oraw[:, 2 * (i // 4) + i % 2, tile(i // 2 % 2)], rec(i), ALU.mult)\
                        .then_inc(sem("og"), 1)

            def norm(k, g, b, out, tiles=range(NT)):
                for t in tiles:
                    dve.wait_ge(sem("rs"), NT * k + t + 1)
                    v.scalar_tensor_tensor(t1s(k, t), ps[:, cen_bank(k, t), :], vv(g), rss(k, t), ALU.mult, ALU.mult).then_inc(sem("ng"), 1)
                    dve.wait_ge(sem("ng"), NT * k + t + 1)
                    dst, src = out(t), t1s(k, t)
                    if len(dst.shape) == 3:
                        src = src.rearrange("p (r c) -> p r c", c=W)
                    v.tensor_scalar(dst, src, vv(b), None, ALU.add).then_inc(sem("lnout"), 1)

            dve.wait_ge(sem("in_w0"), 16)
            dve.wait_ge(sem("in_vec"), 16)
            scale = float(HD) ** -0.5
            v.tensor_scalar(ww(w0, W0A, "wq"), ww(w0, W0A, "wq"), scale, None, ALU.mult).then_inc(sem("wq_scaled"), 1)
            v.tensor_scalar(vv("bq0"), vv("bq0"), scale, None, ALU.mult).then_inc(sem("wq_scaled"), 1)
            v.tensor_scalar(gb2, vv("bv2"), vv("gamma"), None, ALU.mult).then_inc(sem("gb2"), 1)
            split(0, "bq0", "bk0", range(NT))

            def table_rest(i):
                s = slice(HT * i, HT * (i + 1))
                dve.wait_ge(sem("tab_hi"), i + 1)
                v.tensor_tensor(tab2f[1][:, s], u_raw[:, s], tab2f[0][:, s].bitcast(F32), ALU.subtract).then_inc(sem("tab2_ready"), 1)

            dve.wait_ge(sem("in_tab1"), 16)
            for b in range(NB):
                for r in range(U0 - 1):
                    i = U0 * b + r
                    qb, h = r // HG, r % HG
                    k0, k1 = key_rows(qb)
                    n = (k1 - k0) * W
                    o = (k0 - QROWS * qb + K // 2) * CCOLS
                    dve.wait_ge(sem("s1_0"), i + 1)
                    if i > 1:
                        dve.wait_ge(sem("p1_taken0"), i - 1)
                    if r == 0:
                        if b:
                            dve.wait_ge(sem("mcat0"), b)
                    v.tensor_tensor_reduce(junk[:, i % 2, 0:n].rearrange("p (f n) -> p f n", f=2),
                                           ps[:, i % 2, 0:n].rearrange("p (f n) -> p f n", f=2),
                                           tab1[:, HG * (b % NG) + h, :, o:o + n // 2],
                                           1.0, -3.0e38, ALU.add, ALU.max, mx[:, 8 * h + qb:8 * h + qb + 1])\
                        .then_inc(sem("p1_taken0"), 1)
                maxima(0, U0 * b, U0, 32, b)
                if b == 0:
                    for t in range(NT):
                        dve.wait_ge(sem(f"parts_out0_{t}"), 32)
                    table_rest(0)
                    table_rest(1)

            tap_steps = 0

            def convolve(img):
                nonlocal tap_steps
                dve.wait_ge(sem("lnout"), 2 * (img + 1))
                for j, i in enumerate(DVE_TAPS):
                    for t in (2 * img, 2 * img + 1):
                        r0 = 16 * (t % 2) + i // 3
                        src = pad[:, img, r0:r0 + 16, i % 3:i % 3 + W]
                        dst = x2[:, tile(t)].rearrange("p (r c) -> p r c", c=W)
                        if j == 0:
                            v.tensor_scalar(dst, src, vv(f"kc{i}"), None, ALU.mult).then_inc(sem("tap"), 1)
                        else:
                            dve.wait_ge(sem("tap"), tap_steps - 1)
                            v.scalar_tensor_tensor(dst, src, vv(f"kc{i}"), dst, ALU.mult, ALU.add).then_inc(sem("tap"), 1)
                        tap_steps += 1

            def add_taps(t):
                dve.wait_ge(sem("tap"), len(DVE_TAPS) * 2 * (t // 2 + 1))
                dve.wait_ge(sem("conv"), t + 1)
                v.tensor_tensor(x2[:, tile(t)], ps[:, t, :], x2[:, tile(t)], ALU.add).then_inc(sem("x2_ready"), 1)

            def gated(t):
                dve.wait_ge(sem("hb"), t + 1)
                v.scalar_tensor_tensor(x2[:, tile(t)], ps[:, t, :], pbe, gate[:, t, :], ALU.add, ALU.mult).then_inc(sem("yg"), 1)
                dve.wait_ge(sem("yg"), t + 1)
                v.tensor_tensor(ysum[:, t, :], x2[:, tile(t)], xt[:, tile(t)], ALU.add).then_inc(sem("y3"), 1)

            def norm0(tiles):
                norm(0, "lng0", "lnb0", lambda t: pad[:, t // 2, 1 + 16 * (t % 2):17 + 16 * (t % 2), 1:1 + W], tiles)

            dve.wait_ge(sem("sig"), NT)
            dve.wait_ge(sem("pad0"), 1)
            normalised(3, range(4))
            gated(0)
            gated(1)
            norm0((0, 1))
            convolve(0)
            normalised(3, range(4, 8))
            add_taps(0)
            add_taps(1)
            gated(2)
            gated(3)
            split(2, "bq2", "bk2", (0,))
            norm0((2, 3))
            split(2, "bq2", "bk2", (1,))
            convolve(1)
            add_taps(2)
            add_taps(3)
            split(2, "bq2", "bk2", (2, 3))
            for n in range(NB2):
                for r in range(U2 - 1):
                    i = U2 * n + r
                    qt, h = r // HG, r % HG
                    bank = 2 * (i % 2)
                    dve.wait_ge(sem("s1_2"), i + 1)
                    if r == 0:
                        if n:
                            dve.wait_ge(sem("mcat2"), n)
                    v.tensor_reduce(mx[:, 4 * h + qt:4 * h + qt + 1], ps[:, bank:bank + 2, :], AXIS.XY, ALU.max)\
                        .then_inc(sem("p1_taken2"), 1)
                maxima(2, U2 * n, U2, 16, n)

            normalised(4, range(2 * NT))
            for t in range(NT):
                dve.wait_ge(sem("gx"), t + 1)
                v.tensor_tensor(xt[:, tile(t)], tmp[:, t, :], x2[:, tile(t)], ALU.add).then_inc(sem("x3_ready"), 1)
            norm(1, "n1g", "n1b", lambda t: x3n[:, tile(t)])

            for t in range(NT):
                dve.wait_ge(sem("fb"), t + 1)
                dst = a1.rearrange("p (i j h f) -> p i j h f", i=IMG, j=8, h=H)[:, t // 2, :, 16 * (t % 2):16 * (t % 2) + 16, :]
                v.tensor_copy(dst, ps[:, 4 + t, :].rearrange("p (h j f) -> p j h f", j=8, f=4)).then_inc(sem("fb_ev"), 1)
            for img in range(IMG):
                dve.wait_ge(sem("fd"), 4)
                m = 2 * img + 1
                s = sf[1].rearrange("p (k i h) -> p k i h", i=IMG, h=H)
                v.tensor_copy(s[:, 3:KX, img, :], ps[:, (5, 6, 7, 0)[m], 0:448].rearrange("p (k h) -> p k h", h=H)).then_inc(sem("fdD"), 1)
            dve.wait_ge(sem("fdA"), 4)
            for img in range(IMG):
                m = 2 * img + 1
                v.tensor_copy(s[:, 0:3, img, :], ps[:, 4, 96 * m:96 * m + 96].rearrange("p (k h) -> p k h", h=H)).then_inc(sem("fdD"), 1)

            def shrink(q):
                half, (o, n) = q // 3, ftiles[q % 3]
                dve.wait_ge(sem("tsh"), q + 1)
                v.tensor_scalar(csh[:, q % 2, 0:n], tsh[:, q % 2, 0:n], 0.01, -0.01, ALU.min, ALU.max).then_inc(sem("csh"), 1)
                dve.wait_ge(sem("csh"), q + 1)
                v.tensor_tensor(yf[half][:, o:o + n], tsh[:, q % 2, 0:n], csh[:, q % 2, 0:n], ALU.subtract).then_inc(sem("yf"), 1)

            for q in range(6):
                half, (o, n) = q // 3, ftiles[q % 3]
                for m in range(1, 8, 2):
                    dve.wait_ge(sem("au"), 8 * q + m + 1)
                    if q > 1:
                        dve.wait_ge(sem("ad"), q - 1)
                    v.tensor_scalar(hid[:, q % 2, m, 0:n], ps[:, (8 * q + m) % 6, 0:n], vv(f"ab1_{8 * half + m}"), 0.0,
                                    ALU.add, ALU.max).then_inc(sem("ahD"), 1)
                if q:
                    shrink(q - 1)
            shrink(5)
            zv = zf.rearrange("p (i h f) -> p i f h", i=IMG, f=W)
            for kp in range(9):
                dve.wait_ge(sem("bb"), kp + 1)
                n, f0, fn = (128, 0, 2) if kp == 0 else (128, 30, 2) if kp == 8 else (256, 4 * kp - 2, 4)
                v.tensor_copy(zv[:, :, f0:f0 + fn, :], ps[:, 5 + kp % 3, 0:n].rearrange("p (i f h) -> p i f h", i=IMG, h=H))\
                    .then_inc(sem("bb_ev"), 1)
            for t in range(NT):
                dve.wait_ge(sem("bd"), t + 1)
                v.tensor_tensor(x4[:, tile(t)], ps[:, 4 + t, :], x3n[:, tile(t)], ALU.add).then_inc(sem("x4a"), 1)
                dve.wait_ge(sem("x4a"), t + 1)
                v.tensor_tensor(x4[:, tile(t)], x4[:, tile(t)], xt[:, tile(t)], ALU.add).then_inc(sem("x4_ready"), 1)
            norm(2, "n2g", "n2b", lambda t: h5[:, tile(t)])

            for a, b in enumerate(("bk3", "bv3")):
                v.tensor_scalar(cbs[:, 128 * a:128 * a + 128], cc("cenhead"), vv(b), None, ALU.mult).then_inc(sem("cbs"), 1)
            dve.wait_ge(sem("gw_ev"), 2)
            bias2 = cwb.rearrange("p (a n) -> p a n", a=2).unsqueeze(1).to_broadcast([C, 2, 2, C])
            for j in range(8):
                dve.wait_ge(sem("gk"), j + 1)
                v.tensor_tensor(kc[:, 2 * j:2 * j + 2, :, 0:C], ps[:, j, :].rearrange("p (t a n) -> p t a n", t=2, a=2), bias2, ALU.add).then_inc(sem("kc"), 1)
            for j in range(8):
                dve.wait_ge(sem("ksq"), j + 1)
                v.tensor_reduce(rsk[:, 32 * j:32 * j + 32], ksq[:, 512 * j:512 * j + 512].rearrange("p (g d) -> p g d", d=DH_G),
                                AXIS.X, ALU.add).then_inc(sem("kvar"), 1)
            for j in range(8):
                dve.wait_ge(sem("krs"), j // 4 + 1)
                kv_ = kcm[:, 4 * j:4 * j + 4, 0:C].rearrange("p m (g d) -> p m g d", d=DH_G)
                rs_ = rsk[:, 32 * j:32 * j + 32].rearrange("p (m g) -> p m g", m=4).unsqueeze(3).to_broadcast([C, 4, 8, DH_G])
                v.tensor_tensor(kv_, kv_, rs_, ALU.mult).then_inc(sem("kn"), 1)
                if j % 4 == 3:
                    img = j // 4
                    dve.wait_ge(sem("kn"), j + 1)
                    v.tensor_reduce(ksum[:, img, :], kc[:, 8 * img:8 * img + 8, 0, 0:C].rearrange("p t n -> p n t"), AXIS.X, ALU.add)\
                        .then_inc(sem("ksum"), 1)
            done = [0]

            def step(ins):
                done[0] += 1
                ins.then_inc(sem("kvchain"), 1)
                dve.wait_ge(sem("kvchain"), done[0])

            lkg, lkb = ww(r_tab, W3A, "lkg"), ww(r_tab, W3A, "lkb")
            for img in range(IMG):
                dve.wait_ge(sem("kv"), img + 1)
                step(v.tensor_copy(sv, ps[:, 3 * img, C:C + 1]))
                step(v.tensor_tensor(kvx[:, 0, :], ps[:, 3 * img, 0:128], lkg, ALU.mult))
                step(v.scalar_tensor_tensor(kvx[:, 1, :], lkb, sv, kvx[:, 0, :], ALU.mult, ALU.add))
                step(v.tensor_tensor(kvx[:, 2, :], ps[:, 3 * img + 2, 0:128], lkg, ALU.mult))
                step(v.scalar_tensor_tensor(kvx[:, 3, :], lkb, float(TOK), kvx[:, 2, :], ALU.mult, ALU.add))
                step(v.tensor_scalar(kvx[:, 4, :], kvx[:, 1, :], vv("lvg"), None, ALU.mult))
                step(v.scalar_tensor_tensor(kvx[:, 5, :], kvx[:, 3, :], vv("lvb"), kvx[:, 4, :], ALU.mult, ALU.add))
                v.tensor_tensor(kvt[:, img, :], kvx[:, 5, :], cc("kvmask"), ALU.mult).then_inc(sem("kvt"), 1)
            for t in range(NT):
                dve.wait_ge(sem("att"), t + 1)
                v.scalar_tensor_tensor(xt[:, tile(t)], ps[:, t, :], bvecs[:, t // 2:t // 2 + 1], h5[:, tile(t)], ALU.add, ALU.add)\
                    .then_inc(sem("x6_ready"), 1)
            norm(3, "n3g", "n3b", lambda t: x7[:, tile(t)])
            for t in range(NT):
                dve.wait_ge(sem("lnout"), 3 * NT + t + 1)
                v.tensor_copy(x7hi[:, tile(t)], x7[:, tile(t)]).then_inc(sem("x7hi"), 1)
                dve.wait_ge(sem("x7hi"), t + 1)
                v.tensor_tensor(x7lo[:, tile(t)], x7[:, tile(t)], x7hi[:, tile(t)].bitcast(F32), ALU.subtract).then_inc(sem("x7lo"), 1)

            def finish(t):
                dve.wait_ge(sem("down"), FF * (t + 1))
                v.scalar_tensor_tensor(x2[:, tile(t)], ps[:, 6 + t % 2, :], vv("bdn"), x7[:, tile(t)], ALU.add, ALU.add)\
                    .then_inc(sem("y_ready"), 1)

            for cnt in range(FF * NT):
                s, g = cnt % HRING, cnt % GRING
                dve.wait_ge(sem("gelu"), cnt + 1)
                if cnt >= HRING:
                    dve.wait_ge(sem("down"), cnt - HRING + 1)
                v.tensor_copy(hidhi[:, s, :], hidraw[:, g, :]).then_inc(sem("hidhi"), 1)
                dve.wait_ge(sem("hidhi"), cnt + 1)
                v.tensor_tensor(hidlo[:, s, :], hidraw[:, g, :], hidhi[:, s, :].bitcast(F32), ALU.subtract).then_inc(sem("hidlo"), 1)
                if cnt >= FF and cnt % FF == LAG + 1:
                    finish(cnt // FF - 1)
            finish(NT - 1)

        @block.gpsimd
        def _(pool):
            g = nc.gpsimd

            def split(layer):
                for i in range(2 * NT):
                    t, a = i // 2, i % 2
                    pool.wait_ge(sem("mid"), 2 * NT * (layer // 2) + i + 1)
                    g.tensor_tensor(parts[t // 2][:, t % 2, a, 2, :], rem[:, i % 2, :], parts[t // 2][:, t % 2, a, 1, :], ALU.subtract)\
                        .then_inc(sem("split"), 1)

            g.memset(zerob[:, :], 0.0).then_inc(sem("zeros"), 1)
            g.memset(eps, 1e-5).then_inc(sem("zeros"), 1)
            g.memset(vaug[:, :, :, :], 0.0).then_inc(sem("vaug0"), 1)
            pool.wait_ge(sem("vaug0"), 1)
            g.memset(vaug[:, :, :, HD:HD + 1], 1.0).then_inc(sem("vaug0"), 1)
            g.memset(ones[:, :], 1.0).then_inc(sem("zeros"), 1)
            split(0)
            g.memset(pad[:, :, :, :], 0.0).then_inc(sem("pad0"), 1)
            pool.wait_ge(sem("in_cst"), 16)
            pool.wait_ge(sem("in_vec"), 16)
            for i in PE_TAPS:
                if i == 4:
                    g.tensor_copy(kd[:, i, :], ident).then_inc(sem("kd"), 1)
                else:
                    g.tensor_scalar(kd[:, i, :], ident, vv(f"kc{i}"), None, ALU.mult).then_inc(sem("kd"), 1)
            pool.wait_ge(sem("pv0"), NCH * NB)
            g.tensor_copy(vaug[:, :, :, HD].rearrange("p (i c) h -> p i c h", i=IMG),
                          cc("mult").unsqueeze(1).unsqueeze(3).to_broadcast([C, IMG, NCH, NH])).then_inc(sem("vaug2"), 1)
            split(2)
            pool.wait_ge(sem("in_w3"), 16)
            for half in range(2):
                g.tensor_scalar(aw1[:, half, 0, :, :], aw1[:, half, 0, :, :], cc("sign"), None, ALU.mult).then_inc(sem("aw1s"), 1)
            pool.wait_ge(sem("aw1s"), 2)
            for half in range(2):
                g.tensor_scalar(aw2[:, half, 1, :, 0:16], aw2[:, half, 1, :, 0:16], -1.0, None, ALU.mult).then_inc(sem("aw_signed"), 1)
            pool.wait_ge(sem("pv2"), NCH * NB2)
            o = W3A["wup"][0]
            g.tensor_copy(whi[:, :], r_tab[:, o:o + 2048]).then_inc(sem("wsplit"), 1)
            pool.wait_ge(sem("wsplit"), 1)
            g.tensor_tensor(wlo[:, :], r_tab[:, o:o + 2048], whi[:, :].bitcast(F32), ALU.subtract).then_inc(sem("wsplit"), 1)
            pool.wait_ge(sem("lnout"), 3 * NT)
            g.memset(kc[:, :, 0, C:C + 1], 1.0).then_inc(sem("kc_ones"), 1)
    return


def bias_tables(rpb):
    n, k = NH, K - 1
    s = window(W)
    t1 = np.zeros((QROWS, W, n, KWIN, W), rpb.dtype)
    for r in range(QROWS):
        for v in range(KWIN):
            dr = v - K // 2 - r + k
            if not 0 <= dr <= 2 * k:
                continue
            for q in range(W):
                t1[r, q, :, v, :] = NEG
                t1[r, q, :, v, s[q]:s[q] + K] = rpb[:, dr, s[q] - q + k:s[q] - q + k + K]
    t1 = t1.reshape(QROWS, W, n, KWIN, 2, CCOLS).transpose(0, 1, 2, 4, 3, 5)
    t2 = np.zeros((CROWS, CCOLS, n, 2, QWIN_R, QWIN_C), rpb.dtype)
    for half in range(2):
        c0, c1 = query_cols(half)
        for kc in range(CCOLS):
            key = CCOLS * half + kc
            for j, q in enumerate(range(c0, c1)):
                inside = s[q] <= key < s[q] + K
                for r in range(CROWS):
                    for u in range(QWIN_R):
                        dr = r - (u - K // 2) + k
                        if 0 <= dr <= 2 * k:
                            t2[r, kc, :, half, u, j] = rpb[:, dr, key - q + k] if inside else NEG
    return t1.reshape(128, -1), t2.reshape(128, -1)


def pack(**a):
    f = np.float32
    heads = np.zeros((NG, 128, C), f)
    for g in range(NG):
        for h in range(HG):
            heads[g, 32 * h:32 * h + HD] = a["L0_conv_proj_w"][64 * g + HD * h:64 * g + HD * (h + 1)]

    def column(x):
        out = np.zeros((C, 1), f)
        out[:x.size, 0] = x
        return out

    def every(x):
        return np.broadcast_to(x.reshape(1, -1), (C, x.size)).astype(f)

    qkv_b = a["L0_conv_qkv_b"]
    kern = a["L1_conv_kernel"].reshape(9, C)
    b1 = a["L3_conv_afno_b1"]
    b2 = a["L3_conv_afno_b2"].reshape(2, 2, 4, 2, BS)
    qk = np.arange(C).reshape(NG, HG, HD).transpose(0, 2, 1).reshape(-1)
    v = {"bq0": column(qkv_b[0:C][qk]), "bk0": column(qkv_b[C:2 * C][qk]), "bv0": column(qkv_b[2 * C:]),
         "pb0": column(a["L0_conv_proj_b"]), "lng0": column(a["L0_conv_ln_g"]), "lnb0": column(a["L0_conv_ln_b"]),
         "g1b": column(a["L0_conv_g1_b"]), "g2b": every(a["L0_conv_g2_b"]),
         "bq2": column(a["L2_conv_bq"][qk]), "bk2": column(a["L2_conv_bk"][qk]), "bv2": column(a["L2_conv_bv"]),
         "gamma": every(a["L2_conv_gamma"]), "bq3": column(a["L3_conv_bq"]), "bk3": column(a["L3_conv_bk"]),
         "bv3": column(a["L3_conv_bv"]), "bo3": column(a["L3_conv_bo"]), "bdn": column(a["L3_conv_b_down"]),
         "lvg": column(a["L3_conv_lnv_g"].reshape(-1)), "lvb": column(a["L3_conv_lnv_b"].reshape(-1))}
    for i in range(1, 4):
        v[f"n{i}g"], v[f"n{i}b"] = column(a[f"L3_conv_n{i}_g"]), column(a[f"L3_conv_n{i}_b"])
    for i in range(9):
        v[f"kc{i}"] = column(kern[i])
    for i in range(FF):
        v[f"bup{i}"] = column(a["L3_conv_b_up"][128 * i:128 * i + 128])
    for half in range(2):
        for t in range(2):
            for p in range(4):
                v[f"ab1_{8 * half + 4 * t + p}"] = column(b1[t, 8 * half + 2 * p:8 * half + 2 * p + 2].reshape(-1))
        v[f"ab2_{half}"] = column(b2[:, half].transpose(1, 0, 2, 3).reshape(-1))
    aw1 = np.zeros((128, 2, 2, 4, 128), f)
    aw2 = np.zeros((128, 2, 2, 4, 32), f)
    w1, w2 = a["L3_conv_afno_w1"], a["L3_conv_afno_w2"]
    E = BS * EXPF
    for half in range(2):
        for t in range(2):
            for p in range(4):
                for b in range(2):
                    n = 8 * half + 2 * p + b
                    c = HD * p + BS * b
                    for part in range(2):
                        aw1[HALF * part + c:HALF * part + c + BS, half, t, p, E * b:E * (b + 1)] = w1[part ^ t, n]
                        aw2[E * b:E * (b + 1), half, t, p, 16 * part + BS * b:16 * part + BS * (b + 1)] = w2[part ^ t, n]
    w = {"wq": a["L0_conv_qkv_w"][:, 0:C][:, qk], "wk": a["L0_conv_qkv_w"][:, C:2 * C][:, qk], "wv": a["L0_conv_qkv_w"][:, 2 * C:],
         "pw": a["L0_conv_proj_w"], "pwg0": heads[0], "pwg1": heads[1], "g1w": a["L0_conv_g1_w"],
         "g2w": np.concatenate([np.broadcast_to(a["L0_conv_g2_w"], (C // 4, C)), np.zeros((3 * C // 4, C), f)]),
         "wq2": a["L2_conv_Wq"][:, qk], "wk2": a["L2_conv_Wk"][:, qk], "wv2": a["L2_conv_Wv"],
         "wq3": a["L3_conv_wq"], "wk3": a["L3_conv_wk"], "wv3": a["L3_conv_wv"], "wo3": a["L3_conv_wo"].T,
         "lkg": every(a["L3_conv_lnk_g"]), "lkb": every(a["L3_conv_lnk_b"]),
         "aw1": aw1.reshape(128, -1), "aw2": aw2.reshape(128, -1), "wup": a["L3_conv_w_up"].T,
         "wdn": a["L3_conv_w_down"].T.reshape(FF, 128, C).transpose(1, 0, 2).reshape(128, -1)}

    def row(names):
        return np.ascontiguousarray(np.concatenate([np.asarray(w[n], f) for n, _ in names], axis=1))

    t1, t2 = bias_tables(a["L0_conv_rpb"])
    xt = a["x"].reshape(IMG, TOK, C)
    return {"xT": np.ascontiguousarray(xt.reshape(T, C).T), "xK": np.ascontiguousarray(xt[:, key_order()].reshape(T, C).T), "w0": row(W0), "w2": row(W2), "w3": row(W3),
            "vec": np.ascontiguousarray(np.concatenate([v[n] for n in VEC], axis=1)),
            "cst": CONSTS, "tab1": np.ascontiguousarray(t1), "tab2": np.ascontiguousarray(t2), "mrows": mask_rows()}


def kernel(**inputs):
    import concourse.bacc as bacc
    from concourse.bass_utils import run_bass_kernel_spmd

    arrays = pack(**{k: np.asarray(a) for k, a in inputs.items()})
    nc = bacc.Bacc("TRN2", target_bir_lowering=False, num_devices=1)
    io = {n: nc.dram_tensor(f"in_{n}", a.shape, mybir.dt.from_np(a.dtype), kind="ExternalInput").ap() for n, a in arrays.items()}
    io["out"] = nc.dram_tensor("y", (C, T), F32, kind="ExternalOutput").ap()
    build(nc, io)
    r = run_bass_kernel_spmd(nc, [{f"in_{n}": a for n, a in arrays.items()}], core_ids=[0])
    y = r.results[0]["y"]
    return np.ascontiguousarray(y.T).reshape(IMG, H, W, C)
```
